# Optimizing a Trainium2 kernel written in Bass

```python
import numpy as np
import jax
import jax.numpy as jnp

def _softmax(x, axis=-1):
    return jax.nn.softmax(x, axis=axis)

def _gelu(x):
    return jax.nn.gelu(x, approximate=True)

def _silu(x):
    return jax.nn.silu(x)

def _sigmoid(x):
    return jax.nn.sigmoid(x)

def _layernorm(x, axis=-1, eps=1e-05):
    m = jnp.mean(x, axis=axis, keepdims=True)
    v = jnp.var(x, axis=axis, keepdims=True)
    return (x - m) / jnp.sqrt(v + eps)

def _scatter_add(tgt, idx, src, axis=0):
    return tgt.at[idx].add(src)

def _segment_sum(src, seg, n):
    return jax.ops.segment_sum(src, seg, n)
kernel_name = 'mk_gps_d1_gnn_r32_3e2af1'

def setup_inputs(seed: int=0):
    np.random.seed(seed)
    _w = jnp.asarray

    def _rec_inputs():
        import jax
        import jax.numpy as jnp
        _gk = jax.random.key(seed)
        x = -8.776e-05 + 1 * jax.random.normal(jax.random.fold_in(_gk, 1), (3125, 256), jnp.float32)
        src = jax.random.randint(jax.random.fold_in(_gk, 2), (50000,), 0, 3125, jnp.int32)
        dst = jnp.minimum((3125 * jax.random.uniform(jax.random.fold_in(_gk, 3), (50000,)) ** 2.0).astype(jnp.int32), 99999)
        _o = jnp.argsort(dst, stable=True)
        src = src[_o]
        dst = dst[_o]
        edge_type_8 = jax.random.randint(jax.random.fold_in(_gk, 12), (50000,), 0, 8, jnp.int32)
        return (x, src, dst, edge_type_8)
    x, src, dst, edge_type_8 = _rec_inputs()

    def _L0_gnn_setup():
        import jax, jax.numpy as jnp
        import numpy as np
        N_NODES = 625
        N_EDGES = 20000
        D = 256
        N_RELS = 8
        N_BASES = 4
        LN_EPS = 1e-05
        key = jax.random.key(seed)
        ks = jax.random.split(key, 8)
        node_feats = jax.random.normal(ks[0], (N_NODES, D), dtype=jnp.float32)
        src = jax.random.randint(ks[1], (N_EDGES,), 0, N_NODES, dtype=jnp.int32)
        dst = jax.random.randint(ks[2], (N_EDGES,), 0, N_NODES, dtype=jnp.int32)
        edge_types = jax.random.randint(ks[3], (N_EDGES,), 0, N_RELS, dtype=jnp.int32)
        basis = jax.random.normal(ks[4], (N_BASES, D, D), dtype=jnp.float32) * (1.0 / np.sqrt(D))
        comp = jax.random.normal(ks[5], (N_RELS, N_BASES), dtype=jnp.float32) * (1.0 / np.sqrt(N_BASES))
        loop_w = jax.random.normal(ks[6], (D, D), dtype=jnp.float32) * (1.0 / np.sqrt(D))
        h_bias = jnp.zeros((D,), dtype=jnp.float32)
        ln_gamma = jnp.ones((D,), dtype=jnp.float32)
        ln_beta = jnp.zeros((D,), dtype=jnp.float32)
        return {'node_feats': node_feats, 'src': src, 'dst': dst, 'edge_types': edge_types, 'basis': basis, 'comp': comp, 'loop_w': loop_w, 'h_bias': h_bias, 'ln_gamma': ln_gamma, 'ln_beta': ln_beta}
    _L0_gnn_all = _L0_gnn_setup()
    _L0_gnn_in = {k: v for k, v in _L0_gnn_all.items() if k in ('basis', 'comp', 'loop_w', 'h_bias', 'ln_gamma', 'ln_beta')}
    del _L0_gnn_all

    def _L0_mix_setup():
        import jax, jax.numpy as jnp
        import numpy as np
        BN_EPS = 1e-05
        key = jax.random.key(seed)
        ks = jax.random.split(key, 4)
        B, N, D = (8, 256, 256)
        outD = 256
        s = 1.0 / np.sqrt(D)
        return {'feature': jax.random.normal(ks[0], (B, N, D), dtype=jnp.float32), 'W_qk': jax.random.normal(ks[1], (2, D, D), dtype=jnp.float32) * s, 'b_qk': jnp.zeros((2, D), dtype=jnp.float32), 'W_v': jax.random.normal(ks[2], (D, outD), dtype=jnp.float32) * s, 'b_v': jnp.zeros((outD,), dtype=jnp.float32), 'gamma': jnp.ones((D,), dtype=jnp.float32), 'beta': jnp.zeros((D,), dtype=jnp.float32)}
    _L0_mix_all = _L0_mix_setup()
    _L0_mix_in = {k: v for k, v in _L0_mix_all.items() if k in ('W_qk', 'b_qk', 'W_v', 'b_v', 'gamma', 'beta')}
    del _L0_mix_all

    def _L0_ffn_setup():
        import jax, jax.numpy as jnp
        import numpy as np
        B, K, D = (512, 16, 256)
        E = 32
        H = int(D * 0.25)
        key = jax.random.key(seed)
        ks = jax.random.split(key, 7)
        d_rs = D ** (-0.5)
        h_rs = H ** (-0.5)
        x = jax.random.normal(ks[0], (B, K, D), dtype=jnp.float32)
        router_w = jax.random.uniform(ks[1], (E, D), jnp.float32, -d_rs, d_rs)
        router_b = jax.random.uniform(ks[2], (E,), jnp.float32, -d_rs, d_rs)
        W1 = jax.random.uniform(ks[3], (E, D, H), jnp.float32, -h_rs, h_rs)
        b1 = jax.random.uniform(ks[4], (E, H), jnp.float32, -h_rs, h_rs)
        W2 = jax.random.uniform(ks[5], (E, H, D), jnp.float32, -d_rs, d_rs)
        b2 = jax.random.uniform(ks[6], (E, D), jnp.float32, -d_rs, d_rs)
        return {'x': x, 'router_w': router_w, 'router_b': router_b, 'W1': W1, 'b1': b1, 'W2': W2, 'b2': b2}
    _L0_ffn_all = _L0_ffn_setup()
    _L0_ffn_in = {k: v for k, v in _L0_ffn_all.items() if k in ('router_w', 'router_b', 'W1', 'b1', 'W2', 'b2')}
    del _L0_ffn_all
    return {'x': x, 'src': src, 'dst': dst, 'edge_type_8': edge_type_8, 'L0_gnn_basis': _L0_gnn_in['basis'], 'L0_gnn_comp': _L0_gnn_in['comp'], 'L0_gnn_loop_w': _L0_gnn_in['loop_w'], 'L0_gnn_h_bias': _L0_gnn_in['h_bias'], 'L0_gnn_ln_gamma': _L0_gnn_in['ln_gamma'], 'L0_gnn_ln_beta': _L0_gnn_in['ln_beta'], 'L0_mix_W_qk': _L0_mix_in['W_qk'], 'L0_mix_b_qk': _L0_mix_in['b_qk'], 'L0_mix_W_v': _L0_mix_in['W_v'], 'L0_mix_b_v': _L0_mix_in['b_v'], 'L0_mix_gamma': _L0_mix_in['gamma'], 'L0_mix_beta': _L0_mix_in['beta'], 'L0_ffn_router_w': _L0_ffn_in['router_w'], 'L0_ffn_router_b': _L0_ffn_in['router_b'], 'L0_ffn_W1': _L0_ffn_in['W1'], 'L0_ffn_b1': _L0_ffn_in['b1'], 'L0_ffn_W2': _L0_ffn_in['W2'], 'L0_ffn_b2': _L0_ffn_in['b2']}

def reference(x, src, dst, edge_type_8, L0_gnn_basis, L0_gnn_comp, L0_gnn_loop_w, L0_gnn_h_bias, L0_gnn_ln_gamma, L0_gnn_ln_beta, L0_mix_W_qk, L0_mix_b_qk, L0_mix_W_v, L0_mix_b_v, L0_mix_gamma, L0_mix_beta, L0_ffn_router_w, L0_ffn_router_b, L0_ffn_W1, L0_ffn_b1, L0_ffn_W2, L0_ffn_b2):
    import jax
    import jax.numpy as jnp

    def _L0_gnn_ref(node_feats, src, dst, edge_types, basis, comp, loop_w, h_bias, ln_gamma, ln_beta):
        import jax, jax.numpy as jnp
        import numpy as np
        N_NODES = 625
        N_EDGES = 20000
        D = 256
        N_RELS = 8
        N_BASES = 4
        LN_EPS = 1e-05
        W = jnp.einsum('rb,bio->rio', comp, basis)
        h_all = jnp.einsum('ni,rio->nro', node_feats, W)
        msgs = h_all[src, edge_types]
        agg = jax.ops.segment_sum(msgs, dst, num_segments=node_feats.shape[0])
        rgcn_out = agg + node_feats @ loop_w + h_bias
        h = jax.nn.gelu(rgcn_out + node_feats, approximate=False)
        mu = jnp.mean(h, axis=-1, keepdims=True)
        var = jnp.mean(jnp.square(h - mu), axis=-1, keepdims=True)
        return (h - mu) * jax.lax.rsqrt(var + LN_EPS) * ln_gamma + ln_beta

    def _L0_mix_ref(feature, W_qk, b_qk, W_v, b_v, gamma, beta):
        import jax, jax.numpy as jnp
        import numpy as np
        BN_EPS = 1e-05
        QK = jnp.einsum('bnd,kde->bkne', feature, W_qk) + b_qk[None, :, None, :]
        value = jnp.einsum('bnd,de->bne', feature, W_v) + b_v
        query = QK[:, 0]
        key = QK[:, 1]
        sm = jax.nn.softmax(key, axis=1)
        lam = jnp.einsum('bnd,bne->bde', sm, value)
        mean = jnp.mean(lam, axis=(0, 2), keepdims=True)
        var = jnp.var(lam, axis=(0, 2), keepdims=True)
        bn = (lam - mean) * jax.lax.rsqrt(var + BN_EPS)
        bn = bn * gamma[None, :, None] + beta[None, :, None]
        return jnp.einsum('bnd,bde->bne', query, bn)

    def _L0_ffn_ref(x, router_w, router_b, W1, b1, W2, b2):
        import jax, jax.numpy as jnp
        import numpy as np
        B, K, D = (512, 16, 256)
        E = 32
        H = int(D * 0.25)
        xf = x.reshape(-1, D)
        logits = xf @ router_w.T + router_b
        idx = jnp.argmax(logits, axis=-1)
        w1t = jnp.take(W1, idx, axis=0)
        h = jnp.einsum('nd,ndh->nh', xf, w1t) + jnp.take(b1, idx, axis=0)
        h = jax.nn.relu(h)
        w2t = jnp.take(W2, idx, axis=0)
        out = jnp.einsum('nh,nhd->nd', h, w2t) + jnp.take(b2, idx, axis=0)
        out = jax.nn.relu(out)
        return out.reshape(x.shape)
    xn = _layernorm(x, axis=-1)
    x = x + _L0_gnn_ref(xn, src, dst, edge_type_8, L0_gnn_basis, L0_gnn_comp, L0_gnn_loop_w, L0_gnn_h_bias, L0_gnn_ln_gamma, L0_gnn_ln_beta) + _L0_mix_ref(xn[None], L0_mix_W_qk, L0_mix_b_qk, L0_mix_W_v, L0_mix_b_v, L0_mix_gamma, L0_mix_beta)[0]
    x = x + _L0_ffn_ref(_layernorm(x, axis=-1)[None], L0_ffn_router_w, L0_ffn_router_b, L0_ffn_W1, L0_ffn_b1, L0_ffn_W2, L0_ffn_b2)[0]
    return x

_drawn_inputs = setup_inputs


def setup_inputs(seed=0):
    import zlib

    import numpy as np

    out = dict(_drawn_inputs(seed))
    spreads = {'L0_gnn_h_bias': (0.0, 0.8),
     'L0_gnn_ln_gamma': (1.0, 0.6),
     'L0_gnn_ln_beta': (0.0, 0.8),
     'L0_mix_b_qk': (0.0, 0.1),
     'L0_mix_b_v': (0.0, 0.1),
     'L0_mix_gamma': (1.0, 0.2),
     'L0_mix_beta': (0.0, 0.1)}
    factors = {'L0_gnn_loop_w': 3.042,
     'L0_ffn_router_w': 6.974,
     'L0_ffn_router_b': 8.0,
     'L0_ffn_W1': 8.0,
     'L0_ffn_b1': 8.0,
     'L0_ffn_W2': 6.644,
     'L0_ffn_b2': 43.756}
    for name, (base, spread) in spreads.items():
        noise = np.random.default_rng([zlib.crc32(name.encode()), seed]).standard_normal(out[name].shape)
        drawn = base * np.exp(spread * noise) if base else spread * noise
        out[name] = jnp.asarray(drawn.astype(out[name].dtype))
    for name, factor in factors.items():
        out[name] = (out[name] * factor).astype(out[name].dtype)
    return out
```

```python
from contextlib import ExitStack

import concourse.bass as bass
from concourse import mybir
from concourse.bass import ds

P = 128
N, D, E = 3125, 256, 50000
R, B, X, H = 8, 4, 32, 64
KD = D // P
NT = -(-N // P)
LAST = N - (NT - 1) * P
NPAD = NT * P
WIN = 32
OCT = 8
NOCT = -(-E // (P * OCT))
ETAB = (NOCT + 1) * OCT
ROWG = 4
PAIRS = (NT - 1) // 2
SLOT_TILES = X + (N - X) // P
GROUPS, GT = 5, NT // 5
EPS = 1e-5
FT = 4
YB = 8
assert NT % GROUPS == 0 and SLOT_TILES % FT == 0 and ETAB % ROWG == 0

ALU = mybir.AluOpType
ACT = mybir.ActivationFunctionType
AX = mybir.AxisListType
F32, BF16 = mybir.dt.float32, mybir.dt.bfloat16
I32, U32 = mybir.dt.int32, mybir.dt.uint32


def rows(t):
    return P if t < NT - 1 else LAST


class Tally:

    def __init__(self, sem, at=0):
        self.sem, self.at = sem, at

    def mark(self, instruction, by=1):
        instruction.then_inc(self.sem, by)
        self.at += by
        return self.at


def gps_layer(nc, x, src_t, type_t, dst_t, dst_rows, basis, comp, loop_w, h_bias, ln_gamma, ln_beta,
              w_qk, b_qk, w_v, b_v, bn_gamma, bn_beta, router_w, router_b, w1, b1, w2, b2, out):
    with ExitStack() as ctx:
        def sb(name, shape, dt=F32):
            return ctx.enter_context(nc.sbuf_tensor(name, shape, dt))

        def sem(name):
            return ctx.enter_context(nc.semaphore(name))

        xn_d = nc.dram_tensor("xn_d", [N, D], F32).ap()
        bounds_d = nc.dram_tensor("bounds_d", [2, ETAB], I32).ap()
        early_d = nc.dram_tensor("early_d", [NT, P, 2 * D], F32).ap()
        slots_in_d = nc.dram_tensor("slots_in_d", [SLOT_TILES * P, D], F32).ap()
        slots_out_d = nc.dram_tensor("slots_out_d", [SLOT_TILES * P, D], F32).ap()

        acc_raw = sb("acc_raw", [P, KD * B * NPAD])
        acc = acc_raw[:, :].rearrange("p (c n) -> p c n", n=NPAD)
        xn_raw = sb("xn_raw", [P, NT * (D + 1)])
        xn = xn_raw[:, :].rearrange("p (t f) -> p t f", f=D + 1)
        x2 = xn_raw[:, 0:NT * D].rearrange("p (t f) -> p t f", f=D)
        xnt_raw = sb("xnt_raw", [P, KD * NPAD])
        xnt = xnt_raw[:, :].rearrange("p (k n) -> p k n", n=NPAD)
        x2n = xnt_raw[:, :].rearrange("p (t f) -> p t f", f=D)
        gath = sb("gath", [P, OCT, D])
        wmat = sb("wmat", [P, OCT, B, WIN])
        hit = sb("hit", [P, OCT // 2, WIN])
        rel = sb("rel", [P, ETAB])
        wts = sb("wts", [P, B, ETAB])
        src_i = sb("src_i", [P, ETAB], I32)
        dst_i = sb("dst_i", [P, ETAB], I32)
        idx_st = sb("idx_st", [P, OCT], I32)
        base_row = sb("base_row", [1, ETAB], I32)
        comp_bc = sb("comp_bc", [P, R, B])
        type_i = wmat[:, :, :, :].rearrange("p a b w -> p (a b w)")[:, 0:ETAB].bitcast(I32)
        type_f = wmat[:, :, :, :].rearrange("p a b w -> p (a b w)")[:, ETAB:2 * ETAB]
        gath_flat = gath[:, :, :].rearrange("p a f -> p (a f)")
        is_rel = [gath_flat[:, 0:ETAB], gath_flat[:, 3 * ETAB:4 * ETAB]]
        pool_term = gath_flat[:, ETAB:2 * ETAB]
        base_bc = gath_flat[:, 2 * ETAB:3 * ETAB].bitcast(I32)
        dstr_i = gath_flat[:, 3 * ETAB:3 * ETAB + ROWG * P].bitcast(I32)
        wk_et = sb("wk_et", [P, 2 * KD * D])
        wk = wk_et[:, 0:KD * D].rearrange("p (k f) -> p k f", k=KD)
        et = wk_et[:, KD * D:2 * KD * D].rearrange("p (j f) -> p j f", j=2)
        wq = sb("wq", [P, KD, D])
        wv = sb("wv", [P, KD, D])
        cmat = sb("cmat", [P, KD, 2 * D])
        xst = sb("xst", [P, 2, KD, P])
        xin = sb("xin", [P, 2, D])
        eout = sb("eout", [P, 2, 2 * D])
        ident = sb("ident", [P, P])
        identb = sb("identb", [P, P], BF16)
        before = sb("before", [P, P], BF16)
        onesb = sb("onesb", [P, P], BF16)
        ones_row = sb("ones_row", [1, P])
        iota_i = sb("iota_i", [P, P], I32)
        iota = sb("iota", [P, P])
        zeros = sb("zeros", [P, D])
        eps_col = sb("eps_col", [P, 1])
        neg_half = sb("neg_half", [P, 1])
        stats = sb("stats", [P, GT, 6])
        mv = sb("mv", [P, NT, 2])
        rstd = sb("rstd", [P, NT])
        low = sb("low", [ETAB // ROWG, ROWG], I32)
        high = sb("high", [ETAB // ROWG, ROWG], I32)
        span = sb("span", [ETAB // ROWG, ROWG], I32)
        span_row = sb("span_row", [1, ETAB], I32)
        flag = sb("flag", [1, 1], I32)
        top = sb("top", [P, PAIRS + 1, KD])
        cols = sb("cols", [P, 8])
        qk_col = sb("qk_col", [P, 2, KD])
        bn_col = sb("bn_col", [P, 2, KD])
        hb_col = sb("hb_col", [P, 2, KD])
        parts = sb("parts", [P, 4, 3], BF16)
        rest = sb("rest", [P, 2, 4])
        shift3 = sb("shift3", [3, D], BF16)
        bias3 = sb("bias3", [3, 2 * D], BF16)
        bv_bc = sb("bv_bc", [P, D])
        gam_bc = sb("gam_bc", [P, D])
        rw = sb("rw", [X, D])
        rwt = sb("rwt", [P, KD, X])
        rb_row = sb("rb_row", [1, X])
        tn = eout[:, 0, :].rearrange("p (m f) -> p m f", m=KD)
        tnt = eout[:, 1, :].rearrange("p (k d) -> p k d", k=KD)
        lam = xst[:, :, :, :].rearrange("p j k n -> p (j k n)").rearrange("p (m e) -> p m e", m=KD)
        wqt = xin[:, :, :]

        ps = [ctx.enter_context(nc.psum_tensor(f"ps{i}", [P, 512], F32)) for i in range(8)]
        ps_edge = ps[0:4]
        ps_mix = ps[4:6]
        ps_sum = ps[6:8]

        rows_loaded = sem("rows_loaded")
        x_loaded = [sem(f"x_loaded{g}") for g in range(GROUPS)]
        pad_zeroed = sem("pad_zeroed")
        tables_loaded = sem("tables_loaded")
        weights_loaded = sem("weights_loaded")
        bounds_ready = sem("bounds_ready")
        bounds_stored = sem("bounds_stored")
        bounds_loaded = sem("bounds_loaded")
        ln_done = sem("ln_done")
        xn_stored = sem("xn_stored")
        eps_made = sem("eps_made")
        var_ready = sem("var_ready")
        std_ready = sem("std_ready")
        var_a = sem("var_a")
        rs_a_ready = sem("rs_a_ready")
        var_b = sem("var_b")
        rs_b_ready = sem("rs_b_ready")
        consts_made = sem("consts_made")
        turned = sem("turned")
        xnt_ready = sem("xnt_ready")
        pool_wts = sem("pool_wts")
        type_ready = sem("type_ready")
        v_own = Tally(sem("v_own"))
        p_own = Tally(sem("p_own"))
        zeros_made = sem("zeros_made")
        slots_cleared = sem("slots_cleared")
        rwt_turned = sem("rwt_turned")
        rwt_ready = sem("rwt_ready")
        loopw_ready = sem("loopw_ready")
        gathered = [sem(f"gathered{k}") for k in range(OCT)]
        slots_taken = sem("slots_taken")
        idx_staged = sem("idx_staged")
        multiplied = sem("multiplied")
        hit_built = sem("hit_built")
        wmat_built = sem("wmat_built")
        added = sem("added")
        acc_zeroed = sem("acc_zeroed")
        flag_ready = sem("flag_ready")
        max_mult = sem("max_mult")
        max_done = sem("max_done")
        shift_cols = sem("shift_cols")
        shift_turned = sem("shift_turned")
        shift_ready = sem("shift_ready")
        st_copied = sem("st_copied")
        keyed = sem("keyed")
        exped = sem("exped")
        summed = sem("summed")
        tn_ready = sem("tn_ready")
        s_turned = sem("s_turned")
        s_copied = sem("s_copied")
        lam_mult = sem("lam_mult")
        bn_ready = sem("bn_ready")
        m_mult = sem("m_mult")
        m_copied = sem("m_copied")
        cols_ready = sem("cols_ready")
        bias_turned = sem("bias_turned")
        bias_ready = sem("bias_ready")
        c_copied = sem("c_copied")
        early_mult = sem("early_mult")
        pre_out = sem("pre_out")
        mix_out = sem("mix_out")
        xin_loaded = [sem(f"xin_loaded{j}") for j in range(2)]
        early_stored = [sem(f"early_stored{j}") for j in range(2)]
        eout_free = sem("eout_free")
        slow_idx = sem("slow_idx")
        slow_gath = sem("slow_gath")
        slow_built = sem("slow_built")
        slow_seen = sem("slow_seen")
        slow_mult = sem("slow_mult")
        slow_step = sem("slow_step")
        acc_final = sem("acc_final")
        basis_loaded = sem("basis_loaded")
        early_loaded = [sem(f"early_loaded{j}") for j in range(4)]
        z_mult = sem("z_mult")
        u_done = sem("u_done")
        gelu_done = sem("gelu_done")
        lna_done = sem("lna_done")
        x2_done = sem("x2_done")
        lnb_done = sem("lnb_done")
        t_turned = sem("t_turned")
        t_copied = sem("t_copied")
        logits_mult = sem("logits_mult")
        routed = sem("routed")
        ranked = sem("ranked")
        rank_out = sem("rank_out")
        counted = sem("counted")
        pos_ready = sem("pos_ready")
        expert_ready = sem("expert_ready")
        scattered = sem("scattered")
        ffn_loaded = sem("ffn_loaded")
        f_in = [sem(f"f_in{s}") for s in range(FT)]
        f_turned = sem("f_turned")
        f_xt = sem("f_xt")
        f_hid = sem("f_hid")
        f_relu = sem("f_relu")
        f_hturn = sem("f_hturn")
        f_ht = sem("f_ht")
        f_out = sem("f_out")
        f_y = sem("f_y")
        f_relu_seen = sem("f_relu_seen")
        f_stored = [sem(f"f_stored{s}") for s in range(FT)]
        y_back = [sem(f"y_back{j}") for j in range(YB)]
        out_ready = sem("out_ready")
        out_stored = sem("out_stored")

        wm_flat = wmat[:, :, :, :].rearrange("p a b w -> p (a b w)")
        basis_sb = [cmat[:, :, :].rearrange("p k (c f) -> p (k c) f", f=D), wk_et[:, :].rearrange("p (b f) -> p b f", b=B)]
        early_in = [eout[:, 0, :], eout[:, 1, :],
                    xst[:, :, :, :].rearrange("p j k n -> p (j k n)"), xin[:, :, :].rearrange("p j f -> p (j f)")]
        far_w4 = wm_flat[:, 0:B * P]
        u = wq[:, :, :]
        h = wv[:, :, :]
        y = wm_flat[:, 0:2 * D].rearrange("p (j f) -> p j f", j=2)
        yg = wm_flat[:, 2 * D:4 * D].rearrange("p (j f) -> p j f", j=2)
        x2nt = gath[:, 0:2, :].rearrange("p j (k n) -> p j k n", k=KD)
        stat_a = gath[:, 2, 0:6]
        stat_b = gath[:, 2, 8:14]
        mv_a = gath[:, 2, 16:18]
        mv_b = gath[:, 2, 24:26]
        rs_a = gath[:, 2, 32:33]
        rs_b = gath[:, 2, 40:41]
        best = gath[:, 2, 48:56]
        best_i = gath[:, 2, 64:72].bitcast(U32)
        best_f = gath[:, 2, 80:81]
        wts_flat = wts[:, :, :].rearrange("p b t -> p (b t)")
        oh = gath_flat[:, 1600:1600 + NT * X // 2].bitcast(BF16).rearrange("p (t e) -> p t e", e=X)
        oh_sum = wts_flat[:, 800:800 + (NT + 1) * X // 2].bitcast(BF16).rearrange("p (t e) -> p t e", e=X)
        rk = wts_flat[:, 0:NT * X].rearrange("p (t e) -> p t e", e=X)
        rank_pick = gath_flat[:, 3 * D:3 * D + NT * X].rearrange("p (t e) -> p t e", e=X)
        cnt = rel[:, 0:X]
        n_tiles = rel[:, X:2 * X]
        tile_end = rel[:, 2 * X:3 * X]
        slot_base = rel[:, 3 * X:4 * X]
        over = acc_raw[:, 22000:22000 + X * NT].rearrange("p (e k) -> p e k", k=NT)
        ended = acc_raw[:, 23000:23000 + SLOT_TILES * X].rearrange("p (j e) -> p j e", e=X)
        pos_f = rel[:, 5 * X:5 * X + NT]
        ex_f = rel[:, 6 * X:6 * X + SLOT_TILES]
        pos_i = sb("pos_i", [P, NT], I32)
        ex_i = sb("ex_i", [P, SLOT_TILES], I32)
        at = 0
        w1_sb = acc_raw[:, at:at + X * KD * H].rearrange("p (e k h) -> p e k h", k=KD, h=H)
        at += X * KD * H
        w2_sb = acc_raw[0:H + 1, at:at + X * D]
        at += X * D
        b1_sb = acc_raw[0:1, at:at + X * H]
        at += X * H
        yback = acc_raw[:, at:at + NT * D].rearrange("p (t f) -> p t f", f=D)
        at += NT * D
        f_x = gath[:, 0:FT, :]
        f_xts = gath[:, FT:2 * FT, :]
        f_h = wm_flat[:, 0:FT * H].rearrange("p (s h) -> p s h", h=H)
        f_hts = wm_flat[0:H + 1, 4 * H:4 * H + FT * P].rearrange("p (s n) -> p s n", n=P)
        f_ys = [wq[:, 0, :], wq[:, 1, :], wv[:, 0, :], wv[:, 1, :]]

        block = ctx.enter_context(nc.Block())

        def edge_schedule(eng, octet):
            with eng.Fori(0, PAIRS) as i:
                octet(i, "max", i)
            q = PAIRS
            octet(q, "max_last", None)
            octet(q + 1, "sum_first", None)
            q += 2
            with eng.Fori(0, PAIRS - 1) as i:
                octet(i + q, "sum", i)
            q += PAIRS - 1
            octet(q, "sum_last", PAIRS - 1)
            octet(q + 1, "small_a", None)
            octet(q + 2, "small_b", None)
            q += 3
            with eng.Fori(0, PAIRS) as i:
                octet(i + q, "early", i)
            q += PAIRS
            octet(q, "early_last", None)
            q += 1
            with eng.Fori(0, NOCT - q) as i:
                octet(i + q, "plain", None)

        @block.sync
        def _(sp):
            sp.dma_start(dstr_i[0:ETAB // ROWG, :], dst_rows.rearrange("(r g) e -> r (g e)", g=ROWG)).then_inc(rows_loaded, 16)
            for g in range(GROUPS):
                full = GT if g < GROUPS - 1 else GT - 1
                a = g * GT * P
                if g == GROUPS - 1:
                    sp.wait_ge(pad_zeroed, 1)
                    sp.dma_start(xn[0:LAST, NT - 1, 0:D], x[(NT - 1) * P:N, :]).then_inc(x_loaded[g], 16)
                sp.dma_start(xn[:, g * GT:g * GT + full, 0:D],
                             x[a:a + full * P, :].rearrange("(t p) f -> p t f", p=P)).then_inc(x_loaded[g], 16)
            sp.wait_ge(bounds_ready, 1)
            sp.dma_start(bounds_d[0, :].rearrange("(r g) -> r g", g=ROWG), low[:, :]).then_inc(bounds_stored, 16)
            sp.dma_start(bounds_d[1, :].rearrange("(r g) -> r g", g=ROWG), span[:, :]).then_inc(bounds_stored, 16)
            sp.wait_ge(bounds_stored, 32)
            sp.dma_start(base_bc, bounds_d[0:1, :].to_broadcast([P, ETAB])).then_inc(bounds_loaded, 16)
            sp.dma_start(base_row[:, :], bounds_d[0:1, :]).then_inc(bounds_loaded, 16)
            sp.dma_start(span_row[:, :], bounds_d[1:2, :]).then_inc(bounds_loaded, 16)
            for g in range(GROUPS):
                full = GT if g < GROUPS - 1 else GT - 1
                a = g * GT * P
                sp.wait_ge(ln_done, g + 1)
                sp.dma_start(xn_d[a:a + full * P, :].rearrange("(t p) f -> p t f", p=P),
                             xn[:, g * GT:g * GT + full, 0:D]).then_inc(xn_stored, 16)
            sp.dma_start(xn_d[(NT - 1) * P:N, :], xn[0:LAST, NT - 1, 0:D]).then_inc(xn_stored, 16)
            sp.wait_ge(zeros_made, 1)
            sp.dma_start(slots_in_d.rearrange("(a p) f -> p a f", p=P),
                         zeros[:, :].unsqueeze(1).to_broadcast([P, SLOT_TILES, D])).then_inc(slots_cleared, 16)

            sp.wait_ge(s_copied, 1)
            sp.wait_ge(m_mult, 1)
            sp.sem_inc(eout_free, 2)
            with sp.Fori(0, PAIRS) as i:
                for j in range(2):
                    sp.wait_ge(mix_out, 2 * i + j + 1)
                    sp.dma_start(xin[:, j, :], x[ds(256 * i + P * j, P), :]).then_inc(xin_loaded[j], 16)
                for j in range(2):
                    sp.wait_ge(pre_out, 2 * i + j + 3)
                    sp.wait_ge(mix_out, 2 * i + j + 3)
                    sp.dma_start(early_d[ds(2 * i + j, 1), :, :].rearrange("a p f -> (a p) f"), eout[:, j, :]).then_inc(early_stored[j], 16)
                for j in range(2):
                    sp.wait_ge(early_stored[j], 16 * i + 16)
                    sp.sem_inc(eout_free, 1)
            t = NT - 1
            sp.wait_ge(mix_out, t + 1)
            sp.dma_start(xin[0:LAST, 0, :], x[t * P:N, :]).then_inc(xin_loaded[0], 16)
            sp.wait_ge(pre_out, t + 3)
            sp.wait_ge(mix_out, t + 3)
            sp.dma_start(early_d[t, 0:LAST, :], eout[0:LAST, 0, :]).then_inc(early_stored[0], 16)

            sp.wait_ge(early_stored[0], 16 * (PAIRS + 1))
            sp.wait_ge(early_stored[1], 16 * PAIRS)
            sp.wait_ge(early_mult, NT + 1)
            for m in range(KD):
                sp.dma_start(basis_sb[m], basis[:, m * P:(m + 1) * P, :].rearrange("b p f -> p b f")).then_inc(basis_loaded, 16)
            for t in range(NT):
                if t >= 4:
                    sp.wait_ge(x2_done, t - 3)
                sp.dma_start(early_in[t % 4][0:rows(t), :], early_d[t, 0:rows(t), :]).then_inc(early_loaded[t % 4], 16)
            sp.wait_ge(z_mult, NT)
            sp.dma_start(w1_sb, w1.rearrange("e (k p) h -> p e k h", p=P)).then_inc(ffn_loaded, 16)
            sp.dma_start(w2_sb[0:H, :].rearrange("p (e f) -> p e f", f=D), w2.rearrange("e h f -> h e f")).then_inc(ffn_loaded, 16)
            sp.dma_start(w2_sb[H:H + 1, :].rearrange("p (e f) -> p e f", f=D), b2.rearrange("(a e) f -> a e f", a=1)).then_inc(ffn_loaded, 16)
            sp.dma_start(b1_sb.rearrange("p (e h) -> p e h", h=H), b1.rearrange("(a e) h -> a e h", a=1)).then_inc(ffn_loaded, 16)

            sp.wait_ge(scattered, 16 * NT)
            for s in range(FT):
                sp.dma_start(f_x[:, s, :], slots_in_d[s * P:(s + 1) * P, :]).then_inc(f_in[s], 16)
            with sp.Fori(0, SLOT_TILES // FT - 1) as i:
                for s in range(FT):
                    sp.wait_ge(f_turned, FT * i + s + 1)
                    sp.dma_start(f_x[:, s, :], slots_in_d[ds((FT * i + FT + s) * P, P), :]).then_inc(f_in[s], 16)
                for s in range(FT):
                    sp.wait_ge(f_y, FT * i + FT + s + 1)
                    sp.dma_start(slots_out_d[ds((FT * i + s) * P, P), :], f_ys[s]).then_inc(f_stored[s], 16)
            for s in range(FT):
                sp.wait_ge(f_y, SLOT_TILES + s + 1)
                sp.dma_start(slots_out_d[(SLOT_TILES - FT + s) * P:(SLOT_TILES - FT + s + 1) * P, :], f_ys[s]).then_inc(f_stored[s], 16)
            for t in range(NT):
                sp.wait_ge(out_ready, t + 1)
                sp.dma_start(out[t * P:t * P + rows(t), :], x2[0:rows(t), t, :]).then_inc(out_stored, 16)
            sp.wait_ge(out_stored, 16 * NT)

        @block.gpsimd
        def _(pool):
            g = nc.gpsimd
            p_own.mark(g.memset(ident[:, :], 0.0))
            p_own.mark(g.memset(identb[:, :], 0.0))
            p_own.mark(g.memset(before[:, :], 1.0))
            p_own.mark(g.memset(neg_half[:, :], -0.5))
            g.memset(onesb[:, :], 1.0).then_inc(consts_made, 1)
            g.memset(ones_row[:, :], 1.0).then_inc(consts_made, 1)
            g.memset(zeros[:, :], 0.0).then_inc(zeros_made, 1)
            at = p_own.mark(g.iota(iota_i[:, :], pattern=[[1, P]], base=0, channel_multiplier=0))
            pool.wait_ge(p_own.sem, at)
            g.affine_select(out=ident[:, :], in_=ident[:, :], compare_op=ALU.not_equal, fill=1.0, base=0,
                            pattern=[[-1, P]], channel_multiplier=1).then_inc(consts_made, 1)
            g.affine_select(out=identb[:, :], in_=identb[:, :], compare_op=ALU.not_equal, fill=1.0, base=0,
                            pattern=[[-1, P]], channel_multiplier=1).then_inc(consts_made, 1)
            g.affine_select(out=before[:, :], in_=before[:, :], compare_op=ALU.is_gt, fill=0.0, base=0,
                            pattern=[[1, P]], channel_multiplier=-1).then_inc(consts_made, 1)
            g.tensor_copy(iota[:, :], iota_i[:, :]).then_inc(consts_made, 1)
            pool.wait_ge(type_ready, 1)
            for b in range(B // 2, B):
                at = p_own.mark(g.tensor_scalar(wts[:, b, :], type_f, 0.0, comp_bc[:, 0, b:b + 1], ALU.is_equal, ALU.mult))
                for r in range(1, R):
                    pool.wait_ge(p_own.sem, at)
                    at = p_own.mark(g.tensor_scalar(pool_term, type_f, float(r), comp_bc[:, r, b:b + 1], ALU.is_equal, ALU.mult))
                    pool.wait_ge(p_own.sem, at)
                    at = p_own.mark(g.tensor_tensor(wts[:, b, :], wts[:, b, :], pool_term, ALU.add))
            pool.wait_ge(p_own.sem, at)
            pool.sem_inc(pool_wts, 1)

            pool.wait_ge(xn_stored, 16 * (GROUPS + 1))
            pool.wait_ge(wmat_built, 2)

            def octet(q, beside, i):
                for k in range(OCT):
                    if k % (OCT // 2) == 0:
                        pool.wait_ge(idx_staged, 2 * q + 2 * k // OCT + 1)
                    pool.wait_ge(multiplied, OCT * q + k + 1)
                    pool.sem_inc(slots_taken, 1)
                    g.indirect_dma_start(gath[:, k, :], None, xn_d,
                                         bass.IndirectOffsetOnAxis(ap=idx_st[:, k:k + 1], axis=0)).then_inc(gathered[k], 16)

            edge_schedule(pool, octet)

            pool.wait_ge(flag_ready, 1)
            far = pool.value_load(flag[0:1, 0:1], min_val=0, max_val=1)
            with pool.If(far > 0):
                pool.wait_ge(multiplied, OCT * (NOCT + 1))
                pool.wait_ge(idx_staged, 2 * (NOCT + 1))
                with pool.Fori(0, NOCT * OCT) as t:
                    pool.wait_ge(slow_step, (2 * NT + 2) * t + 1)
                    g.tensor_copy(idx_st[:, 0:1], src_i[:, ds(t, 1)]).then_inc(slow_idx, 1)
                    pool.wait_ge(slow_idx, t + 1)
                    pool.sem_inc(slots_taken, 1)
                    g.indirect_dma_start(gath[:, 0, :], None, xn_d,
                                         bass.IndirectOffsetOnAxis(ap=idx_st[:, 0:1], axis=0)).then_inc(slow_gath, 16)
                    pool.wait_ge(slow_gath, 16 * t + 16)

            for t in range(NT + 2):
                a, b = t - 1, t - 2
                if 0 <= a < NT:
                    pool.wait_ge(var_a, a + 1)
                    at = p_own.mark(g.tensor_scalar(rs_a[0:rows(a), :], mv_a[0:rows(a), 1:2], EPS, None, ALU.add))
                    pool.wait_ge(p_own.sem, at)
                    g.tensor_tensor(rs_a[0:rows(a), :], rs_a[0:rows(a), :], neg_half[0:rows(a), :], ALU.pow).then_inc(rs_a_ready, 1)
                if 0 <= b < NT:
                    pool.wait_ge(var_b, b + 1)
                    at = p_own.mark(g.tensor_scalar(rs_b[0:rows(b), :], mv_b[0:rows(b), 1:2], EPS, None, ALU.add))
                    pool.wait_ge(p_own.sem, at)
                    g.tensor_tensor(rs_b[0:rows(b), :], rs_b[0:rows(b), :], neg_half[0:rows(b), :], ALU.pow).then_inc(rs_b_ready, 1)
                if 0 <= a < NT:
                    n = rows(a)
                    pool.wait_ge(lna_done, a + 1)
                    at = p_own.mark(g.tensor_tensor(yg[0:n, a % 2, :], y[0:n, a % 2, :], gam_bc[0:n, :], ALU.mult))
                    pool.wait_ge(early_loaded[a % 4], 16 * (a // 4 + 1))
                    pool.wait_ge(p_own.sem, at)
                    g.tensor_tensor(x2[0:n, a, :], yg[0:n, a % 2, :], early_in[a % 4][0:n, D:2 * D], ALU.add).then_inc(x2_done, 1)
            pool.wait_ge(pos_ready, 1)
            pool.wait_ge(slots_cleared, 16)
            for t in range(NT):
                n = rows(t)
                g.indirect_dma_start(slots_in_d, bass.IndirectOffsetOnAxis(ap=pos_i[0:n, t:t + 1], axis=0),
                                     x2n[0:n, t, :], None).then_inc(scattered, 16)
            for s in range(FT):
                pool.wait_ge(f_stored[s], 16 * SLOT_TILES // FT)
            for t in range(NT):
                n = rows(t)
                if t >= YB:
                    pool.wait_ge(y_back[t % YB], 16 * (t // YB))
                g.indirect_dma_start(yback[0:n, t, :], None, slots_out_d,
                                     bass.IndirectOffsetOnAxis(ap=pos_i[0:n, t:t + 1], axis=0)).then_inc(y_back[t % YB], 16)

        @block.scalar
        def _(act):
            s = nc.scalar
            act.dma_start(type_i, type_t).then_inc(tables_loaded, 16)
            act.dma_start(comp_bc[:, :, :], comp.rearrange("(a r) b -> a r b", a=1).to_broadcast([P, R, B])).then_inc(tables_loaded, 16)
            act.dma_start(dst_i[:, :], dst_t).then_inc(tables_loaded, 16)
            act.dma_start(src_i[:, :], src_t).then_inc(tables_loaded, 16)
            for dst, frm in ((wk[:, :, :], w_qk[1].rearrange("(k p) f -> p k f", p=P)),
                             (cmat[:, :, 0:D], loop_w.rearrange("(k p) f -> p k f", p=P)),
                             (wq[:, :, :], w_qk[0].rearrange("(k p) f -> p k f", p=P)),
                             (wv[:, :, :], w_v.rearrange("(k p) f -> p k f", p=P)),
                             (rw[:, :], router_w),
                             (rb_row[:, :], router_b.rearrange("(a e) -> a e", a=1)),
                             (bv_bc[:, :], b_v.rearrange("(a f) -> a f", a=1).to_broadcast([P, D])),
                             (gam_bc[:, :], ln_gamma.rearrange("(a f) -> a f", a=1).to_broadcast([P, D]))):
                act.dma_start(dst, frm).then_inc(weights_loaded, 16)
            with nc.allow_non_contiguous_dma(reason="a few short bias vectors as columns"):
                for dst, frm in ((qk_col[:, 0, :], b_qk[0]), (qk_col[:, 1, :], b_qk[1]), (bn_col[:, 0, :], bn_gamma),
                                 (bn_col[:, 1, :], bn_beta), (hb_col[:, 0, :], h_bias), (hb_col[:, 1, :], ln_beta)):
                    act.dma_start(dst, frm.rearrange("(k p) -> p k", p=P)).then_inc(weights_loaded, 16)

            act.wait_ge(eps_made, 1)
            for g in range(GROUPS):
                act.wait_ge(var_ready, g + 1)
                s.activation(rstd[:, g * GT:(g + 1) * GT], mv[:, g * GT:(g + 1) * GT, 1], ACT.Sqrt, bias=eps_col[:, :]).then_inc(std_ready, 1)
            for w in range(PAIRS + 1):
                n = 2 * P if w < PAIRS else P
                act.wait_ge(turned, w + 1)
                s.copy(xnt[:, :, 2 * P * w:2 * P * w + n],
                       ps_mix[w % 2][:, :].rearrange("p (k n) -> p k n", k=KD)[:, :, 0:n]).then_inc(xnt_ready, 1)
            act.wait_ge(rwt_turned, 1)
            s.copy(rwt[:, :, :], ps_sum[0][:, 0:KD * X].rearrange("p (k e) -> p k e", k=KD)).then_inc(rwt_ready, 1)
            act.wait_ge(tables_loaded, 64)
            s.copy(idx_st[:, :], src_i[:, 0:OCT]).then_inc(idx_staged, 2)

            def stage_idx(q, half):
                w = OCT // 2
                for k in range(half * w, half * w + w):
                    act.wait_ge(gathered[k], 16 * q + 16)
                s.copy(idx_st[:, half * w:half * w + w], src_i[:, ds(OCT * q + OCT + half * w, w)]).then_inc(idx_staged, 1)

            def octet(q, beside, i):
                if beside in ("sum", "sum_last"):
                    act.wait_ge(keyed, 2 * i + 1)
                    for j in range(2):
                        s.copy(xst[:, j, :, :], xnt[:, :, ds(2 * P * i + P * j, P)]).then_inc(st_copied, 1)
                if beside == "sum_first":
                    s.copy(xst[:, 0, :, :], xnt[:, :, (NT - 1) * P:NT * P]).then_inc(st_copied, 1)
                if beside == "early":
                    act.wait_ge(early_mult, 2 * i + 1)
                    for j in range(2):
                        s.copy(xst[:, j, :, :], xnt[:, :, ds(2 * P * i + P * j, P)]).then_inc(c_copied, 1)
                if beside == "early_last":
                    act.wait_ge(early_mult, 2 * PAIRS + 1)
                    s.copy(xst[:, 0, :, :], xnt[:, :, (NT - 1) * P:NT * P]).then_inc(c_copied, 1)
                if beside == "small_b":
                    act.wait_ge(m_mult, 1)
                    s.copy(cmat[:, :, D:2 * D], ps_mix[0][:, :].rearrange("p (k f) -> p k f", k=KD)).then_inc(m_copied, 1)
                stage_idx(q, 0)
                if beside in ("sum", "sum_last"):
                    act.wait_ge(summed, 2 * i + 1)
                    for j in range(2):
                        act.wait_ge(keyed, 2 * i + j + 2)
                        s.activation(et[:, j, :], ps_mix[j][:, 0:D], ACT.Exp).then_inc(exped, 1)
                if beside == "sum_first":
                    act.wait_ge(keyed, 1)
                    s.activation(et[0:LAST, 0, :], ps_mix[0][0:LAST, 0:D], ACT.Exp).then_inc(exped, 1)
                if beside == "early":
                    for j in range(2):
                        act.wait_ge(early_mult, 2 * i + j + 2)
                        act.wait_ge(eout_free, 2 * i + j + 1)
                        s.copy(eout[:, j, 0:D], ps_mix[j][:, 0:D]).then_inc(pre_out, 1)
                if beside == "early_last":
                    act.wait_ge(early_mult, NT + 1)
                    act.wait_ge(eout_free, NT)
                    s.copy(eout[0:LAST, 0, 0:D], ps_mix[0][0:LAST, 0:D]).then_inc(pre_out, 1)
                if beside == "small_a":
                    act.wait_ge(s_turned, 2)
                    s.copy(tnt, ps_mix[0][:, :].rearrange("p (k d) -> p k d", k=KD)).then_inc(s_copied, 1)
                    s.copy(wqt, ps_mix[1][:, :].rearrange("p (m i) -> p m i", m=KD)).then_inc(s_copied, 1)
                stage_idx(q, 1)
                if beside == "small_a":
                    act.wait_ge(var_ready, GROUPS + 1)
                    s.activation(rstd[:, 0:KD], mv[:, 0:KD, 1], ACT.Sqrt, bias=eps_col[:, :]).then_inc(std_ready, 1)

            act.sem_inc(pre_out, 2)
            edge_schedule(act, octet)

            for t in range(NT + 5):
                if t < NT:
                    n = rows(t)
                    act.wait_ge(u_done, t + 1)
                    if t >= 2:
                        act.wait_ge(lna_done, t - 1)
                    s.activation(h[0:n, t % 2, :], u[0:n, t % 2, :], ACT.Gelu).then_inc(gelu_done, 1)
                a = t - 3
                if 0 <= a < NT:
                    act.wait_ge(t_turned, a + 1)
                    if a >= 2:
                        act.wait_ge(logits_mult, a - 1)
                    s.copy(x2nt[:, a % 2, :, 0:rows(a)],
                           ps[2 + a % 2][:, 0:KD * P].rearrange("p (k n) -> p k n", k=KD)[:, :, 0:rows(a)]).then_inc(t_copied, 1)
                b = t - 5
                if 0 <= b < NT:
                    act.wait_ge(ranked, b + 1)
                    s.copy(rk[:, b, :], ps[6 + b % 2][:, 0:X]).then_inc(rank_out, 1)

            act.wait_ge(pos_ready, 1)
            with act.Fori(0, SLOT_TILES // FT) as i:
                for f in range(FT):
                    act.wait_ge(f_turned, FT * i + f + 1)
                    s.copy(f_xts[:, f, :], ps[f][:, 0:D]).then_inc(f_xt, 1)
                for f in range(FT):
                    act.wait_ge(f_hturn, FT * i + f + 1)
                    s.copy(f_hts[0:H, f, :], ps[f][0:H, 0:P]).then_inc(f_ht, 1)

        @block.tensor
        def _(pe):
            t_ = nc.tensor
            pe.wait_ge(consts_made, 6)
            for w in range(PAIRS + 1):
                tiles = [2 * w, 2 * w + 1] if w < PAIRS else [NT - 1]
                pe.wait_ge(ln_done, tiles[-1] // GT + 1)
                if w >= 2:
                    pe.wait_ge(xnt_ready, w - 1)
                for j, t in enumerate(tiles):
                    for k in range(KD):
                        ins = t_.transpose(ps_mix[w % 2][:, k * 2 * P + j * P:k * 2 * P + j * P + P],
                                           xn[:, t, k * P:(k + 1) * P], ident[:, :])
                ins.then_inc(turned, 1)
            pe.wait_ge(weights_loaded, 16 * 14)
            for k in range(KD):
                ins = t_.transpose(ps_sum[0][:, k * X:(k + 1) * X], rw[:, k * P:(k + 1) * P], ident[0:X, 0:X])
            ins.then_inc(rwt_turned, 1)
            pe.wait_ge(xnt_ready, PAIRS + 1)
            pe.wait_ge(rwt_ready, 1)
            pe.wait_ge(loopw_ready, 1)
            pe.sem_inc(multiplied, OCT)

            def edges(q, half):
                pe.wait_ge(wmat_built, 2 * q + half + 1)
                for k in range(half * OCT // 2, (half + 1) * OCT // 2):
                    pe.wait_ge(gathered[k], 16 * q + 16)
                    pe.wait_ge(added, OCT * q + k + 1)
                    for m in range(KD):
                        ins = t_.matmul(ps_edge[k % 4][:, m * B * WIN:(m + 1) * B * WIN], gath[:, k, m * P:(m + 1) * P],
                                        wmat[:, k, :, :].rearrange("p b w -> p (b w)"), start=True, stop=True)
                    ins.then_inc(multiplied, 1)

            def key_max(first, n):
                for m in range(KD):
                    for k in range(KD):
                        ins = t_.matmul(ps_mix[0][:, m * 2 * P:m * 2 * P + n], wk[:, k, m * P:(m + 1) * P],
                                        xnt[:, k, ds(first, n)], start=k == 0, stop=k == KD - 1)
                ins.then_inc(max_mult, 1)

            def keys(j, n):
                for k in range(KD):
                    t_.matmul(ps_mix[j][0:n, 0:D], xst[:, j, k, 0:n], wk[:, k, :], start=k == 0, stop=False)
                t_.matmul(ps_mix[j][0:n, 0:D], onesb[0:3, 0:n], shift3[:, :], start=False, stop=True).then_inc(keyed, 1)

            def weigh(j, tile, n, start, stop):
                for m in range(KD):
                    ins = t_.matmul(ps_sum[m][:, 0:D + 1], et[0:n, j, m * P:(m + 1) * P], tile,
                                    start=start, stop=stop)
                ins.then_inc(summed, 1)

            def early(j, n):
                for k in range(KD):
                    t_.matmul(ps_mix[j][0:n, :], xst[:, j, k, 0:n], cmat[:, k, :], start=k == 0, stop=False)
                t_.matmul(ps_mix[j][0:n, :], onesb[0:3, 0:n], bias3[:, :], start=False, stop=True).then_inc(early_mult, 1)

            def octet(q, beside, i):
                edges(q, 0)
                if beside == "max":
                    pe.wait_ge(max_done, i + 1)
                    key_max(2 * P * i, 2 * P)
                elif beside == "max_last":
                    pe.wait_ge(max_done, PAIRS + 1)
                    key_max((NT - 1) * P, LAST)
                elif beside == "sum_first":
                    pe.wait_ge(shift_ready, 1)
                    pe.wait_ge(st_copied, 1)
                    keys(0, LAST)
                elif beside in ("sum", "sum_last"):
                    pe.wait_ge(exped, 2 * i + 1)
                    for j in range(2):
                        pe.wait_ge(st_copied, 2 * i + j + 2)
                        keys(j, P)
                elif beside == "small_a":
                    for m in range(KD):
                        for k in range(KD):
                            if m == k == 0:
                                pe.wait_ge(exped, NT)
                            t_.transpose(ps_mix[1][:, m * D + k * P:m * D + (k + 1) * P],
                                         wq[:, k, m * P:(m + 1) * P], ident[:, :])
                    pe.wait_ge(tn_ready, 2)
                    pe.sem_inc(s_turned, 1)
                    for m in range(KD):
                        for k in range(KD):
                            ins = t_.transpose(ps_mix[0][:, k * D + m * P:k * D + (m + 1) * P],
                                               tn[:, m, k * P:(k + 1) * P], ident[:, :])
                    ins.then_inc(s_turned, 1)
                elif beside == "small_b":
                    pe.wait_ge(bn_ready, 2)
                    for k in range(KD):
                        for m in range(KD):
                            t_.matmul(ps_mix[0][:, k * D:(k + 1) * D], wqt[:, m, k * P:(k + 1) * P], lam[:, m, :],
                                      start=m == 0, stop=m == KD - 1)
                    for k in range(KD):
                        for m in range(KD):
                            ins = t_.matmul(ps_mix[1][:, k:k + 1], lam[:, m, k * P:(k + 1) * P], qk_col[:, 0, m:m + 1],
                                            start=m == 0, stop=m == KD - 1)
                    ins.then_inc(m_mult, 1)
                elif beside == "early":
                    for j in range(2):
                        pe.wait_ge(c_copied, 2 * i + j + 1)
                        pe.wait_ge(pre_out, 2 * i + j + 1)
                        pe.wait_ge(mix_out, 2 * i + j + 1)
                        early(j, P)
                elif beside == "early_last":
                    pe.wait_ge(c_copied, NT)
                    pe.wait_ge(pre_out, NT)
                    pe.wait_ge(mix_out, NT)
                    early(0, LAST)
                edges(q, 1)
                if beside == "max_last":
                    pe.wait_ge(shift_cols, 1)
                    for m in range(KD):
                        ins = t_.matmul(ps_sum[0][0:3, m * P:(m + 1) * P], parts[:, m, :], identb[:, :], start=True, stop=True)
                    ins.then_inc(shift_turned, 1)
                elif beside == "sum_first":
                    pe.wait_ge(exped, 1)
                    weigh(0, xn[0:LAST, NT - 1, :], LAST, True, False)
                elif beside in ("sum", "sum_last"):
                    for j in range(2):
                        pe.wait_ge(exped, 2 * i + j + 2)
                        weigh(j, xn_raw[:, ds((D + 1) * (2 * i + j), D + 1)], P, False, beside == "sum_last" and j == 1)
                elif beside == "small_a":
                    pe.wait_ge(s_copied, 2)
                    for m in range(KD):
                        for k in range(KD):
                            ins = t_.matmul(ps_sum[0][:, m * D:(m + 1) * D], tnt[:, k, m * P:(m + 1) * P], wv[:, k, :],
                                            start=k == 0, stop=k == KD - 1)
                    ins.then_inc(lam_mult, 1)
                elif beside == "small_b":
                    pe.wait_ge(cols_ready, 1)
                    for c in range(4):
                        ins = t_.matmul(ps_sum[1][0:3, c * P:(c + 1) * P], parts[:, c, :], identb[:, :], start=True, stop=True)
                    ins.then_inc(bias_turned, 1)
                    pe.wait_ge(bias_ready, 1)
                    pe.wait_ge(m_copied, 1)
                    pe.sem_inc(early_mult, 1)

            edge_schedule(pe, octet)

            pe.wait_ge(flag_ready, 1)
            far = pe.value_load(flag[0:1, 0:1], min_val=0, max_val=1)
            with pe.If(far > 0):
                with pe.Fori(0, NOCT * OCT) as t:
                    pe.wait_ge(slow_gath, 16 * t + 16)
                    pe.sem_inc(slow_seen, 1)
                    with pe.Fori(0, NT) as w:
                        pe.wait_ge(slow_built, NT * t + w + 1)
                        for m in range(KD):
                            ins = t_.matmul(ps_edge[m][:, :], gath[:, 0, m * P:(m + 1) * P], far_w4,
                                            start=True, stop=True)
                        ins.then_inc(slow_mult, 1)

            pe.wait_ge(acc_final, 1)
            pe.wait_ge(basis_loaded, 32)
            for t in range(NT + 6):
                a = t - 3
                if 0 <= a < NT:
                    n = rows(a)
                    pe.wait_ge(lnb_done, a + 1)
                    if a >= 2:
                        pe.wait_ge(t_copied, a - 1)
                    for k in range(KD):
                        ins = t_.transpose(ps[2 + a % 2][:, k * P:k * P + n], x2n[0:n, a, k * P:(k + 1) * P], ident[0:n, 0:n])
                    ins.then_inc(t_turned, 1)
                b = t - 4
                if 0 <= b < NT:
                    n = rows(b)
                    pe.wait_ge(t_copied, b + 1)
                    if b >= 2:
                        pe.wait_ge(routed, b - 1)
                    for k in range(KD):
                        t_.matmul(ps[4 + b % 2][0:n, 0:X], x2nt[:, b % 2, k, 0:n], rwt[:, k, :], start=k == 0, stop=False)
                    t_.matmul(ps[4 + b % 2][0:n, 0:X], ones_row[:, 0:n], rb_row[:, :], start=False, stop=True).then_inc(logits_mult, 1)
                c = t - 5
                if 0 <= c < NT:
                    pe.wait_ge(routed, c + 1)
                    if c >= 2:
                        pe.wait_ge(rank_out, c - 1)
                    t_.matmul(ps[6 + c % 2][:, 0:X], before[:, :], oh[:, c, :], start=True, stop=False)
                    t_.matmul(ps[6 + c % 2][:, 0:X], onesb[:, :], oh_sum[:, c, :], start=False, stop=True).then_inc(ranked, 1)
                if t < NT:
                    n = rows(t)
                    if t >= 2:
                        pe.wait_ge(u_done, t - 1)
                    for m in range(KD):
                        for b in range(B):
                            ins = t_.matmul(ps[t % 2][0:n, 0:D], acc[:, m * B + b, t * P:t * P + n], basis_sb[m][:, b, :],
                                            start=m == b == 0, stop=m == KD - 1 and b == B - 1)
                    ins.then_inc(z_mult, 1)
            t_.matmul(ps[0][:, 0:X], onesb[:, :], oh_sum[:, NT, :], start=True, stop=True).then_inc(counted, 1)

            pe.wait_ge(expert_ready, 1)
            pe.wait_ge(rank_out, NT)
            pe.wait_ge(ffn_loaded, 64)
            with pe.Fori(0, SLOT_TILES // FT) as i:
                for f in range(FT):
                    pe.wait_ge(f_in[f], 16 * i + 16)
                    pe.wait_ge(f_ht, FT * i + f + 1)
                    for k in range(KD):
                        ins = t_.transpose(ps[f][:, k * P:(k + 1) * P], f_x[:, f, k * P:(k + 1) * P], ident[:, :])
                    ins.then_inc(f_turned, 1)
                for f in range(FT):
                    e = pe.value_load(ex_i[0:1, ds(FT * i + f, 1)], min_val=0, max_val=X - 1)
                    pe.wait_ge(f_xt, FT * i + f + 1)
                    pe.wait_ge(f_y, FT * i + f + 1)
                    w1_e = w1_sb.rearrange("p e k h -> p (e k h)")
                    for k in range(KD):
                        t_.matmul(ps[FT + f][:, 0:H], f_xts[:, f, k * P:(k + 1) * P], w1_e[:, ds(e * (KD * H) + k * H, H)],
                                  start=k == 0, stop=False)
                    t_.matmul(ps[FT + f][:, 0:H], ones_row[:, :], b1_sb[:, ds(e * H, H)], start=False, stop=True).then_inc(f_hid, 1)
                for f in range(FT):
                    pe.wait_ge(f_relu, FT * i + f + 1)
                    pe.sem_inc(f_relu_seen, 1)
                    t_.transpose(ps[f][0:H, 0:P], f_h[:, f, :], ident[:, :]).then_inc(f_hturn, 1)
                for f in range(FT):
                    e = pe.value_load(ex_i[0:1, ds(FT * i + f, 1)], min_val=0, max_val=X - 1)
                    pe.wait_ge(f_ht, FT * i + FT + f + 1)
                    t_.matmul(ps[FT + f][:, 0:D], f_hts[:, f, :], w2_sb[:, ds(e * D, D)], start=True, stop=True).then_inc(f_out, 1)

        @block.vector
        def _(v):
            d = nc.vector

            def own(at):
                v.wait_ge(v_own.sem, at)

            d.memset(xn[:, NT - 1, :], 0.0).then_inc(pad_zeroed, 1)
            v.wait_ge(pad_zeroed, 1)
            v_own.mark(d.memset(xn[:, :, D:D + 1], 1.0))
            d.memset(eps_col[:, :], EPS).then_inc(eps_made, 1)
            v.wait_ge(rows_loaded, 16)
            er = ETAB // ROWG
            dr = dstr_i[0:er, :].rearrange("p (g e) -> p g e", g=ROWG)
            v_own.mark(d.tensor_reduce(low[:, :], dr, AX.X, ALU.min))
            at = v_own.mark(d.tensor_reduce(high[:, :], dr, AX.X, ALU.max))
            own(at)
            d.tensor_tensor(span[:, :], high[:, :], low[:, :], ALU.subtract).then_inc(bounds_ready, 1)
            v.wait_ge(tables_loaded, 64)
            d.tensor_copy(type_f, type_i).then_inc(type_ready, 1)
            for g in range(GROUPS):
                v.wait_ge(x_loaded[g], 16 if g < GROUPS - 1 else 32)
                tiles = range(g * GT, (g + 1) * GT)
                for t in tiles:
                    at = v_own.mark(d.bn_stats(stats[:, t % GT, :], xn[:, t, 0:D]))
                own(at)
                for t in tiles:
                    at = v_own.mark(d.bn_aggr(mv[:, t, :], stats[:, t % GT, :]))
                own(at)
                v.sem_inc(var_ready, 1)
                v.wait_ge(std_ready, g + 1)
                at = v_own.mark(d.reciprocal(rstd[:, tiles[0]:tiles[-1] + 1], rstd[:, tiles[0]:tiles[-1] + 1]))
                own(at)
                for t in tiles:
                    at = v_own.mark(d.tensor_scalar(xn[:, t, 0:D], xn[:, t, 0:D], mv[:, t, 0:1], rstd[:, t:t + 1], ALU.subtract, ALU.mult))
                own(at)
                v.sem_inc(ln_done, 1)
            v.wait_ge(bounds_loaded, 48)
            v_own.mark(d.tensor_tensor(rel[:, :], dst_i[:, :], base_bc, ALU.subtract))
            v.wait_ge(type_ready, 1)
            for r in range(R):
                at_rel = v_own.mark(d.tensor_scalar(is_rel[r % 2], type_f, float(r), None, ALU.is_equal))
                if r > 0:
                    own(at)
                own(at_rel)
                for b in range(B // 2):
                    if r == 0:
                        at = v_own.mark(d.tensor_scalar(wts[:, b, :], is_rel[0], comp_bc[:, r, b:b + 1], None, ALU.mult))
                    else:
                        at = v_own.mark(d.scalar_tensor_tensor(wts[:, b, :], is_rel[r % 2], comp_bc[:, r, b:b + 1], wts[:, b, :], ALU.mult, ALU.add))
            own(at)
            v.wait_ge(consts_made, 6)
            v.wait_ge(pool_wts, 1)

            def build(q, half):
                w = OCT // 2
                n = 2 * q + half
                cut = ds(OCT * q + half * w, w) if not isinstance(q, int) else slice(OCT * q + half * w, OCT * q + half * w + w)
                v.wait_ge(multiplied, OCT * q + half * w + w) if not isinstance(q, int) or q > 0 else None
                v.wait_ge(wmat_built, n) if not isinstance(q, int) or n > 0 else None
                d.tensor_tensor(hit[:, :, :], rel[:, cut].unsqueeze(2).to_broadcast([P, w, WIN]),
                                iota[:, 0:WIN].unsqueeze(1).to_broadcast([P, w, WIN]), ALU.is_equal).then_inc(hit_built, 1)
                v.wait_ge(hit_built, n + 1)
                d.tensor_tensor(wmat[:, half * w:half * w + w, :, :], hit[:, :, :].unsqueeze(2).to_broadcast([P, w, B, WIN]),
                                wts[:, :, cut].rearrange("p b t -> p t b").unsqueeze(3).to_broadcast([P, w, B, WIN]),
                                ALU.mult).then_inc(wmat_built, 1)

            build(0, 0)
            build(0, 1)
            d.memset(acc_raw[:, :], 0.0).then_inc(acc_zeroed, 1)
            for k in range(KD):
                blockk = cmat[:, k, k * P:(k + 1) * P]
                if k == 0:
                    v.wait_ge(weights_loaded, 16 * 14)
                at = v_own.mark(d.tensor_tensor(blockk, blockk, ident[:, :], ALU.add))
            own(at)
            v.sem_inc(loopw_ready, 1)
            v.wait_ge(acc_zeroed, 1)
            v.sem_inc(added, 4)
            v.sem_inc(max_done, 1)
            v.sem_inc(mix_out, 2)

            def add_edges(q, half):
                for k in range(half * OCT // 2, (half + 1) * OCT // 2):
                    base = v.value_load(base_row[0:1, ds(OCT * q + k, 1)], min_val=0, max_val=N - 1)
                    place = acc[:, :, ds(base, WIN)]
                    v.wait_ge(multiplied, OCT * q + k + OCT + 1)
                    v.wait_ge(added, OCT * q + k + 4)
                    d.tensor_tensor(place, place, ps_edge[k % 4][:, 0:KD * B * WIN].rearrange("p (c w) -> p c w", w=WIN),
                                    ALU.add).then_inc(added, 1)

            def split3(ncol, at):
                own(at)
                at = v_own.mark(d.tensor_copy(parts[:, 0:ncol, 0], cols[:, 0:ncol]))
                own(at)
                at = v_own.mark(d.tensor_tensor(rest[:, 0, 0:ncol], cols[:, 0:ncol], parts[:, 0:ncol, 0], ALU.subtract))
                own(at)
                at = v_own.mark(d.tensor_copy(parts[:, 0:ncol, 1], rest[:, 0, 0:ncol]))
                own(at)
                at = v_own.mark(d.tensor_tensor(rest[:, 1, 0:ncol], rest[:, 0, 0:ncol], parts[:, 0:ncol, 1], ALU.subtract))
                own(at)
                return d.tensor_copy(parts[:, 0:ncol, 2], rest[:, 1, 0:ncol])

            def octet(q, beside, i):
                add_edges(q, 0)
                build(q + 1, 0)
                if beside == "early":
                    for j in range(2):
                        v.wait_ge(early_mult, 2 * i + j + 2)
                        v.wait_ge(pre_out, 2 * i + j + 3)
                        v.wait_ge(xin_loaded[j], 16 * i + 16)
                        v.wait_ge(eout_free, 2 * i + j + 1)
                        d.tensor_tensor(eout[:, j, D:2 * D], ps_mix[j][:, D:2 * D], xin[:, j, :], ALU.add).then_inc(mix_out, 1)
                elif beside == "early_last":
                    v.wait_ge(early_mult, NT + 1)
                    v.wait_ge(pre_out, NT + 2)
                    v.wait_ge(eout_free, NT)
                    v.wait_ge(xin_loaded[0], 16 * (PAIRS + 1))
                    d.tensor_tensor(eout[0:LAST, 0, D:2 * D], ps_mix[0][0:LAST, D:2 * D], xin[0:LAST, 0, :], ALU.add).then_inc(mix_out, 1)
                elif beside == "small_a":
                    v.wait_ge(summed, NT)
                    for m in range(KD):
                        at = v_own.mark(d.reciprocal(cols[:, m:m + 1], ps_sum[m][:, D:D + 1]))
                    own(at)
                    for m in range(KD):
                        d.tensor_scalar(tn[:, m, :], ps_sum[m][:, 0:D], cols[:, m:m + 1], None, ALU.mult).then_inc(tn_ready, 1)
                elif beside == "small_b":
                    v.wait_ge(m_mult, 1)
                    v_own.mark(d.tensor_copy(cols[:, 0:KD], hb_col[:, 0, :]))
                    at = v_own.mark(d.tensor_tensor(cols[:, KD:2 * KD], ps_mix[1][:, 0:KD], hb_col[:, 1, :], ALU.add))
                    split3(4, at).then_inc(cols_ready, 1)
                add_edges(q, 1)
                build(q + 1, 1)
                if beside == "max":
                    v.wait_ge(max_mult, i + 1)
                    d.tensor_reduce(top[:, ds(i, 1), :].rearrange("p a m -> p (a m)"), ps_mix[0][:, :].rearrange("p (m n) -> p m n", m=KD), AX.X, ALU.max).then_inc(max_done, 1)
                elif beside == "max_last":
                    v.wait_ge(max_mult, PAIRS + 1)
                    d.tensor_reduce(top[:, PAIRS, :], ps_mix[0][:, :].rearrange("p (m n) -> p m n", m=KD)[:, :, 0:LAST], AX.X, ALU.max).then_inc(max_done, 1)
                    v.wait_ge(max_done, PAIRS + 2)
                    at = v_own.mark(d.tensor_reduce(cols[:, 4:4 + KD], top[:, :, :].rearrange("p i m -> p m i"), AX.X, ALU.max))
                    own(at)
                    at = v_own.mark(d.tensor_tensor(cols[:, 6:6 + KD], cols[:, 4:4 + KD], qk_col[:, 1, :], ALU.add))
                    own(at)
                    at = v_own.mark(d.tensor_tensor(cols[:, 0:KD], qk_col[:, 1, :], cols[:, 6:6 + KD], ALU.subtract))
                    split3(KD, at).then_inc(shift_cols, 1)
                    v.wait_ge(shift_turned, 1)
                    d.tensor_copy(shift3[:, :], ps_sum[0][0:3, 0:D]).then_inc(shift_ready, 1)
                elif beside == "small_a":
                    v.wait_ge(lam_mult, 1)
                    for m in range(KD):
                        at = v_own.mark(d.tensor_tensor(lam[:, m, :], ps_sum[0][:, m * D:(m + 1) * D], bv_bc[:, :], ALU.add))
                    own(at)
                    for m in range(KD):
                        at = v_own.mark(d.bn_stats(stats[:, m, :], lam[:, m, :]))
                    own(at)
                    for m in range(KD):
                        at = v_own.mark(d.bn_aggr(mv[:, m, :], stats[:, m, :]))
                    own(at)
                    v.sem_inc(var_ready, 1)
                    v.wait_ge(std_ready, GROUPS + 1)
                    at = v_own.mark(d.reciprocal(rstd[:, 0:KD], rstd[:, 0:KD]))
                    own(at)
                    at = v_own.mark(d.tensor_tensor(cols[:, 0:KD], rstd[:, 0:KD], bn_col[:, 0, :], ALU.mult))
                    own(at)
                    for m in range(KD):
                        at = v_own.mark(d.tensor_scalar(lam[:, m, :], lam[:, m, :], mv[:, m, 0:1], cols[:, m:m + 1], ALU.subtract, ALU.mult))
                    own(at)
                    for m in range(KD):
                        d.tensor_scalar(lam[:, m, :], lam[:, m, :], bn_col[:, 1, m:m + 1], None, ALU.add).then_inc(bn_ready, 1)
                elif beside == "small_b":
                    v.wait_ge(bias_turned, 1)
                    d.tensor_copy(bias3[:, :], ps_sum[1][0:3, :]).then_inc(bias_ready, 1)

            edge_schedule(v, octet)

            at = v_own.mark(d.tensor_reduce(high[0:1, 0:1], span_row[:, :], AX.X, ALU.max))
            own(at)
            d.tensor_scalar(flag[:, :], high[0:1, 0:1], float(WIN - 1), None, ALU.is_gt).then_inc(flag_ready, 1)
            v.wait_ge(flag_ready, 1)
            v.wait_ge(added, NOCT * OCT + 4)
            far = v.value_load(flag[0:1, 0:1], min_val=0, max_val=1)
            far_w = cols[:, 0:B]
            far_dst = cols[:, 5:6]
            sgath = hit[:, :, :].rearrange("p a w -> p (a w)")
            with v.If(far > 0):
                v.wait_ge(multiplied, OCT * (NOCT + 1))
                v.sem_inc(slow_step, 1)
                with v.Fori(0, NOCT * OCT) as t:
                    a = (2 * NT + 2) * t
                    v.wait_ge(slow_step, a + 1)
                    for b in range(B):
                        ins = d.scalar_tensor_tensor(far_w[:, b:b + 1], rel[:, ds(t, 1)], float(WIN), wts[:, b, ds(t, 1)], ALU.is_ge, ALU.mult)
                    d.tensor_copy(far_dst, dst_i[:, ds(t, 1)]).then_inc(slow_step, 1)
                    with v.Fori(0, NT) as w:
                        v.wait_ge(slow_step, a + 2 * w + 2)
                        d.tensor_scalar(sgath, iota[:, :], far_dst, None, ALU.is_equal).then_inc(slow_step, 1)
                        v.wait_ge(slow_step, a + 2 * w + 3)
                        d.tensor_tensor(far_w4.rearrange("p (b n) -> p b n", b=B),
                                        sgath.unsqueeze(1).to_broadcast([P, B, P]),
                                        far_w.unsqueeze(2).to_broadcast([P, B, P]), ALU.mult).then_inc(slow_built, 1)
                        d.tensor_scalar(far_dst, far_dst, float(-P), None, ALU.add)
                        v.wait_ge(slow_mult, NT * t + w + 1)
                        for m in range(KD):
                            place = acc[:, m * B:(m + 1) * B, ds(P * w, P)]
                            ins = d.tensor_tensor(place, place, ps_edge[m][:, :].rearrange("p (b n) -> p b n", b=B), ALU.add)
                        ins.then_inc(slow_step, 1)
                    v.wait_ge(slow_step, a + 2 * NT + 2)
                    v.sem_inc(slow_step, 1)
            v.sem_inc(acc_final, 1)

            v.wait_ge(early_mult, NT + 1)
            v_own.mark(d.memset(oh[:, NT - 1, :], 0.0))
            at = v_own.mark(d.memset(oh_sum[:, 0, :], 0.0))
            own(at)
            for t in range(NT + 5):
                if t < NT:
                    n = rows(t)
                    v.wait_ge(z_mult, t + 1)
                    v.wait_ge(early_loaded[t % 4], 16 * (t // 4 + 1))
                    if t >= 2:
                        v.wait_ge(gelu_done, t - 1)
                    d.tensor_tensor(u[0:n, t % 2, :], ps[t % 2][0:n, 0:D], early_in[t % 4][0:n, 0:D], ALU.add).then_inc(u_done, 1)
                a, b = t - 1, t - 2
                if 0 <= a < NT:
                    v.wait_ge(gelu_done, a + 1)
                    at_a = v_own.mark(d.bn_stats(stat_a[0:rows(a), :], h[0:rows(a), a % 2, :]))
                if 0 <= b < NT:
                    v.wait_ge(x2_done, b + 1)
                    at_b = v_own.mark(d.bn_stats(stat_b[0:rows(b), :], x2[0:rows(b), b, :]))
                if 0 <= a < NT:
                    own(at_a)
                    d.bn_aggr(mv_a[0:rows(a), :], stat_a[0:rows(a), :]).then_inc(var_a, 1)
                if 0 <= b < NT:
                    own(at_b)
                    d.bn_aggr(mv_b[0:rows(b), :], stat_b[0:rows(b), :]).then_inc(var_b, 1)
                c = t - 4
                if 0 <= c < NT:
                    n = rows(c)
                    v.wait_ge(logits_mult, c + 1)
                    at = v_own.mark(d.max(best[0:n, :], ps[4 + c % 2][0:n, 0:X]))
                    own(at)
                    at = v_own.mark(d.max_index(best_i[0:n, :], best[0:n, :], ps[4 + c % 2][0:n, 0:X]))
                    own(at)
                    at = v_own.mark(d.tensor_copy(best_f[0:n, :], best_i[0:n, 0:1]))
                    own(at)
                    at = v_own.mark(d.tensor_scalar(oh[0:n, c, :], iota[0:n, 0:X], best_f[0:n, :], None, ALU.is_equal))
                    own(at)
                    d.tensor_tensor(oh_sum[:, c + 1, :], oh_sum[:, c, :], oh[:, c, :], ALU.add).then_inc(routed, 1)
                    v.wait_ge(routed, c + 1)
                if 0 <= a < NT:
                    v.wait_ge(rs_a_ready, a + 1)
                    if a >= 2:
                        v.wait_ge(x2_done, a - 1)
                    d.tensor_scalar(y[0:rows(a), a % 2, :], h[0:rows(a), a % 2, :], mv_a[0:rows(a), 0:1], rs_a[0:rows(a), :],
                                    ALU.subtract, ALU.mult).then_inc(lna_done, 1)
                if 0 <= b < NT:
                    v.wait_ge(rs_b_ready, b + 1)
                    d.tensor_scalar(x2n[0:rows(b), b, :], x2[0:rows(b), b, :], mv_b[0:rows(b), 0:1], rs_b[0:rows(b), :],
                                    ALU.subtract, ALU.mult).then_inc(lnb_done, 1)

            v.wait_ge(z_mult, NT)
            v.wait_ge(counted, 1)
            at = v_own.mark(d.tensor_copy(cnt, ps[0][:, 0:X]))
            at = v_own.mark(d.tensor_scalar(wm_flat[:, 0:SLOT_TILES], iota[:, 0:SLOT_TILES], float(P), None, ALU.mult))
            own(at)
            at = v_own.mark(d.tensor_tensor(over, cnt.unsqueeze(2).to_broadcast([P, X, NT]),
                                            wm_flat[:, 0:NT].unsqueeze(1).to_broadcast([P, X, NT]), ALU.is_gt))
            own(at)
            at = v_own.mark(d.tensor_reduce(n_tiles, over, AX.X, ALU.add))
            own(at)
            at = v_own.mark(d.tensor_tensor_scan(tile_end, onesb[:, 0:X], n_tiles, 0.0, ALU.mult, ALU.add))
            own(at)
            at = v_own.mark(d.tensor_tensor(slot_base, tile_end, n_tiles, ALU.subtract))
            own(at)
            at = v_own.mark(d.tensor_scalar(slot_base, slot_base, float(P), None, ALU.mult))
            own(at)
            v.wait_ge(rank_out, NT)
            at = v_own.mark(d.tensor_tensor(rk, rk, slot_base.unsqueeze(1).to_broadcast([P, NT, X]), ALU.add))
            own(at)
            at = v_own.mark(d.tensor_tensor(rank_pick, rk, oh[:, :, :], ALU.mult))
            own(at)
            at = v_own.mark(d.tensor_reduce(pos_f, rank_pick, AX.X, ALU.add))
            own(at)
            d.tensor_copy(pos_i[:, :], pos_f).then_inc(pos_ready, 1)
            at = v_own.mark(d.tensor_tensor(ended, tile_end.unsqueeze(1).to_broadcast([P, SLOT_TILES, X]),
                                            iota[:, 0:SLOT_TILES].unsqueeze(2).to_broadcast([P, SLOT_TILES, X]), ALU.is_le))
            own(at)
            at = v_own.mark(d.tensor_reduce(ex_f, ended, AX.X, ALU.add))
            own(at)
            at = v_own.mark(d.tensor_scalar(ex_f, ex_f, float(X - 1), None, ALU.min))
            own(at)
            at = v_own.mark(d.tensor_copy(ex_i[:, :], ex_f))
            at = v_own.mark(d.memset(wm_flat[H:H + 1, 4 * H:4 * H + FT * P], 1.0))
            own(at)
            v.sem_inc(expert_ready, 1)
            v.sem_inc(f_y, FT)
            v.sem_inc(f_ht, FT)

            def relus(i, first=False):
                for f in range(FT):
                    v.wait_ge(f_hid, FT * i + f + 1)
                    d.tensor_scalar(f_h[:, f, :], ps[FT + f][:, 0:H], 0.0, None, ALU.max).then_inc(f_relu, 1)
                for f in range(FT):
                    v.wait_ge(f_out, FT * i + f + 1)
                    if not first:
                        v.wait_ge(f_stored[f], 16 * i)
                    d.tensor_scalar(f_ys[f], ps[FT + f][:, 0:D], 0.0, None, ALU.max).then_inc(f_y, 1)

            relus(0, first=True)
            with v.Fori(1, SLOT_TILES // FT) as i:
                relus(i)
            for t in range(NT):
                n = rows(t)
                v.wait_ge(y_back[t % YB], 16 * (t // YB) + 16)
                d.tensor_tensor(x2[0:n, t, :], x2[0:n, t, :], yback[0:n, t, :], ALU.add).then_inc(out_ready, 1)


_INS = ["x", "src_t", "type_t", "dst_t", "dst_rows", "L0_gnn_basis", "L0_gnn_comp", "L0_gnn_loop_w", "L0_gnn_h_bias",
        "L0_gnn_ln_gamma", "L0_gnn_ln_beta", "L0_mix_W_qk", "L0_mix_b_qk", "L0_mix_W_v", "L0_mix_b_v", "L0_mix_gamma",
        "L0_mix_beta", "L0_ffn_router_w", "L0_ffn_router_b", "L0_ffn_W1", "L0_ffn_b1", "L0_ffn_W2", "L0_ffn_b2"]


def lay_out(inputs):
    import numpy as np

    arrays = {k: np.ascontiguousarray(v) for k, v in inputs.items()}
    pad = ETAB * P - E
    src = np.pad(arrays.pop("src"), (0, pad)).reshape(ETAB, P)
    types = np.pad(arrays.pop("edge_type_8"), (0, pad), constant_values=R).reshape(ETAB, P)
    dst = np.pad(arrays.pop("dst"), (0, pad), mode="edge").reshape(ETAB, P)
    arrays["src_t"] = np.ascontiguousarray(src.T)
    arrays["type_t"] = np.ascontiguousarray(types.T)
    arrays["dst_t"] = np.ascontiguousarray(dst.T)
    arrays["dst_rows"] = np.ascontiguousarray(dst)
    return arrays


def kernel(**inputs):
    import numpy as np
    import concourse.bacc as bacc
    from concourse.bass_utils import run_bass_kernel_spmd

    laid = lay_out(inputs)
    nc = bacc.Bacc("TRN2", target_bir_lowering=False, num_devices=1)
    arrays, args = {}, []
    for name in _INS:
        a = laid[name]
        arrays[f"in_{name}"] = a
        args.append(nc.dram_tensor(f"in_{name}", a.shape, mybir.dt.from_np(a.dtype), kind="ExternalInput").ap())
    args.append(nc.dram_tensor("out_0", (N, D), F32, kind="ExternalOutput").ap())
    gps_layer(nc, *args)
    r = run_bass_kernel_spmd(nc, [arrays], core_ids=[0])
    return r.results[0]["out_0"]
```

```python
from contextlib import ExitStack

import concourse.bass as bass
from concourse import mybir
from concourse.bass import ds

P = 128
N, D, E = 3125, 256, 50000
R, B, X, H = 8, 4, 32, 64
KD = D // P
NT = -(-N // P)
LAST = N - (NT - 1) * P
NPAD = NT * P
WIN = 40
PAIR = 2
OCT = 8
NOCT = -(-E // (P * OCT))
ETAB = (NOCT + 1) * OCT
ROWG = 4
TG = P // R
TC = ETAB // TG
CB = 512 // (TG * B)
PAIRS = (NT - 1) // 2
SLOT_TILES = X + (N - X) // P
GROUPS, GT = 5, NT // 5
GA = 3
EPS = 1e-5
FT = 4
CLEARS = 16
YB = 8
WROW = ROWG // PAIR
NWIN = ETAB // PAIR
assert OCT == 4 * PAIR and NT % GROUPS == 0 and SLOT_TILES % FT == 0 and ETAB % ROWG == 0

ALU = mybir.AluOpType
ACT = mybir.ActivationFunctionType
AX = mybir.AxisListType
F32, BF16 = mybir.dt.float32, mybir.dt.bfloat16
I32, U32 = mybir.dt.int32, mybir.dt.uint32


def rows(t):
    return P if t < NT - 1 else LAST


def pairs_within(g):
    return [w for w in range(PAIRS + 1) if min(2 * w + 1, NT - 1) // GT == g]


class Tally:

    def __init__(self, sem, at=0):
        self.sem, self.at = sem, at

    def mark(self, instruction, by=1):
        instruction.then_inc(self.sem, by)
        self.at += by
        return self.at


def gps_layer(nc, x, src_t, type_rows, dst_t, dst_rows, basis, comp, loop_w, h_bias, ln_gamma, ln_beta,
              w_qk, b_qk, w_v, b_v, bn_gamma, bn_beta, router_w, router_b, w1, b1_t, w2, b2, relation_of,
              group_mask, out):
    with ExitStack() as ctx:
        def sb(name, shape, dt=F32):
            return ctx.enter_context(nc.sbuf_tensor(name, shape, dt))

        def sem(name):
            return ctx.enter_context(nc.semaphore(name))

        xn_d = nc.dram_tensor("xn_d", [N, D], F32).ap()
        bounds_d = nc.dram_tensor("bounds_d", [2, NWIN], I32).ap()
        early_d = nc.dram_tensor("early_d", [NT, P, 2 * D], F32).ap()
        slots_in_d = nc.dram_tensor("slots_in_d", [SLOT_TILES * P, D], F32).ap()
        slots_out_d = nc.dram_tensor("slots_out_d", [SLOT_TILES * P, D], F32).ap()

        acc_raw = sb("acc_raw", [P, KD * B * NPAD])
        acc = acc_raw[:, :].rearrange("p (c n) -> p c n", n=NPAD)
        xn_raw = sb("xn_raw", [P, NT * (D + 1)])
        xn = xn_raw[:, :].rearrange("p (t f) -> p t f", f=D + 1)
        x2 = xn_raw[:, 0:NT * D].rearrange("p (t f) -> p t f", f=D)
        xnt_raw = sb("xnt_raw", [P, KD * NPAD])
        xnt = xnt_raw[:, :].rearrange("p (k n) -> p k n", n=NPAD)
        x2n = xnt_raw[:, :].rearrange("p (t f) -> p t f", f=D)
        gath = sb("gath", [P, OCT, D])
        wmat = sb("wmat", [P, OCT, B, WIN])
        hit = sb("hit", [P, OCT // 2, WIN])
        rel = sb("rel", [P, ETAB])
        wts = sb("wts", [P, B, ETAB])
        src_i = sb("src_i", [P, ETAB], I32)
        dst_i = sb("dst_i", [P, ETAB], I32)
        idx_st = sb("idx_st", [P, OCT], I32)
        base_row = sb("base_row", [1, NWIN], I32)
        comp_rep = sb("comp_rep", [P, B])
        comp_diag = sb("comp_diag", [P, TG, B])
        rel_of = sb("rel_of", [P, 1])
        gath_flat = gath[:, :, :].rearrange("p a f -> p (a f)")
        base_bc = gath_flat[:, 2 * ETAB:2 * ETAB + NWIN].bitcast(I32)
        type_g = acc_raw[:, 0:TC * P].bitcast(I32)
        type_hot = acc_raw[:, 0:TC * P]
        dstr_i = gath_flat[:, 3 * ETAB:3 * ETAB + ROWG * P].bitcast(I32)
        wk_et = sb("wk_et", [P, 2 * KD * D])
        wk = wk_et[:, 0:KD * D].rearrange("p (k f) -> p k f", k=KD)
        et = wk_et[:, KD * D:2 * KD * D].rearrange("p (j f) -> p j f", j=2)
        wq = sb("wq", [P, KD, D])
        wv = sb("wv", [P, KD, D])
        cmat = sb("cmat", [P, KD, 2 * D])
        xst = sb("xst", [P, 2, KD, P])
        xin = sb("xin", [P, 2, D])
        eout = sb("eout", [P, 2, 2 * D])
        ident = sb("ident", [P, P])
        identb = sb("identb", [P, P], BF16)
        before = sb("before", [P, P], BF16)
        onesb = sb("onesb", [P, P], BF16)
        ones_row = sb("ones_row", [1, P])
        iota_i = sb("iota_i", [P, P], I32)
        iota = sb("iota", [P, P])
        zeros = sb("zeros", [P, D])
        eps_col = sb("eps_col", [P, 1])
        neg_half = sb("neg_half", [P, 1])
        stats = sb("stats", [P, GT, 6])
        mv = sb("mv", [P, NT, 2])
        rstd = sb("rstd", [P, NT])
        nmr = sb("nmr", [P, NT])
        low = sb("low", [ETAB // ROWG, WROW], I32)
        high = sb("high", [ETAB // ROWG, WROW], I32)
        span = sb("span", [ETAB // ROWG, WROW], I32)
        span_row = sb("span_row", [1, NWIN], I32)
        flag = sb("flag", [1, 1], I32)
        top = sb("top", [P, (PAIRS + 1) * KD])
        cols = sb("cols", [P, 8])
        qk_col = sb("qk_col", [P, 2, KD])
        bn_col = sb("bn_col", [P, 2, KD])
        hb_col = sb("hb_col", [P, 2, KD])
        parts = sb("parts", [P, 4, 3], BF16)
        rest = sb("rest", [P, 2, 4])
        shift3 = sb("shift3", [3, D], BF16)
        bias3 = sb("bias3", [3, 2 * D], BF16)
        bv_bc = sb("bv_bc", [P, D])
        gam_bc = sb("gam_bc", [P, D])
        rw = sb("rw", [X, D])
        rwt = sb("rwt", [P, KD, X])
        rb_row = sb("rb_row", [1, X])
        tn = eout[:, 0, :].rearrange("p (m f) -> p m f", m=KD)
        tnt = eout[:, 1, :].rearrange("p (k d) -> p k d", k=KD)
        lam = xst[:, :, :, :].rearrange("p j k n -> p (j k n)").rearrange("p (m e) -> p m e", m=KD)
        wqt = xin[:, :, :]

        ps = [ctx.enter_context(nc.psum_tensor(f"ps{i}", [P, 512], F32)) for i in range(8)]
        ps_edge = ps[0:4]
        ps_mix = ps[4:6]
        ps_sum = ps[6:8]

        rows_loaded = sem("rows_loaded")
        x_loaded = [sem(f"x_loaded{g}") for g in range(GROUPS)]
        pad_zeroed = sem("pad_zeroed")
        tables_loaded = sem("tables_loaded")
        weights_loaded = sem("weights_loaded")
        bounds_ready = sem("bounds_ready")
        bounds_stored = sem("bounds_stored")
        bounds_loaded = sem("bounds_loaded")
        rel_ready = sem("rel_ready")
        ln_done = sem("ln_done")
        ln_act = sem("ln_act")
        rstd_ready = sem("rstd_ready")
        xn_stored = sem("xn_stored")
        eps_made = sem("eps_made")
        var_ready = sem("var_ready")
        std_ready = sem("std_ready")
        var_a = sem("var_a")
        rs_a_ready = sem("rs_a_ready")
        var_b = sem("var_b")
        rs_b_ready = sem("rs_b_ready")
        consts_made = sem("consts_made")
        turned = sem("turned")
        xnt_ready = sem("xnt_ready")
        types_loaded = sem("types_loaded")
        hot_ready = sem("hot_ready")
        wts_mult = sem("wts_mult")
        wts_ready = sem("wts_ready")
        v_own = Tally(sem("v_own"))
        p_own = Tally(sem("p_own"))
        zeros_made = sem("zeros_made")
        slots_cleared = sem("slots_cleared")
        rwt_turned = sem("rwt_turned")
        rwt_ready = sem("rwt_ready")
        loopw_ready = sem("loopw_ready")
        gathered = [sem(f"gathered{k}") for k in range(OCT)]
        slots_taken = sem("slots_taken")
        idx_staged = sem("idx_staged")
        multiplied = sem("multiplied")
        hit_built = sem("hit_built")
        wmat_built = sem("wmat_built")
        added = sem("added")
        acc_zeroed = sem("acc_zeroed")
        flag_ready = sem("flag_ready")
        max_mult = sem("max_mult")
        max_done = sem("max_done")
        shift_cols = sem("shift_cols")
        shift_turned = sem("shift_turned")
        shift_ready = sem("shift_ready")
        st_copied = sem("st_copied")
        keyed = sem("keyed")
        exped = sem("exped")
        summed = sem("summed")
        tn_ready = sem("tn_ready")
        s_turned = sem("s_turned")
        s_copied = sem("s_copied")
        lam_mult = sem("lam_mult")
        bn_ready = sem("bn_ready")
        m_mult = sem("m_mult")
        m_copied = sem("m_copied")
        cols_ready = sem("cols_ready")
        bias_turned = sem("bias_turned")
        bias_ready = sem("bias_ready")
        c_copied = sem("c_copied")
        early_mult = sem("early_mult")
        pre_out = sem("pre_out")
        mix_out = sem("mix_out")
        xin_loaded = [sem(f"xin_loaded{j}") for j in range(2)]
        early_stored = [sem(f"early_stored{j}") for j in range(2)]
        eout_free = sem("eout_free")
        slow_idx = sem("slow_idx")
        slow_gath = sem("slow_gath")
        slow_built = sem("slow_built")
        slow_seen = sem("slow_seen")
        slow_mult = sem("slow_mult")
        slow_step = sem("slow_step")
        acc_final = sem("acc_final")
        basis_loaded = sem("basis_loaded")
        early_loaded = [sem(f"early_loaded{j}") for j in range(4)]
        z_mult = sem("z_mult")
        u_done = sem("u_done")
        gelu_done = sem("gelu_done")
        lna_done = sem("lna_done")
        x2_done = sem("x2_done")
        lnb_done = sem("lnb_done")
        t_turned = sem("t_turned")
        t_copied = sem("t_copied")
        logits_mult = sem("logits_mult")
        routed = sem("routed")
        ranked = sem("ranked")
        rank_out = sem("rank_out")
        counted = sem("counted")
        pos_ready = sem("pos_ready")
        expert_ready = sem("expert_ready")
        scattered = sem("scattered")
        ffn_loaded = sem("ffn_loaded")
        f_in = [sem(f"f_in{s}") for s in range(FT)]
        f_turned = sem("f_turned")
        f_xt = sem("f_xt")
        f_hid = sem("f_hid")
        f_relu = sem("f_relu")
        f_out = sem("f_out")
        f_y = sem("f_y")
        f_w1 = sem("f_w1")
        f_stored = [sem(f"f_stored{s}") for s in range(FT)]
        y_back = [sem(f"y_back{j}") for j in range(YB)]
        out_ready = sem("out_ready")
        out_stored = sem("out_stored")

        wm_flat = wmat[:, :, :, :].rearrange("p a b w -> p (a b w)")
        basis_sb = [cmat[:, :, :].rearrange("p k (c f) -> p (k c) f", f=D), wk_et[:, :].rearrange("p (b f) -> p b f", b=B)]
        early_in = [eout[:, 0, :], eout[:, 1, :],
                    xst[:, :, :, :].rearrange("p j k n -> p (j k n)"), xin[:, :, :].rearrange("p j f -> p (j f)")]
        far_w4 = wm_flat[:, 0:B * P]
        u = wq[:, :, :]
        h = wv[:, :, :]
        y = wm_flat[:, 0:2 * D].rearrange("p (j f) -> p j f", j=2)
        yg = wm_flat[:, 2 * D:4 * D].rearrange("p (j f) -> p j f", j=2)
        x2nt = gath[:, 0:2, :].rearrange("p j (k n) -> p j k n", k=KD)
        stat_a = gath[:, 2, 0:6]
        stat_b = gath[:, 2, 8:14]
        mv_a = gath[:, 2, 16:18]
        mv_b = gath[:, 2, 24:26]
        rs_a = gath[:, 2, 32:33]
        rs_b = gath[:, 2, 40:41]
        best = gath[:, 2, 48:56]
        best_i = gath[:, 2, 64:72].bitcast(U32)
        best_f = gath[:, 2, 80:81]
        wts_flat = wts[:, :, :].rearrange("p b t -> p (b t)")
        oh = gath_flat[:, 1600:1600 + NT * X // 2].bitcast(BF16).rearrange("p (t e) -> p t e", e=X)
        oh_sum = wts_flat[:, 800:800 + (NT + 1) * X // 2].bitcast(BF16).rearrange("p (t e) -> p t e", e=X)
        rk = wts_flat[:, 0:NT * X].rearrange("p (t e) -> p t e", e=X)
        rank_pick = gath_flat[:, 3 * D:3 * D + NT * X].rearrange("p (t e) -> p t e", e=X)
        cnt = rel[:, 0:X]
        n_tiles = rel[:, X:2 * X]
        tile_end = rel[:, 2 * X:3 * X]
        slot_base = rel[:, 3 * X:4 * X]
        over = acc_raw[:, 22000:22000 + X * NT].rearrange("p (e k) -> p e k", k=NT)
        ended = acc_raw[:, 23000:23000 + SLOT_TILES * X].rearrange("p (j e) -> p j e", e=X)
        pos_f = rel[:, 5 * X:5 * X + NT]
        ex_f = rel[:, 6 * X:6 * X + SLOT_TILES]
        pos_i = sb("pos_i", [P, NT], I32)
        ex_i = sb("ex_i", [P, SLOT_TILES + FT], I32)
        at = 0
        w1_sb = acc_raw[:, at:at + X * KD * H].rearrange("p (e k h) -> p e k h", k=KD, h=H)
        at += X * KD * H
        w2_sb = acc_raw[0:H + 1, at:at + X * D]
        at += X * D
        b1_sb = acc_raw[0:H, at:at + X]
        at += X
        yback = acc_raw[:, at:at + NT * D].rearrange("p (t f) -> p t f", f=D)
        at += NT * D
        f_x = gath[:, 0:FT, :]
        f_xts = gath[:, FT:2 * FT, :]
        w1_flat = w1_sb.rearrange("p e k h -> p (e k h)")
        f_w = wm_flat[:, 0:FT * KD * H].rearrange("p (s h) -> p s h", s=FT)
        f_hts = wm_flat[0:H + 1, FT * KD * H:FT * KD * H + FT * P].rearrange("p (s n) -> p s n", n=P)
        f_ys = [wq[:, 0, :], wq[:, 1, :], wv[:, 0, :], wv[:, 1, :]]

        block = ctx.enter_context(nc.Block())

        def edge_schedule(eng, octet):
            with eng.Fori(0, PAIRS) as i:
                octet(i, "max", i)
            q = PAIRS
            octet(q, "max_last", None)
            octet(q + 1, "sum_first", None)
            q += 2
            with eng.Fori(0, PAIRS - 1) as i:
                octet(i + q, "sum", i)
            q += PAIRS - 1
            octet(q, "sum_last", PAIRS - 1)
            octet(q + 1, "small_a", None)
            octet(q + 2, "small_b", None)
            q += 3
            with eng.Fori(0, PAIRS) as i:
                octet(i + q, "early", i)
            q += PAIRS
            octet(q, "early_last", None)
            q += 1
            with eng.Fori(0, NOCT - q) as i:
                octet(i + q, "plain", None)

        def row_values(eng, row, greatest):
            return nc.values_load_multi_w_load_instructions(row, engines=(eng.engine,), min_val=0, max_val=greatest)[1]

        @block.sync
        def _(sp):
            sp.dma_start(dstr_i[0:ETAB // ROWG, :], dst_rows.rearrange("(r g) e -> r (g e)", g=ROWG)).then_inc(rows_loaded, 16)
            for g in range(GROUPS):
                full = GT if g < GROUPS - 1 else GT - 1
                a = g * GT * P
                if g == GROUPS - 1:
                    sp.wait_ge(pad_zeroed, 1)
                    sp.dma_start(xn[0:LAST, NT - 1, 0:D], x[(NT - 1) * P:N, :]).then_inc(x_loaded[g], 16)
                sp.dma_start(xn[:, g * GT:g * GT + full, 0:D],
                             x[a:a + full * P, :].rearrange("(t p) f -> p t f", p=P)).then_inc(x_loaded[g], 16)
            sp.wait_ge(bounds_ready, 1)
            sp.dma_start(bounds_d[0, :].rearrange("(r g) -> r g", g=WROW), low[:, :]).then_inc(bounds_stored, 16)
            sp.dma_start(bounds_d[1, :].rearrange("(r g) -> r g", g=WROW), span[:, :]).then_inc(bounds_stored, 16)
            sp.wait_ge(bounds_stored, 32)
            sp.dma_start(base_bc, bounds_d[0:1, :].to_broadcast([P, NWIN])).then_inc(bounds_loaded, 16)
            sp.dma_start(base_row[:, :], bounds_d[0:1, :]).then_inc(bounds_loaded, 16)
            sp.dma_start(span_row[:, :], bounds_d[1:2, :]).then_inc(bounds_loaded, 16)
            for dst, frm in ((wk[:, :, :], w_qk[1].rearrange("(k p) f -> p k f", p=P)),
                             (cmat[:, :, 0:D], loop_w.rearrange("(k p) f -> p k f", p=P)),
                             (wq[:, :, :], w_qk[0].rearrange("(k p) f -> p k f", p=P)),
                             (wv[:, :, :], w_v.rearrange("(k p) f -> p k f", p=P)),
                             (rw[:, :], router_w),
                             (rb_row[:, :], router_b.rearrange("(a e) -> a e", a=1)),
                             (bv_bc[:, :], b_v.rearrange("(a f) -> a f", a=1).to_broadcast([P, D])),
                             (gam_bc[:, :], ln_gamma.rearrange("(a f) -> a f", a=1).to_broadcast([P, D]))):
                sp.dma_start(dst, frm).then_inc(weights_loaded, 16)
            with nc.allow_non_contiguous_dma(reason="a few short bias vectors as columns"):
                for dst, frm in ((qk_col[:, 0, :], b_qk[0]), (qk_col[:, 1, :], b_qk[1]), (bn_col[:, 0, :], bn_gamma),
                                 (bn_col[:, 1, :], bn_beta), (hb_col[:, 0, :], h_bias), (hb_col[:, 1, :], ln_beta)):
                    sp.dma_start(dst, frm.rearrange("(k p) -> p k", p=P)).then_inc(weights_loaded, 16)
            for g in range(GROUPS):
                full = GT if g < GROUPS - 1 else GT - 1
                a = g * GT * P
                sp.wait_ge(ln_done, g + 1)
                sp.wait_ge(ln_act, (g + 1) * GA)
                sp.dma_start(xn_d[a:a + full * P, :].rearrange("(t p) f -> p t f", p=P),
                             xn[:, g * GT:g * GT + full, 0:D]).then_inc(xn_stored, 16)
            sp.dma_start(xn_d[(NT - 1) * P:N, :], xn[0:LAST, NT - 1, 0:D]).then_inc(xn_stored, 16)
            sp.wait_ge(s_copied, 1)
            sp.wait_ge(m_mult, 1)
            sp.sem_inc(eout_free, 2)
            with sp.Fori(0, PAIRS) as i:
                for j in range(2):
                    sp.wait_ge(mix_out, 2 * i + j + 1)
                    sp.dma_start(xin[:, j, :], x[ds(256 * i + P * j, P), :]).then_inc(xin_loaded[j], 16)
                for j in range(2):
                    sp.wait_ge(pre_out, 2 * i + j + 3)
                    sp.wait_ge(mix_out, 2 * i + j + 3)
                    sp.dma_start(early_d[ds(2 * i + j, 1), :, :].rearrange("a p f -> (a p) f"), eout[:, j, :]).then_inc(early_stored[j], 16)
                for j in range(2):
                    sp.wait_ge(early_stored[j], 16 * i + 16)
                    sp.sem_inc(eout_free, 1)
            t = NT - 1
            sp.wait_ge(mix_out, t + 1)
            sp.dma_start(xin[0:LAST, 0, :], x[t * P:N, :]).then_inc(xin_loaded[0], 16)
            sp.wait_ge(pre_out, t + 3)
            sp.wait_ge(mix_out, t + 3)
            sp.dma_start(early_d[t, 0:LAST, :], eout[0:LAST, 0, :]).then_inc(early_stored[0], 16)

            sp.wait_ge(zeros_made, 1)
            sp.wait_ge(early_stored[0], 16 * (PAIRS + 1))
            sp.wait_ge(early_stored[1], 16 * PAIRS)
            sp.wait_ge(early_mult, NT + 1)
            for m in range(KD):
                sp.dma_start(basis_sb[m], basis[:, m * P:(m + 1) * P, :].rearrange("b p f -> p b f")).then_inc(basis_loaded, 16)
            for t in range(NT):
                if t >= 4:
                    sp.wait_ge(x2_done, t - 3)
                sp.dma_start(early_in[t % 4][0:rows(t), :], early_d[t, 0:rows(t), :]).then_inc(early_loaded[t % 4], 16)
                if t < CLEARS:
                    a, b = t * SLOT_TILES // CLEARS * P, (t + 1) * SLOT_TILES // CLEARS * P
                    sp.dma_start(slots_in_d[a:b, :].rearrange("(a p) f -> p a f", p=P),
                                 zeros[:, :].unsqueeze(1).to_broadcast([P, (b - a) // P, D])).then_inc(slots_cleared, 16)
            sp.wait_ge(z_mult, NT)
            sp.dma_start(w1_sb, w1.rearrange("e (k p) h -> p e k h", p=P)).then_inc(ffn_loaded, 16)
            sp.dma_start(w2_sb[0:H, :].rearrange("p (e f) -> p e f", f=D), w2.rearrange("e h f -> h e f")).then_inc(ffn_loaded, 16)
            sp.dma_start(w2_sb[H:H + 1, :].rearrange("p (e f) -> p e f", f=D), b2.rearrange("(a e) f -> a e f", a=1)).then_inc(ffn_loaded, 16)
            sp.dma_start(b1_sb, b1_t).then_inc(ffn_loaded, 16)

            sp.wait_ge(scattered, 16 * NT)
            for s in range(FT):
                sp.dma_start(f_x[:, s, :], slots_in_d[s * P:(s + 1) * P, :]).then_inc(f_in[s], 16)
            with sp.Fori(0, SLOT_TILES // FT - 1) as i:
                for s in range(FT):
                    sp.wait_ge(f_turned, FT * i + s + 1)
                    sp.dma_start(f_x[:, s, :], slots_in_d[ds((FT * i + FT + s) * P, P), :]).then_inc(f_in[s], 16)
                for s in range(FT):
                    sp.wait_ge(f_y, FT * i + FT + s + 1)
                    sp.dma_start(slots_out_d[ds((FT * i + s) * P, P), :], f_ys[s]).then_inc(f_stored[s], 16)
            for s in range(FT):
                sp.wait_ge(f_y, SLOT_TILES + s + 1)
                sp.dma_start(slots_out_d[(SLOT_TILES - FT + s) * P:(SLOT_TILES - FT + s + 1) * P, :], f_ys[s]).then_inc(f_stored[s], 16)
            for t in range(NT):
                sp.wait_ge(out_ready, t + 1)
                sp.dma_start(out[t * P:t * P + rows(t), :], x2[0:rows(t), t, :]).then_inc(out_stored, 16)
            sp.wait_ge(out_stored, 16 * NT)

        @block.gpsimd
        def _(pool):
            g = nc.gpsimd
            p_own.mark(g.memset(ident[:, :], 0.0))
            p_own.mark(g.memset(identb[:, :], 0.0))
            p_own.mark(g.memset(before[:, :], 1.0))
            p_own.mark(g.memset(neg_half[:, :], -0.5))
            g.memset(onesb[:, :], 1.0).then_inc(consts_made, 1)
            g.memset(ones_row[:, :], 1.0).then_inc(consts_made, 1)
            g.memset(zeros[:, :], 0.0).then_inc(zeros_made, 1)
            at = p_own.mark(g.iota(iota_i[:, :], pattern=[[1, P]], base=0, channel_multiplier=0))
            pool.wait_ge(p_own.sem, at)
            g.affine_select(out=ident[:, :], in_=ident[:, :], compare_op=ALU.not_equal, fill=1.0, base=0,
                            pattern=[[-1, P]], channel_multiplier=1).then_inc(consts_made, 1)
            g.affine_select(out=identb[:, :], in_=identb[:, :], compare_op=ALU.not_equal, fill=1.0, base=0,
                            pattern=[[-1, P]], channel_multiplier=1).then_inc(consts_made, 1)
            g.affine_select(out=before[:, :], in_=before[:, :], compare_op=ALU.is_gt, fill=0.0, base=0,
                            pattern=[[1, P]], channel_multiplier=-1).then_inc(consts_made, 1)
            g.tensor_copy(iota[:, :], iota_i[:, :]).then_inc(consts_made, 1)
            g.memset(acc_raw[:, TC * P:], 0.0).then_inc(acc_zeroed, 1)
            pool.wait_ge(xn_stored, 16 * (GROUPS + 1))
            pool.wait_ge(rel_ready, 1)

            def octet(q, beside, i):
                for k in range(OCT):
                    if k % (OCT // 2) == 0:
                        pool.wait_ge(idx_staged, 2 * q + 2 * k // OCT + 1)
                    pool.wait_ge(multiplied, OCT * q + k + 1)
                    pool.sem_inc(slots_taken, 1)
                    g.indirect_dma_start(gath[:, k, :], None, xn_d,
                                         bass.IndirectOffsetOnAxis(ap=idx_st[:, k:k + 1], axis=0)).then_inc(gathered[k], 16)

            edge_schedule(pool, octet)

            pool.wait_ge(flag_ready, 1)
            far = pool.value_load(flag[0:1, 0:1], min_val=0, max_val=1)
            with pool.If(far > 0):
                pool.wait_ge(multiplied, OCT * (NOCT + 1))
                pool.wait_ge(idx_staged, 2 * (NOCT + 1))
                with pool.Fori(0, NOCT * OCT) as t:
                    pool.wait_ge(slow_step, (2 * NT + 2) * t + 1)
                    g.tensor_copy(idx_st[:, 0:1], src_i[:, ds(t, 1)]).then_inc(slow_idx, 1)
                    pool.wait_ge(slow_idx, t + 1)
                    pool.sem_inc(slots_taken, 1)
                    g.indirect_dma_start(gath[:, 0, :], None, xn_d,
                                         bass.IndirectOffsetOnAxis(ap=idx_st[:, 0:1], axis=0)).then_inc(slow_gath, 16)
                    pool.wait_ge(slow_gath, 16 * t + 16)

            for t in range(NT + 2):
                a, b = t - 1, t - 2
                if 0 <= a < NT:
                    pool.wait_ge(var_a, a + 1)
                    at = p_own.mark(g.tensor_scalar(rs_a[0:rows(a), :], mv_a[0:rows(a), 1:2], EPS, None, ALU.add))
                    pool.wait_ge(p_own.sem, at)
                    g.tensor_tensor(rs_a[0:rows(a), :], rs_a[0:rows(a), :], neg_half[0:rows(a), :], ALU.pow).then_inc(rs_a_ready, 1)
                if 0 <= b < NT:
                    pool.wait_ge(var_b, b + 1)
                    at = p_own.mark(g.tensor_scalar(rs_b[0:rows(b), :], mv_b[0:rows(b), 1:2], EPS, None, ALU.add))
                    pool.wait_ge(p_own.sem, at)
                    g.tensor_tensor(rs_b[0:rows(b), :], rs_b[0:rows(b), :], neg_half[0:rows(b), :], ALU.pow).then_inc(rs_b_ready, 1)
                if 0 <= a < NT:
                    n = rows(a)
                    pool.wait_ge(lna_done, a + 1)
                    at = p_own.mark(g.tensor_tensor(yg[0:n, a % 2, :], y[0:n, a % 2, :], gam_bc[0:n, :], ALU.mult))
                    pool.wait_ge(early_loaded[a % 4], 16 * (a // 4 + 1))
                    pool.wait_ge(p_own.sem, at)
                    g.tensor_tensor(x2[0:n, a, :], yg[0:n, a % 2, :], early_in[a % 4][0:n, D:2 * D], ALU.add).then_inc(x2_done, 1)
            pool.wait_ge(pos_ready, 1)
            pool.wait_ge(slots_cleared, 16 * CLEARS)
            for t in range(NT):
                n = rows(t)
                g.indirect_dma_start(slots_in_d, bass.IndirectOffsetOnAxis(ap=pos_i[0:n, t:t + 1], axis=0),
                                     x2n[0:n, t, :], None).then_inc(scattered, 16)
            for s in range(FT):
                pool.wait_ge(f_stored[s], 16 * SLOT_TILES // FT)
            for t in range(NT):
                n = rows(t)
                if t >= YB:
                    pool.wait_ge(y_back[t % YB], 16 * (t // YB))
                g.indirect_dma_start(yback[0:n, t, :], None, slots_out_d,
                                     bass.IndirectOffsetOnAxis(ap=pos_i[0:n, t:t + 1], axis=0)).then_inc(y_back[t % YB], 16)

        @block.scalar
        def _(act):
            s = nc.scalar
            act.dma_start(comp_diag[:, :, :], group_mask).then_inc(types_loaded, 16)
            act.dma_start(rel_of[:, :], relation_of).then_inc(types_loaded, 16)
            act.dma_start(comp_rep[:, :], comp.rearrange("(a r) b -> a r b", a=1).to_broadcast([TG, R, B])).then_inc(types_loaded, 16)
            act.dma_start(type_g, type_rows.rearrange("(g a c) e -> g a (c e)", g=TG, a=1).to_broadcast([TG, R, TC * P])).then_inc(types_loaded, 16)
            act.dma_start(dst_i[:, :], dst_t).then_inc(tables_loaded, 16)
            act.dma_start(src_i[:, :], src_t).then_inc(tables_loaded, 16)
            act.wait_ge(eps_made, 1)
            def xnt_out(w):
                n = 2 * P if w < PAIRS else P
                act.wait_ge(turned, w + 1)
                s.copy(xnt[:, :, 2 * P * w:2 * P * w + n],
                       ps_mix[w % 2][:, :].rearrange("p (k n) -> p k n", k=KD)[:, :, 0:n]).then_inc(xnt_ready, 1)

            for g in range(GROUPS):
                act.wait_ge(var_ready, g + 1)
                s.activation(rstd[:, g * GT:(g + 1) * GT], mv[:, g * GT:(g + 1) * GT, 1], ACT.Sqrt, bias=eps_col[:, :]).then_inc(std_ready, 1)
                act.wait_ge(rstd_ready, g + 1)
                for t in range(g * GT, g * GT + GA):
                    s.activation(xn[:, t, 0:D], xn[:, t, 0:D], ACT.Identity, bias=nmr[:, t:t + 1], scale=rstd[:, t:t + 1]).then_inc(ln_act, 1)
                if g > 0:
                    for w in pairs_within(g - 1):
                        xnt_out(w)
                if g == 2:
                    act.wait_ge(tables_loaded, 32)
                    s.copy(idx_st[:, :], src_i[:, 0:OCT]).then_inc(idx_staged, 2)
                if g == GROUPS - 1:
                    for n, c in enumerate(range(0, TC, CB)):
                        w = min(CB, TC - c)
                        act.wait_ge(wts_mult, n + 1)
                        s.copy(wts[:, :, :].rearrange("p b (g c) -> p c g b", g=TG)[:, c:c + w, :, :],
                               ps_edge[n][:, 0:w * TG * B].rearrange("p (c g b) -> p c g b", c=w, b=B)).then_inc(wts_ready, 1)
            for w in pairs_within(GROUPS - 1):
                xnt_out(w)
            act.wait_ge(rwt_turned, 1)
            s.copy(rwt[:, :, :], ps_sum[0][:, 0:KD * X].rearrange("p (k e) -> p k e", k=KD)).then_inc(rwt_ready, 1)

            def stage_idx(q, half):
                w = OCT // 2
                for k in range(half * w, half * w + w):
                    act.wait_ge(gathered[k], 16 * q + 16)
                s.copy(idx_st[:, half * w:half * w + w], src_i[:, ds(OCT * q + OCT + half * w, w)]).then_inc(idx_staged, 1)

            def octet(q, beside, i):
                if beside in ("sum", "sum_last"):
                    act.wait_ge(keyed, 2 * i + 1)
                    for j in range(2):
                        s.copy(xst[:, j, :, :], xnt[:, :, ds(2 * P * i + P * j, P)]).then_inc(st_copied, 1)
                if beside == "sum_first":
                    s.copy(xst[:, 0, :, :], xnt[:, :, (NT - 1) * P:NT * P]).then_inc(st_copied, 1)
                if beside == "early":
                    act.wait_ge(early_mult, 2 * i + 1)
                    for j in range(2):
                        s.copy(xst[:, j, :, :], xnt[:, :, ds(2 * P * i + P * j, P)]).then_inc(c_copied, 1)
                if beside == "early_last":
                    act.wait_ge(early_mult, 2 * PAIRS + 1)
                    s.copy(xst[:, 0, :, :], xnt[:, :, (NT - 1) * P:NT * P]).then_inc(c_copied, 1)
                if beside == "small_b":
                    act.wait_ge(m_mult, 1)
                    s.copy(cmat[:, :, D:2 * D], ps_mix[0][:, :].rearrange("p (k f) -> p k f", k=KD)).then_inc(m_copied, 1)
                def first(j):
                    if beside in ("sum", "sum_last"):
                        act.wait_ge(summed, 2 * i + 1)
                        act.wait_ge(keyed, 2 * i + j + 2)
                        s.activation(et[:, j, :], ps_mix[j][:, 0:D], ACT.Exp).then_inc(exped, 1)
                    if beside == "early":
                        act.wait_ge(early_mult, 2 * i + j + 2)
                        act.wait_ge(eout_free, 2 * i + j + 1)
                        s.copy(eout[:, j, 0:D], ps_mix[j][:, 0:D]).then_inc(pre_out, 1)

                stage_idx(q, 0)
                first(0)
                if beside == "sum_first":
                    act.wait_ge(keyed, 1)
                    s.activation(et[0:LAST, 0, :], ps_mix[0][0:LAST, 0:D], ACT.Exp).then_inc(exped, 1)
                if beside == "early_last":
                    act.wait_ge(early_mult, NT + 1)
                    act.wait_ge(eout_free, NT)
                    s.copy(eout[0:LAST, 0, 0:D], ps_mix[0][0:LAST, 0:D]).then_inc(pre_out, 1)
                if beside in ("sum", "sum_last", "early"):
                    stage_idx(q, 1)
                    first(1)
                if beside == "small_a":
                    act.wait_ge(s_turned, 2)
                    s.copy(tnt, ps_mix[0][:, :].rearrange("p (k d) -> p k d", k=KD)).then_inc(s_copied, 1)
                    s.copy(wqt, ps_mix[1][:, :].rearrange("p (m i) -> p m i", m=KD)).then_inc(s_copied, 1)
                if beside not in ("sum", "sum_last", "early"):
                    stage_idx(q, 1)
                if beside == "small_a":
                    act.wait_ge(var_ready, GROUPS + 1)
                    s.activation(rstd[:, 0:KD], mv[:, 0:KD, 1], ACT.Sqrt, bias=eps_col[:, :]).then_inc(std_ready, 1)

            act.sem_inc(pre_out, 2)
            edge_schedule(act, octet)

            for t in range(NT + 5):
                if t < NT:
                    n = rows(t)
                    act.wait_ge(u_done, t + 1)
                    if t >= 2:
                        act.wait_ge(lna_done, t - 1)
                    s.activation(h[0:n, t % 2, :], u[0:n, t % 2, :], ACT.Gelu).then_inc(gelu_done, 1)
                a = t - 3
                if 0 <= a < NT:
                    act.wait_ge(t_turned, a + 1)
                    if a >= 2:
                        act.wait_ge(logits_mult, a - 1)
                    s.copy(x2nt[:, a % 2, :, 0:rows(a)],
                           ps[2 + a % 2][:, 0:KD * P].rearrange("p (k n) -> p k n", k=KD)[:, :, 0:rows(a)]).then_inc(t_copied, 1)
                b = t - 5
                if 0 <= b < NT:
                    act.wait_ge(ranked, b + 1)
                    s.copy(rk[:, b, :], ps[6 + b % 2][:, 0:X]).then_inc(rank_out, 1)

            act.wait_ge(expert_ready, 1)
            act.wait_ge(ffn_loaded, 64)
            for f, e in enumerate(row_values(act, ex_i[0:1, 0:FT], X - 1)):
                s.copy(f_w[:, f, :], w1_flat[:, ds(e * (KD * H), KD * H)]).then_inc(f_w1, 1)
            with act.Fori(0, SLOT_TILES // FT) as i:
                for f in range(FT):
                    act.wait_ge(f_turned, FT * i + f + 1)
                    s.copy(f_xts[:, f, :], ps[f][:, 0:D]).then_inc(f_xt, 1)
                for f, e in enumerate(row_values(act, ex_i[0:1, ds(FT * i + FT, FT)], X - 1)):
                    act.wait_ge(f_hid, FT * i + f + 1)
                    s.copy(f_w[:, f, :], w1_flat[:, ds(e * (KD * H), KD * H)]).then_inc(f_w1, 1)

        @block.tensor
        def _(pe):
            t_ = nc.tensor
            pe.wait_ge(consts_made, 6)
            pe.sem_inc(multiplied, OCT)

            def turn(w):
                tiles = [2 * w, 2 * w + 1] if w < PAIRS else [NT - 1]
                pe.wait_ge(ln_done, tiles[-1] // GT + 1)
                pe.wait_ge(ln_act, (tiles[-1] // GT + 1) * GA)
                if w >= 2:
                    pe.wait_ge(xnt_ready, w - 1)
                for j, t in enumerate(tiles):
                    for k in range(KD):
                        ins = t_.transpose(ps_mix[w % 2][:, k * 2 * P + j * P:k * 2 * P + j * P + P],
                                           xn[:, t, k * P:(k + 1) * P], ident[:, :])
                ins.then_inc(turned, 1)

            for g in range(GROUPS):
                for w in pairs_within(g):
                    turn(w)
                if g == 2:
                    pe.wait_ge(hot_ready, 2)
                    for n, c0 in enumerate(range(0, TC, CB)):
                        for c in range(c0, min(c0 + CB, TC)):
                            ins = t_.matmul(ps_edge[n][:, (c - c0) * TG * B:(c - c0 + 1) * TG * B], type_hot[:, c * P:(c + 1) * P],
                                            comp_diag[:, :, :].rearrange("p g b -> p (g b)"), start=True, stop=True)
                        ins.then_inc(wts_mult, 1)
            pe.wait_ge(weights_loaded, 16 * 14)
            for k in range(KD):
                ins = t_.transpose(ps_sum[0][:, k * X:(k + 1) * X], rw[:, k * P:(k + 1) * P], ident[0:X, 0:X])
            ins.then_inc(rwt_turned, 1)
            pe.wait_ge(xnt_ready, PAIRS + 1)
            pe.wait_ge(rwt_ready, 1)
            pe.wait_ge(loopw_ready, 1)

            def edges(q, quarter):
                if quarter % 2 == 0:
                    pe.wait_ge(wmat_built, 2 * q + quarter // 2 + 1)
                pair = range(PAIR * quarter, PAIR * quarter + PAIR)
                pe.wait_ge(added, KD * (4 * q + quarter + 1))
                for m in range(KD):
                    for k in pair:
                        if m == 0:
                            pe.wait_ge(gathered[k], 16 * q + 16)
                        ins = t_.matmul(ps_edge[quarter][:, m * B * WIN:(m + 1) * B * WIN], gath[:, k, m * P:(m + 1) * P],
                                        wmat[:, k, :, :].rearrange("p b w -> p (b w)"), start=k == pair[0], stop=k == pair[-1])
                        if m == KD - 1:
                            ins.then_inc(multiplied, 1)

            def key_max(m, first, n):
                for k in range(KD):
                    ins = t_.matmul(ps_mix[m][:, 0:n], wk[:, k, m * P:(m + 1) * P],
                                    xnt[:, k, ds(first, n)], start=k == 0, stop=k == KD - 1)
                ins.then_inc(max_mult, 1)

            def keys(j, n):
                for k in range(KD):
                    t_.matmul(ps_mix[j][0:n, 0:D], xst[:, j, k, 0:n], wk[:, k, :], start=k == 0, stop=False)
                t_.matmul(ps_mix[j][0:n, 0:D], onesb[0:3, 0:n], shift3[:, :], start=False, stop=True).then_inc(keyed, 1)

            def weigh(j, tile, n, start, stop):
                for m in range(KD):
                    ins = t_.matmul(ps_sum[m][:, 0:D + 1], et[0:n, j, m * P:(m + 1) * P], tile,
                                    start=start, stop=stop)
                ins.then_inc(summed, 1)

            def early(j, n):
                for k in range(KD):
                    t_.matmul(ps_mix[j][0:n, :], xst[:, j, k, 0:n], cmat[:, k, :], start=k == 0, stop=False)
                t_.matmul(ps_mix[j][0:n, :], onesb[0:3, 0:n], bias3[:, :], start=False, stop=True).then_inc(early_mult, 1)

            def turn_for_small():
                pe.wait_ge(exped, NT)
                for m in range(KD):
                    for k in range(KD):
                        ins = t_.transpose(ps_mix[1][:, m * D + k * P:m * D + (k + 1) * P],
                                           wq[:, k, m * P:(m + 1) * P], ident[:, :])
                ins.then_inc(s_turned, 1)
                pe.wait_ge(tn_ready, 2)
                for m in range(KD):
                    for k in range(KD):
                        ins = t_.transpose(ps_mix[0][:, k * D + m * P:k * D + (m + 1) * P],
                                           tn[:, m, k * P:(k + 1) * P], ident[:, :])
                ins.then_inc(s_turned, 1)

            def lam_product():
                pe.wait_ge(s_copied, 2)
                for m in range(KD):
                    for k in range(KD):
                        ins = t_.matmul(ps_sum[0][:, m * D:(m + 1) * D], tnt[:, k, m * P:(m + 1) * P], wv[:, k, :],
                                        start=k == 0, stop=k == KD - 1)
                ins.then_inc(lam_mult, 1)

            def m_product():
                pe.wait_ge(bn_ready, 2)
                for k in range(KD):
                    for m in range(KD):
                        t_.matmul(ps_mix[0][:, k * D:(k + 1) * D], wqt[:, m, k * P:(k + 1) * P], lam[:, m, :],
                                  start=m == 0, stop=m == KD - 1)
                for k in range(KD):
                    for m in range(KD):
                        ins = t_.matmul(ps_mix[1][:, k:k + 1], lam[:, m, k * P:(k + 1) * P], qk_col[:, 0, m:m + 1],
                                        start=m == 0, stop=m == KD - 1)
                ins.then_inc(m_mult, 1)

            def to_rows(n, bank, done):
                for c in range(n):
                    ins = t_.matmul(bank[0:3, c * P:(c + 1) * P], parts[:, c, :], identb[:, :], start=True, stop=True)
                ins.then_inc(done, 1)

            def piece(quarter, beside, i):
                j = quarter // 2
                if beside == "max" and quarter in (0, 2):
                    pe.wait_ge(max_done, 2 * i + j + 1)
                    key_max(j, 2 * P * i, 2 * P)
                elif beside == "max_last" and quarter in (0, 2):
                    pe.wait_ge(max_done, 2 * PAIRS + j + 1)
                    key_max(j, (NT - 1) * P, LAST)
                elif beside == "max_last" and quarter == 3:
                    pe.wait_ge(shift_cols, 1)
                    to_rows(KD, ps_sum[0], shift_turned)
                elif beside == "sum_first" and quarter == 0:
                    pe.wait_ge(shift_ready, 1)
                    pe.wait_ge(st_copied, 1)
                    keys(0, LAST)
                elif beside == "sum_first" and quarter == 2:
                    pe.wait_ge(exped, 1)
                    weigh(0, xn[0:LAST, NT - 1, :], LAST, True, False)
                elif beside in ("sum", "sum_last") and quarter < 2:
                    pe.wait_ge(exped, 2 * i + 1)
                    pe.wait_ge(st_copied, 2 * i + quarter + 2)
                    keys(quarter, P)
                elif beside in ("sum", "sum_last"):
                    j = quarter - 2
                    pe.wait_ge(exped, 2 * i + j + 2)
                    weigh(j, xn_raw[:, ds((D + 1) * (2 * i + j), D + 1)], P, False, beside == "sum_last" and j == 1)
                elif beside == "small_a" and quarter == 1:
                    turn_for_small()
                elif beside == "small_a" and quarter == 3:
                    lam_product()
                elif beside == "small_b" and quarter == 1:
                    m_product()
                elif beside == "small_b" and quarter == 3:
                    pe.wait_ge(cols_ready, 1)
                    to_rows(4, ps_sum[1], bias_turned)
                    pe.wait_ge(bias_ready, 1)
                    pe.wait_ge(m_copied, 1)
                    pe.sem_inc(early_mult, 1)
                elif beside == "early" and quarter in (0, 2):
                    pe.wait_ge(c_copied, 2 * i + j + 1)
                    pe.wait_ge(pre_out, 2 * i + j + 1)
                    pe.wait_ge(mix_out, 2 * i + j + 1)
                    early(j, P)
                elif beside == "early_last" and quarter == 0:
                    pe.wait_ge(c_copied, NT)
                    pe.wait_ge(pre_out, NT)
                    pe.wait_ge(mix_out, NT)
                    early(0, LAST)

            def octet(q, beside, i):
                for quarter in range(4):
                    edges(q, quarter)
                    piece(quarter, beside, i)

            edge_schedule(pe, octet)

            pe.wait_ge(flag_ready, 1)
            far = pe.value_load(flag[0:1, 0:1], min_val=0, max_val=1)
            with pe.If(far > 0):
                with pe.Fori(0, NOCT * OCT) as t:
                    pe.wait_ge(slow_gath, 16 * t + 16)
                    pe.sem_inc(slow_seen, 1)
                    with pe.Fori(0, NT) as w:
                        pe.wait_ge(slow_built, NT * t + w + 1)
                        for m in range(KD):
                            ins = t_.matmul(ps_edge[m][:, :], gath[:, 0, m * P:(m + 1) * P], far_w4,
                                            start=True, stop=True)
                        ins.then_inc(slow_mult, 1)

            pe.wait_ge(acc_final, 1)
            pe.wait_ge(basis_loaded, 32)
            for t in range(NT + 6):
                if t < NT:
                    n = rows(t)
                    if t >= 2:
                        pe.wait_ge(u_done, t - 1)
                    for m in range(KD):
                        for b in range(B):
                            ins = t_.matmul(ps[t % 2][0:n, 0:D], acc[:, m * B + b, t * P:t * P + n], basis_sb[m][:, b, :],
                                            start=m == b == 0, stop=m == KD - 1 and b == B - 1)
                    ins.then_inc(z_mult, 1)
                a = t - 3
                if 0 <= a < NT:
                    n = rows(a)
                    pe.wait_ge(lnb_done, a + 1)
                    if a >= 2:
                        pe.wait_ge(t_copied, a - 1)
                    for k in range(KD):
                        ins = t_.transpose(ps[2 + a % 2][:, k * P:k * P + n], x2n[0:n, a, k * P:(k + 1) * P], ident[0:n, 0:n])
                    ins.then_inc(t_turned, 1)
                b = t - 4
                if 0 <= b < NT:
                    n = rows(b)
                    pe.wait_ge(t_copied, b + 1)
                    if b >= 2:
                        pe.wait_ge(routed, b - 1)
                    for k in range(KD):
                        t_.matmul(ps[4 + b % 2][0:n, 0:X], x2nt[:, b % 2, k, 0:n], rwt[:, k, :], start=k == 0, stop=False)
                    t_.matmul(ps[4 + b % 2][0:n, 0:X], ones_row[:, 0:n], rb_row[:, :], start=False, stop=True).then_inc(logits_mult, 1)
                c = t - 5
                if 0 <= c < NT:
                    pe.wait_ge(routed, c + 1)
                    if c >= 2:
                        pe.wait_ge(rank_out, c - 1)
                    t_.matmul(ps[6 + c % 2][:, 0:X], before[:, :], oh[:, c, :], start=True, stop=False)
                    t_.matmul(ps[6 + c % 2][:, 0:X], onesb[:, :], oh_sum[:, c, :], start=False, stop=True).then_inc(ranked, 1)
            t_.matmul(ps[0][:, 0:X], onesb[:, :], oh_sum[:, NT, :], start=True, stop=True).then_inc(counted, 1)

            pe.wait_ge(expert_ready, 1)
            pe.wait_ge(rank_out, NT)
            pe.wait_ge(ffn_loaded, 64)
            with pe.Fori(0, SLOT_TILES // FT) as i:
                for f in range(FT):
                    pe.wait_ge(f_in[f], 16 * i + 16)
                    pe.wait_ge(f_xt, FT * i + f + 1)
                    for k in range(KD):
                        ins = t_.transpose(ps[f][:, k * P:(k + 1) * P], f_x[:, f, k * P:(k + 1) * P], ident[:, :])
                    ins.then_inc(f_turned, 1)
                for f in range(FT):
                    pe.wait_ge(f_xt, FT * i + FT + f + 1)
                    pe.wait_ge(f_w1, FT * i + f + 1)
                    pe.wait_ge(f_y, FT * i + f + 1)
                    for k in range(KD):
                        ins = t_.matmul(ps[FT + f][0:H, 0:P], f_w[:, f, k * H:(k + 1) * H], f_xts[:, f, k * P:(k + 1) * P],
                                        start=k == 0, stop=k == KD - 1)
                    ins.then_inc(f_hid, 1)
                for f, e in enumerate(row_values(pe, ex_i[0:1, ds(FT * i, FT)], X - 1)):
                    pe.wait_ge(f_relu, FT * i + f + 1)
                    t_.matmul(ps[FT + f][:, 0:D], f_hts[:, f, :], w2_sb[:, ds(e * D, D)], start=True, stop=True).then_inc(f_out, 1)

        @block.vector
        def _(v):
            d = nc.vector

            def own(at):
                v.wait_ge(v_own.sem, at)

            d.memset(xn[:, NT - 1, :], 0.0).then_inc(pad_zeroed, 1)
            v.wait_ge(pad_zeroed, 1)
            v_own.mark(d.memset(xn[:, :, D:D + 1], 1.0))
            d.memset(eps_col[:, :], EPS).then_inc(eps_made, 1)
            v.wait_ge(rows_loaded, 16)
            er = ETAB // ROWG
            dr = dstr_i[0:er, :].rearrange("p (g e) -> p g e", g=WROW)
            v_own.mark(d.tensor_reduce(low[:, :], dr, AX.X, ALU.min))
            at = v_own.mark(d.tensor_reduce(high[:, :], dr, AX.X, ALU.max))
            own(at)
            d.tensor_tensor(span[:, :], high[:, :], low[:, :], ALU.subtract).then_inc(bounds_ready, 1)
            for g in range(GROUPS):
                v.wait_ge(x_loaded[g], 16 if g < GROUPS - 1 else 32)
                tiles = range(g * GT, (g + 1) * GT)
                for t in tiles:
                    at = v_own.mark(d.bn_stats(stats[:, t % GT, :], xn[:, t, 0:D]))
                own(at)
                for t in tiles:
                    at = v_own.mark(d.bn_aggr(mv[:, t, :], stats[:, t % GT, :]))
                own(at)
                v.sem_inc(var_ready, 1)
                v.wait_ge(std_ready, g + 1)
                cut = slice(tiles[0], tiles[-1] + 1)
                at = v_own.mark(d.reciprocal(rstd[:, cut], rstd[:, cut]))
                own(at)
                d.scalar_tensor_tensor(nmr[:, cut], mv[:, cut, 0], -1.0, rstd[:, cut], ALU.mult, ALU.mult).then_inc(rstd_ready, 1)
                for t in tiles[GA:]:
                    at = v_own.mark(d.tensor_scalar(xn[:, t, 0:D], xn[:, t, 0:D], mv[:, t, 0:1], rstd[:, t:t + 1], ALU.subtract, ALU.mult))
                own(at)
                v.sem_inc(ln_done, 1)
                if g == 1:
                    v.wait_ge(types_loaded, 64)
                    d.tensor_scalar(type_hot, type_g, rel_of[:, :], None, ALU.is_equal).then_inc(hot_ready, 1)
                    d.tensor_tensor(comp_diag[:, :, :], comp_diag[:, :, :], comp_rep[:, :].unsqueeze(1).to_broadcast([P, TG, B]), ALU.mult).then_inc(hot_ready, 1)
            v.wait_ge(bounds_loaded, 48)
            v.wait_ge(tables_loaded, 32)
            d.tensor_tensor(rel[:, :].rearrange("p (w j) -> p w j", j=PAIR), dst_i[:, :].rearrange("p (w j) -> p w j", j=PAIR),
                            base_bc.unsqueeze(2).to_broadcast([P, NWIN, PAIR]), ALU.subtract).then_inc(rel_ready, 1)
            v.wait_ge(consts_made, 6)
            v.wait_ge(rel_ready, 1)
            v.wait_ge(wts_ready, -(-TC // CB))

            def build_hit(q, half):
                w = OCT // 2
                n = 2 * q + half
                cut = ds(OCT * q + half * w, w) if not isinstance(q, int) else slice(OCT * q + half * w, OCT * q + half * w + w)
                v.wait_ge(wmat_built, n) if not isinstance(q, int) or n > 0 else None
                d.tensor_tensor(hit[:, :, :], rel[:, cut].unsqueeze(2).to_broadcast([P, w, WIN]),
                                iota[:, 0:WIN].unsqueeze(1).to_broadcast([P, w, WIN]), ALU.is_equal).then_inc(hit_built, 1)

            def build_weights(q, half):
                w = OCT // 2
                n = 2 * q + half
                cut = ds(OCT * q + half * w, w) if not isinstance(q, int) else slice(OCT * q + half * w, OCT * q + half * w + w)
                if not isinstance(q, int) or q > 0:
                    v.wait_ge(multiplied, OCT * q + half * w + w)
                v.wait_ge(hit_built, n + 1)
                d.tensor_tensor(wmat[:, half * w:half * w + w, :, :], hit[:, :, :].unsqueeze(2).to_broadcast([P, w, B, WIN]),
                                wts[:, :, cut].rearrange("p b t -> p t b").unsqueeze(3).to_broadcast([P, w, B, WIN]),
                                ALU.mult).then_inc(wmat_built, 1)

            for half in range(2):
                build_hit(0, half)
                build_weights(0, half)
            d.memset(acc_raw[:, 0:TC * P].bitcast(BF16), 0.0).then_inc(acc_zeroed, 1)
            for k in range(KD):
                blockk = cmat[:, k, k * P:(k + 1) * P]
                if k == 0:
                    v.wait_ge(weights_loaded, 16 * 14)
                at = v_own.mark(d.tensor_tensor(blockk, blockk, ident[:, :], ALU.add))
            own(at)
            v.sem_inc(loopw_ready, 1)
            v.wait_ge(acc_zeroed, 2)
            v.sem_inc(added, 4 * KD)
            v.sem_inc(max_done, 2)
            v.sem_inc(mix_out, 2)

            def add_edges(q, half, bases):
                for w in range(half * OCT // PAIR // 2, (half + 1) * OCT // PAIR // 2):
                    v.wait_ge(multiplied, OCT * q + PAIR * (w + 1) + OCT)
                    for m in range(KD):
                        place = acc[:, m * B:(m + 1) * B, ds(bases[w], WIN)]
                        v.wait_ge(added, KD * (OCT // PAIR * q + w + 3) + m + 1)
                        d.tensor_tensor(place, place, ps_edge[w][:, m * B * WIN:(m + 1) * B * WIN].rearrange("p (b w) -> p b w", w=WIN),
                                        ALU.add).then_inc(added, 1)
                    if w % 2 == 0:
                        build_hit(q + 1, half)
                build_weights(q + 1, half)

            def reduce_max(i, m, n):
                v.wait_ge(max_mult, 2 * i + m + 1)
                d.tensor_reduce(top[:, ds(2 * i + m, 1)], ps_mix[m][:, 0:n], AX.X, ALU.max).then_inc(max_done, 1)

            def early_out(i, j):
                v.wait_ge(early_mult, 2 * i + j + 2)
                v.wait_ge(pre_out, 2 * i + j + 3)
                v.wait_ge(xin_loaded[j], 16 * i + 16)
                v.wait_ge(eout_free, 2 * i + j + 1)
                d.tensor_tensor(eout[:, j, D:2 * D], ps_mix[j][:, D:2 * D], xin[:, j, :], ALU.add).then_inc(mix_out, 1)

            def split3(ncol, at):
                own(at)
                at = v_own.mark(d.tensor_copy(parts[:, 0:ncol, 0], cols[:, 0:ncol]))
                own(at)
                at = v_own.mark(d.tensor_tensor(rest[:, 0, 0:ncol], cols[:, 0:ncol], parts[:, 0:ncol, 0], ALU.subtract))
                own(at)
                at = v_own.mark(d.tensor_copy(parts[:, 0:ncol, 1], rest[:, 0, 0:ncol]))
                own(at)
                at = v_own.mark(d.tensor_tensor(rest[:, 1, 0:ncol], rest[:, 0, 0:ncol], parts[:, 0:ncol, 1], ALU.subtract))
                own(at)
                return d.tensor_copy(parts[:, 0:ncol, 2], rest[:, 1, 0:ncol])

            def octet(q, beside, i):
                bases = row_values(v, base_row[0:1, ds(OCT // PAIR * q, OCT // PAIR)], N - 1)
                add_edges(q, 0, bases)
                if beside == "max":
                    reduce_max(i, 0, 2 * P)
                elif beside == "max_last":
                    reduce_max(PAIRS, 0, LAST)
                elif beside == "early":
                    early_out(i, 0)
                elif beside == "early_last":
                    v.wait_ge(early_mult, NT + 1)
                    v.wait_ge(pre_out, NT + 2)
                    v.wait_ge(eout_free, NT)
                    v.wait_ge(xin_loaded[0], 16 * (PAIRS + 1))
                    d.tensor_tensor(eout[0:LAST, 0, D:2 * D], ps_mix[0][0:LAST, D:2 * D], xin[0:LAST, 0, :], ALU.add).then_inc(mix_out, 1)
                elif beside == "small_a":
                    v.wait_ge(summed, NT)
                    for m in range(KD):
                        at = v_own.mark(d.reciprocal(cols[:, m:m + 1], ps_sum[m][:, D:D + 1]))
                    own(at)
                    for m in range(KD):
                        d.tensor_scalar(tn[:, m, :], ps_sum[m][:, 0:D], cols[:, m:m + 1], None, ALU.mult).then_inc(tn_ready, 1)
                elif beside == "small_b":
                    v.wait_ge(m_mult, 1)
                    v_own.mark(d.tensor_copy(cols[:, 0:KD], hb_col[:, 0, :]))
                    at = v_own.mark(d.tensor_tensor(cols[:, KD:2 * KD], ps_mix[1][:, 0:KD], hb_col[:, 1, :], ALU.add))
                    split3(4, at).then_inc(cols_ready, 1)
                add_edges(q, 1, bases)
                if beside == "max":
                    reduce_max(i, 1, 2 * P)
                elif beside == "max_last":
                    reduce_max(PAIRS, 1, LAST)
                    v.wait_ge(max_done, 2 * PAIRS + 4)
                    at = v_own.mark(d.tensor_reduce(cols[:, 4:4 + KD], top[:, :].rearrange("p (i m) -> p m i", m=KD), AX.X, ALU.max))
                    own(at)
                    at = v_own.mark(d.tensor_tensor(cols[:, 6:6 + KD], cols[:, 4:4 + KD], qk_col[:, 1, :], ALU.add))
                    own(at)
                    at = v_own.mark(d.tensor_tensor(cols[:, 0:KD], qk_col[:, 1, :], cols[:, 6:6 + KD], ALU.subtract))
                    split3(KD, at).then_inc(shift_cols, 1)
                    v.wait_ge(shift_turned, 1)
                    d.tensor_copy(shift3[:, :], ps_sum[0][0:3, 0:D]).then_inc(shift_ready, 1)
                elif beside == "small_a":
                    v.wait_ge(lam_mult, 1)
                    for m in range(KD):
                        at = v_own.mark(d.tensor_tensor(lam[:, m, :], ps_sum[0][:, m * D:(m + 1) * D], bv_bc[:, :], ALU.add))
                    own(at)
                    for m in range(KD):
                        at = v_own.mark(d.bn_stats(stats[:, m, :], lam[:, m, :]))
                    own(at)
                    for m in range(KD):
                        at = v_own.mark(d.bn_aggr(mv[:, m, :], stats[:, m, :]))
                    own(at)
                    v.sem_inc(var_ready, 1)
                    v.wait_ge(std_ready, GROUPS + 1)
                    at = v_own.mark(d.reciprocal(rstd[:, 0:KD], rstd[:, 0:KD]))
                    own(at)
                    at = v_own.mark(d.tensor_tensor(cols[:, 0:KD], rstd[:, 0:KD], bn_col[:, 0, :], ALU.mult))
                    own(at)
                    for m in range(KD):
                        at = v_own.mark(d.tensor_scalar(lam[:, m, :], lam[:, m, :], mv[:, m, 0:1], cols[:, m:m + 1], ALU.subtract, ALU.mult))
                    own(at)
                    for m in range(KD):
                        d.tensor_scalar(lam[:, m, :], lam[:, m, :], bn_col[:, 1, m:m + 1], None, ALU.add).then_inc(bn_ready, 1)
                elif beside == "early":
                    early_out(i, 1)
                elif beside == "small_b":
                    v.wait_ge(bias_turned, 1)
                    d.tensor_copy(bias3[:, :], ps_sum[1][0:3, :]).then_inc(bias_ready, 1)

            edge_schedule(v, octet)

            at = v_own.mark(d.tensor_reduce(high[0:1, 0:1], span_row[:, :], AX.X, ALU.max))
            own(at)
            d.tensor_scalar(flag[:, :], high[0:1, 0:1], float(WIN - 1), None, ALU.is_gt).then_inc(flag_ready, 1)
            v.wait_ge(flag_ready, 1)
            v.wait_ge(added, KD * (NOCT * OCT // PAIR + 4))
            far = v.value_load(flag[0:1, 0:1], min_val=0, max_val=1)
            far_w = cols[:, 0:B]
            far_dst = cols[:, 5:6]
            sgath = hit[:, :, :].rearrange("p a w -> p (a w)")[:, 0:P]
            with v.If(far > 0):
                v.wait_ge(multiplied, OCT * (NOCT + 1))
                v.sem_inc(slow_step, 1)
                with v.Fori(0, NOCT * OCT) as t:
                    a = (2 * NT + 2) * t
                    v.wait_ge(slow_step, a + 1)
                    for b in range(B):
                        ins = d.scalar_tensor_tensor(far_w[:, b:b + 1], rel[:, ds(t, 1)], float(WIN), wts[:, b, ds(t, 1)], ALU.is_ge, ALU.mult)
                    d.tensor_copy(far_dst, dst_i[:, ds(t, 1)]).then_inc(slow_step, 1)
                    with v.Fori(0, NT) as w:
                        v.wait_ge(slow_step, a + 2 * w + 2)
                        d.tensor_scalar(sgath, iota[:, :], far_dst, None, ALU.is_equal).then_inc(slow_step, 1)
                        v.wait_ge(slow_step, a + 2 * w + 3)
                        d.tensor_tensor(far_w4.rearrange("p (b n) -> p b n", b=B),
                                        sgath.unsqueeze(1).to_broadcast([P, B, P]),
                                        far_w.unsqueeze(2).to_broadcast([P, B, P]), ALU.mult).then_inc(slow_built, 1)
                        d.tensor_scalar(far_dst, far_dst, float(-P), None, ALU.add)
                        v.wait_ge(slow_mult, NT * t + w + 1)
                        for m in range(KD):
                            place = acc[:, m * B:(m + 1) * B, ds(P * w, P)]
                            ins = d.tensor_tensor(place, place, ps_edge[m][:, :].rearrange("p (b n) -> p b n", b=B), ALU.add)
                        ins.then_inc(slow_step, 1)
                    v.wait_ge(slow_step, a + 2 * NT + 2)
                    v.sem_inc(slow_step, 1)
            v.sem_inc(acc_final, 1)

            v.wait_ge(early_mult, NT + 1)
            v_own.mark(d.memset(oh[:, NT - 1, :], 0.0))
            at = v_own.mark(d.memset(oh_sum[:, 0, :], 0.0))
            own(at)
            for t in range(NT + 5):
                if t < NT:
                    n = rows(t)
                    v.wait_ge(z_mult, t + 1)
                    v.wait_ge(early_loaded[t % 4], 16 * (t // 4 + 1))
                    if t >= 2:
                        v.wait_ge(gelu_done, t - 1)
                    d.tensor_tensor(u[0:n, t % 2, :], ps[t % 2][0:n, 0:D], early_in[t % 4][0:n, 0:D], ALU.add).then_inc(u_done, 1)
                a, b = t - 1, t - 2
                if 0 <= a < NT:
                    v.wait_ge(gelu_done, a + 1)
                    at_a = v_own.mark(d.bn_stats(stat_a[0:rows(a), :], h[0:rows(a), a % 2, :]))
                if 0 <= b < NT:
                    v.wait_ge(x2_done, b + 1)
                    at_b = v_own.mark(d.bn_stats(stat_b[0:rows(b), :], x2[0:rows(b), b, :]))
                if 0 <= a < NT:
                    own(at_a)
                    d.bn_aggr(mv_a[0:rows(a), :], stat_a[0:rows(a), :]).then_inc(var_a, 1)
                if 0 <= b < NT:
                    own(at_b)
                    d.bn_aggr(mv_b[0:rows(b), :], stat_b[0:rows(b), :]).then_inc(var_b, 1)
                c = t - 4
                if 0 <= c < NT:
                    n = rows(c)
                    v.wait_ge(logits_mult, c + 1)
                    at = v_own.mark(d.max(best[0:n, :], ps[4 + c % 2][0:n, 0:X]))
                    own(at)
                    at = v_own.mark(d.max_index(best_i[0:n, :], best[0:n, :], ps[4 + c % 2][0:n, 0:X]))
                    own(at)
                    at = v_own.mark(d.tensor_copy(best_f[0:n, :], best_i[0:n, 0:1]))
                    own(at)
                    at = v_own.mark(d.tensor_scalar(oh[0:n, c, :], iota[0:n, 0:X], best_f[0:n, :], None, ALU.is_equal))
                    own(at)
                    d.tensor_tensor(oh_sum[:, c + 1, :], oh_sum[:, c, :], oh[:, c, :], ALU.add).then_inc(routed, 1)
                    v.wait_ge(routed, c + 1)
                if 0 <= a < NT:
                    v.wait_ge(rs_a_ready, a + 1)
                    if a >= 2:
                        v.wait_ge(x2_done, a - 1)
                    d.tensor_scalar(y[0:rows(a), a % 2, :], h[0:rows(a), a % 2, :], mv_a[0:rows(a), 0:1], rs_a[0:rows(a), :],
                                    ALU.subtract, ALU.mult).then_inc(lna_done, 1)
                if 0 <= b < NT:
                    v.wait_ge(rs_b_ready, b + 1)
                    d.tensor_scalar(x2n[0:rows(b), b, :], x2[0:rows(b), b, :], mv_b[0:rows(b), 0:1], rs_b[0:rows(b), :],
                                    ALU.subtract, ALU.mult).then_inc(lnb_done, 1)

            v.wait_ge(z_mult, NT)
            v.wait_ge(counted, 1)
            at = v_own.mark(d.tensor_copy(cnt, ps[0][:, 0:X]))
            at = v_own.mark(d.tensor_scalar(wm_flat[:, 0:SLOT_TILES], iota[:, 0:SLOT_TILES], float(P), None, ALU.mult))
            own(at)
            at = v_own.mark(d.tensor_tensor(over, cnt.unsqueeze(2).to_broadcast([P, X, NT]),
                                            wm_flat[:, 0:NT].unsqueeze(1).to_broadcast([P, X, NT]), ALU.is_gt))
            own(at)
            at = v_own.mark(d.tensor_reduce(n_tiles, over, AX.X, ALU.add))
            own(at)
            at = v_own.mark(d.tensor_tensor_scan(tile_end, onesb[:, 0:X], n_tiles, 0.0, ALU.mult, ALU.add))
            own(at)
            at = v_own.mark(d.tensor_tensor(slot_base, tile_end, n_tiles, ALU.subtract))
            own(at)
            at = v_own.mark(d.tensor_scalar(slot_base, slot_base, float(P), None, ALU.mult))
            own(at)
            v.wait_ge(rank_out, NT)
            at = v_own.mark(d.tensor_tensor(rk, rk, slot_base.unsqueeze(1).to_broadcast([P, NT, X]), ALU.add))
            own(at)
            at = v_own.mark(d.tensor_tensor(rank_pick, rk, oh[:, :, :], ALU.mult))
            own(at)
            at = v_own.mark(d.tensor_reduce(pos_f, rank_pick, AX.X, ALU.add))
            own(at)
            d.tensor_copy(pos_i[:, :], pos_f).then_inc(pos_ready, 1)
            at = v_own.mark(d.tensor_tensor(ended, tile_end.unsqueeze(1).to_broadcast([P, SLOT_TILES, X]),
                                            iota[:, 0:SLOT_TILES].unsqueeze(2).to_broadcast([P, SLOT_TILES, X]), ALU.is_le))
            own(at)
            at = v_own.mark(d.tensor_reduce(ex_f, ended, AX.X, ALU.add))
            own(at)
            at = v_own.mark(d.tensor_scalar(ex_f, ex_f, float(X - 1), None, ALU.min))
            own(at)
            at = v_own.mark(d.tensor_copy(ex_i[:, 0:SLOT_TILES], ex_f))
            at = v_own.mark(d.memset(ex_i[:, SLOT_TILES:SLOT_TILES + FT], 0))
            at = v_own.mark(d.memset(f_hts[H:H + 1, :, :], 1.0))
            own(at)
            v.sem_inc(expert_ready, 1)
            v.sem_inc(f_y, FT)
            v.sem_inc(f_xt, FT)

            def relus(i, first=False):
                for f, e in enumerate(row_values(v, ex_i[0:1, ds(FT * i, FT)], X - 1)):
                    v.wait_ge(f_hid, FT * i + f + 1)
                    d.tensor_scalar(f_hts[0:H, f, :], ps[FT + f][0:H, 0:P], b1_sb[:, ds(e, 1)], 0.0, ALU.add, ALU.max).then_inc(f_relu, 1)
                for f in range(FT):
                    v.wait_ge(f_out, FT * i + f + 1)
                    if not first:
                        v.wait_ge(f_stored[f], 16 * i)
                    d.tensor_scalar(f_ys[f], ps[FT + f][:, 0:D], 0.0, None, ALU.max).then_inc(f_y, 1)

            relus(0, first=True)
            with v.Fori(1, SLOT_TILES // FT) as i:
                relus(i)
            for t in range(NT):
                n = rows(t)
                v.wait_ge(y_back[t % YB], 16 * (t // YB) + 16)
                d.tensor_tensor(x2[0:n, t, :], x2[0:n, t, :], yback[0:n, t, :], ALU.add).then_inc(out_ready, 1)


_INS = ["x", "src_t", "type_rows", "dst_t", "dst_rows", "L0_gnn_basis", "L0_gnn_comp", "L0_gnn_loop_w", "L0_gnn_h_bias",
        "L0_gnn_ln_gamma", "L0_gnn_ln_beta", "L0_mix_W_qk", "L0_mix_b_qk", "L0_mix_W_v", "L0_mix_b_v", "L0_mix_gamma",
        "L0_mix_beta", "L0_ffn_router_w", "L0_ffn_router_b", "L0_ffn_W1", "b1_t", "L0_ffn_W2", "L0_ffn_b2",
        "relation_of", "group_mask"]


def lay_out(inputs):
    import numpy as np

    arrays = {k: np.ascontiguousarray(v) for k, v in inputs.items()}
    pad = ETAB * P - E
    src = np.pad(arrays.pop("src"), (0, pad)).reshape(ETAB, P)
    types = np.pad(arrays.pop("edge_type_8"), (0, pad), constant_values=R).reshape(ETAB, P)
    dst = np.pad(arrays.pop("dst"), (0, pad), mode="edge").reshape(ETAB, P)
    arrays["b1_t"] = np.ascontiguousarray(arrays.pop("L0_ffn_b1").T)
    arrays["src_t"] = np.ascontiguousarray(src.T)
    arrays["type_rows"] = np.ascontiguousarray(types)
    arrays["dst_t"] = np.ascontiguousarray(dst.T)
    arrays["dst_rows"] = np.ascontiguousarray(dst)
    arrays["relation_of"] = (np.arange(P, dtype=np.float32) % R).reshape(P, 1)
    arrays["group_mask"] = np.repeat(np.repeat(np.eye(TG, dtype=np.float32), R, 0)[:, :, None], B, 2)
    return arrays


def kernel(**inputs):
    import numpy as np
    import concourse.bacc as bacc
    from concourse.bass_utils import run_bass_kernel_spmd

    laid = lay_out(inputs)
    nc = bacc.Bacc("TRN2", target_bir_lowering=False, num_devices=1)
    arrays, args = {}, []
    for name in _INS:
        a = laid[name]
        arrays[f"in_{name}"] = a
        args.append(nc.dram_tensor(f"in_{name}", a.shape, mybir.dt.from_np(a.dtype), kind="ExternalInput").ap())
    args.append(nc.dram_tensor("out_0", (N, D), F32, kind="ExternalOutput").ap())
    gps_layer(nc, *args)
    r = run_bass_kernel_spmd(nc, [arrays], core_ids=[0])
    return r.results[0]["out_0"]
```

```python
from contextlib import ExitStack

import concourse.bass as bass
from concourse import mybir
from concourse.bass import ds

P = 128
N, D, E = 3125, 256, 50000
R, B, X, H = 8, 4, 32, 64
KD = D // P
NT = -(-N // P)
LAST = N - (NT - 1) * P
NPAD = NT * P
WIN = 36
PAIR = 2
OCT = 8
NOCT = -(-E // (P * OCT))
ETAB = (NOCT + 1) * OCT
ROWG = 4
WROW = ROWG // PAIR
NWIN = ETAB // PAIR
TG = P // R
TC = ETAB // TG
CB = 512 // (TG * B)
PAIRS = (NT - 1) // 2
MAXO = PAIRS // 2
NZ = NOCT - (MAXO + 2 * PAIRS + 6)
LATE = NT - NZ
SLOT_TILES = X + (N - X) // P
GROUPS, GT = 5, NT // 5
GA = 3
EPS = 1e-5
FT = 4
FG = 2
ROW = 2 * D + 1
POS_PARTS = (slice(0, 5), slice(5, NT))
ROUND = float(1 << 23)
NOWHERE = 1 << 20
assert OCT == 4 * PAIR and ETAB % ROWG == 0 and NT % GROUPS == 0 and PAIRS % 2 == 0 and 2 * LATE <= NT
assert SLOT_TILES % (FG * FT) == 0 and SLOT_TILES // FG <= 2 * NZ + 2

ALU = mybir.AluOpType
ACT = mybir.ActivationFunctionType
AX = mybir.AxisListType
F32, BF16 = mybir.dt.float32, mybir.dt.bfloat16
I32, U32 = mybir.dt.int32, mybir.dt.uint32


def rows(t):
    return P if t < NT - 1 else LAST


def pairs_within(g):
    return [w for w in range(PAIRS + 1) if min(2 * w + 1, NT - 1) // GT == g]


def within(n):
    return max(0, min(n, NT))


class Tally:

    def __init__(self, sem, at=0):
        self.sem, self.at = sem, at

    def mark(self, instruction, by=1):
        instruction.then_inc(self.sem, by)
        self.at += by
        return self.at


def gps_layer(nc, x, src_t, type_rows, dst_t, dst_rows, basis, comp, loop_w, h_bias, ln_gamma, ln_beta,
              w_qk, b_qk, w_v, b_v, bn_gamma, bn_beta, router_w, router_b, w1, b1_t, w2, b2, relation_of,
              group_mask, out):
    with ExitStack() as ctx:
        def sb(name, shape, dt=F32):
            return ctx.enter_context(nc.sbuf_tensor(name, shape, dt))

        def sem(name):
            return ctx.enter_context(nc.semaphore(name))

        xn_d = nc.dram_tensor("xn_d", [N, D], F32).ap()
        bounds_d = nc.dram_tensor("bounds_d", [2, NWIN], I32).ap()
        early_d = nc.dram_tensor("early_d", [NT, P, 2 * D], F32).ap()
        slots_d = nc.dram_tensor("slots_d", [SLOT_TILES * P, ROW], F32).ap()

        acc_raw = sb("acc_raw", [P, KD * B * NPAD])
        acc = acc_raw[:, :].rearrange("p (c n) -> p c n", n=NPAD)
        both = sb("both", [P, NT * ROW])
        xn_raw = both[:, 0:NT * (D + 1)]
        xn = xn_raw.rearrange("p (t f) -> p t f", f=D + 1)
        xnt = both[:, NT * (D + 1):NT * ROW].rearrange("p (k n) -> p k n", n=NPAD)
        token = both[:, :].rearrange("p (t f) -> p t f", f=ROW)
        x2n, x2 = token[:, :, 0:D], token[:, :, D:2 * D]
        gath = sb("gath", [P, OCT, D])
        wmat = sb("wmat", [P, OCT, B, WIN])
        hit = sb("hit", [P, OCT // 2, WIN])
        rel = sb("rel", [P, ETAB])
        wts = sb("wts", [P, B, ETAB])
        src_i = sb("src_i", [P, ETAB], I32)
        dst_i = sb("dst_i", [P, ETAB], I32)
        idx_st = sb("idx_st", [P, OCT], I32)
        base_row = sb("base_row", [1, NWIN], I32)
        comp_rep = sb("comp_rep", [P, B])
        comp_diag = sb("comp_diag", [P, TG, B])
        comp3 = sb("comp3", [P, 3, TG * B], BF16)
        rel_of = sb("rel_of", [P, 1])
        gath_flat = gath[:, :, :].rearrange("p a f -> p (a f)")
        base_bc = gath_flat[:, OCT * D - NWIN:OCT * D].bitcast(I32)
        type_g = acc_raw[:, 0:TC * P].bitcast(I32)
        type_hot = gath_flat[:, 0:TC * P // 2].bitcast(BF16)
        dstr_i = gath_flat[:, 3 * ETAB:3 * ETAB + ROWG * P].bitcast(I32)
        wk_et = sb("wk_et", [P, 2 * KD * D])
        wk = wk_et[:, 0:KD * D].rearrange("p (k f) -> p k f", k=KD)
        et = wk_et[:, KD * D:2 * KD * D].rearrange("p (j f) -> p j f", j=2)
        wq = sb("wq", [P, KD, D])
        wv = sb("wv", [P, KD, D])
        cmat = sb("cmat", [P, KD, 2 * D])
        xst = sb("xst", [P, 2, KD, P])
        xin = sb("xin", [P, 2, D])
        eout = sb("eout", [P, 2, 2 * D])
        ident = sb("ident", [P, P])
        identb = sb("identb", [P, P], BF16)
        before = sb("before", [P, P], BF16)
        onesb = sb("onesb", [P, P], BF16)
        ones_row = sb("ones_row", [1, P])
        iota_i = wmat[:, 0, :, :].rearrange("p b w -> p (b w)")[:, 0:P].bitcast(I32)
        iota = sb("iota", [P, P])
        empty = sb("empty", [P, ROW])
        eps_col = sb("eps_col", [P, 1])
        neg_half = sb("neg_half", [P, 1])
        stats = sb("stats", [P, GT, 6])
        mv = sb("mv", [P, NT, 2])
        rstd = sb("rstd", [P, NT])
        nmr = sb("nmr", [P, NT])
        low = sb("low", [ETAB // ROWG, WROW], I32)
        high = sb("high", [ETAB // ROWG, WROW], I32)
        span = sb("span", [ETAB // ROWG, WROW], I32)
        span_row = sb("span_row", [1, NWIN], I32)
        flag = sb("flag", [1, 2], I32)
        reach = sb("reach", [1, NZ * OCT // PAIR], I32)
        late = sb("late", [1, 2], I32)
        top = sb("top", [P, (PAIRS + 1) * KD])
        cols = sb("cols", [P, 8])
        qk_col = sb("qk_col", [P, 2, KD])
        bn_col = sb("bn_col", [P, 2, KD])
        hb_col = sb("hb_col", [P, 2, KD])
        parts = sb("parts", [P, 4, 3], BF16)
        rest = sb("rest", [P, 2, 4])
        shift3 = sb("shift3", [3, D], BF16)
        bias3 = sb("bias3", [3, 2 * D], BF16)
        bv_bc = sb("bv_bc", [P, D])
        gam_bc = sb("gam_bc", [P, D])
        rw = sb("rw", [X, D])
        rwt = sb("rwt", [P, KD, X])
        rb_row = sb("rb_row", [1, X])
        tn = eout[:, 0, :].rearrange("p (m f) -> p m f", m=KD)
        tnt = eout[:, 1, :].rearrange("p (k d) -> p k d", k=KD)
        lam = xst[:, :, :, :].rearrange("p j k n -> p (j k n)").rearrange("p (m e) -> p m e", m=KD)
        wqt = xin[:, :, :]

        ps = [ctx.enter_context(nc.psum_tensor(f"ps{i}", [P, 512], F32)) for i in range(8)]
        ps_edge = ps[0:4]
        ps_mix = ps[4:6]
        ps_sum = ps[6:8]

        rows_loaded = sem("rows_loaded")
        x_loaded = [sem(f"x_loaded{g}") for g in range(GROUPS)]
        pad_zeroed = sem("pad_zeroed")
        tables_loaded = sem("tables_loaded")
        weights_loaded = sem("weights_loaded")
        bounds_ready = sem("bounds_ready")
        bounds_stored = sem("bounds_stored")
        bounds_loaded = sem("bounds_loaded")
        rel_ready = sem("rel_ready")
        ln_done = sem("ln_done")
        ln_act = sem("ln_act")
        rstd_ready = sem("rstd_ready")
        xn_stored = sem("xn_stored")
        eps_made = sem("eps_made")
        var_ready = sem("var_ready")
        std_ready = sem("std_ready")
        var_ab = sem("var_ab")
        rs_ready = sem("rs_ready")
        consts_made = sem("consts_made")
        turned = sem("turned")
        xnt_ready = sem("xnt_ready")
        types_loaded = sem("types_loaded")
        hot_ready = sem("hot_ready")
        wts_mult = sem("wts_mult")
        wts_ready = sem("wts_ready")
        v_own = Tally(sem("v_own"))
        p_own = Tally(sem("p_own"))
        empty_made = sem("empty_made")
        numbered = sem("numbered")
        slots_cleared = sem("slots_cleared")
        rwt_turned = sem("rwt_turned")
        rwt_ready = sem("rwt_ready")
        loopw_ready = sem("loopw_ready")
        gathered = [sem(f"gathered{k}") for k in range(OCT)]
        slots_taken = sem("slots_taken")
        idx_staged = sem("idx_staged")
        multiplied = sem("multiplied")
        hit_built = sem("hit_built")
        wmat_built = sem("wmat_built")
        added = sem("added")
        acc_zeroed = sem("acc_zeroed")
        flag_ready = sem("flag_ready")
        max_mult = sem("max_mult")
        max_done = sem("max_done")
        shift_cols = sem("shift_cols")
        shift_turned = sem("shift_turned")
        shift_ready = sem("shift_ready")
        st_copied = sem("st_copied")
        keyed = sem("keyed")
        exped = sem("exped")
        summed = sem("summed")
        tn_ready = sem("tn_ready")
        s_turned = sem("s_turned")
        s_copied = sem("s_copied")
        lam_mult = sem("lam_mult")
        bn_ready = sem("bn_ready")
        m_mult = sem("m_mult")
        m_copied = sem("m_copied")
        cols_ready = sem("cols_ready")
        bias_turned = sem("bias_turned")
        bias_ready = sem("bias_ready")
        c_copied = sem("c_copied")
        early_mult = sem("early_mult")
        pre_out = sem("pre_out")
        mix_out = sem("mix_out")
        xin_loaded = [sem(f"xin_loaded{j}") for j in range(2)]
        early_stored = [sem(f"early_stored{j}") for j in range(2)]
        eout_free = sem("eout_free")
        slow_idx = sem("slow_idx")
        slow_gath = sem("slow_gath")
        slow_built = sem("slow_built")
        slow_seen = sem("slow_seen")
        slow_mult = sem("slow_mult")
        slow_step = sem("slow_step")
        acc_final = sem("acc_final")
        basis_loaded = [sem(f"basis_loaded{m}") for m in range(KD)]
        early_loaded = [sem(f"early_loaded{j}") for j in range(5)]
        z_staged = sem("z_staged")
        z_part = sem("z_part")
        z_out = sem("z_out")
        z_redone = sem("z_redone")
        z_mult = sem("z_mult")
        z_ready = sem("z_ready")
        u_done = sem("u_done")
        gelu_done = sem("gelu_done")
        lna_done = sem("lna_done")
        x2_done = sem("x2_done")
        lnb_done = sem("lnb_done")
        t_turned = sem("t_turned")
        t_copied = sem("t_copied")
        logits_mult = sem("logits_mult")
        routed = sem("routed")
        ranked = sem("ranked")
        rank_out = sem("rank_out")
        counted = sem("counted")
        pos_ready = sem("pos_ready")
        expert_ready = sem("expert_ready")
        scattered = sem("scattered")
        ffn_loaded = sem("ffn_loaded")
        f_in = [sem(f"f_in{s}") for s in range(FG * FT)]
        f_turned = sem("f_turned")
        f_xt = sem("f_xt")
        f_hid = sem("f_hid")
        f_relu = sem("f_relu")
        f_out = sem("f_out")
        f_y = sem("f_y")
        f_numbers = sem("f_numbers")
        f_w1 = sem("f_w1")
        f_stored = [sem(f"f_stored{s}") for s in range(FG * FT)]

        wm_flat = wmat[:, :, :, :].rearrange("p a b w -> p (a b w)")
        basis_sb = [wk_et[:, :].rearrange("p (b f) -> p b f", b=B), cmat[:, :, :].rearrange("p k (c f) -> p (k c) f", f=D)]
        early_in = [eout[:, 0, :], eout[:, 1, :],
                    xst[:, :, :, :].rearrange("p j k n -> p (j k n)"), xin[:, :, :].rearrange("p j f -> p (j f)"),
                    gath_flat[:, 3 * D:5 * D]]
        EI = len(early_in)
        far_w4 = wm_flat[:, 0:B * P]
        u = wq[:, :, :]
        h = wv[:, :, :]
        zst = [wq[:, :, :].rearrange("p k f -> p (k f)").rearrange("p (b n) -> p b n", b=B),
               wv[:, :, :].rearrange("p k f -> p (k f)").rearrange("p (b n) -> p b n", b=B)]
        y = wm_flat[:, 0:2 * D].rearrange("p (j f) -> p j f", j=2)
        yg = wm_flat[:, 2 * D:4 * D].rearrange("p (j f) -> p j f", j=2)
        x2nt = gath[:, 0:2, :].rearrange("p j (k n) -> p j k n", k=KD)
        stat_a = gath[:, 2, 0:6]
        stat_b = gath[:, 2, 8:14]
        mv_ab = gath[:, 2, 16:24].rearrange("p (j l c) -> p j l c", j=2, l=2)
        rs_ab = gath[:, 2, 24:28].rearrange("p (j l) -> p j l", j=2)
        best = gath[:, 2, 48:56]
        best_i = gath[:, 2, 64:72].bitcast(U32)
        best_f = gath[:, 2, 80:81]
        wts_flat = wts[:, :, :].rearrange("p b t -> p (b t)")
        oh = gath_flat[:, 1600:1600 + NT * X // 2].bitcast(BF16).rearrange("p (t e) -> p t e", e=X)
        oh_sum = wts_flat[:, 800:800 + (NT + 1) * X // 2].bitcast(BF16).rearrange("p (t e) -> p t e", e=X)
        rk = wts_flat[:, 0:NT * X].rearrange("p (t e) -> p t e", e=X)
        rank_pick = gath_flat[:, 3 * D:3 * D + NT * X].rearrange("p (t e) -> p t e", e=X)
        cnt = rel[:, 0:X]
        n_tiles = rel[:, X:2 * X]
        tile_end = rel[:, 2 * X:3 * X]
        slot_base = rel[:, 3 * X:4 * X]
        ended = acc_raw[:, 23000:23000 + SLOT_TILES * X].rearrange("p (j e) -> p j e", e=X)
        pos_f = rel[:, 5 * X:5 * X + NT]
        ex_f = rel[:, 6 * X:6 * X + SLOT_TILES]
        pos_i = sb("pos_i", [P, NT], I32)
        ex_i = sb("ex_i", [P, SLOT_TILES + FT], I32)
        at = 0
        w1_sb = acc_raw[:, at:at + X * KD * H].rearrange("p (e k h) -> p e k h", k=KD, h=H)
        at += X * KD * H
        w2_sb = acc_raw[0:H + 1, at:at + X * D]
        at += X * D
        b1_sb = acc_raw[0:H, at:at + X]
        at += X
        f_x = acc_raw[:, at:at + FG * FT * ROW].rearrange("p (s f) -> p s f", f=ROW)
        at += FG * FT * ROW
        f_ys = acc_raw[:, at:at + FG * FT * D].rearrange("p (s f) -> p s f", f=D)
        f_xts = gath[:, FT:2 * FT, :]
        f_id = gath_flat[:, 0:FG * FT].bitcast(I32)
        w1_flat = w1_sb.rearrange("p e k h -> p (e k h)")
        f_w = wm_flat[:, 0:FT * KD * H].rearrange("p (s h) -> p s h", s=FT)
        f_hts = wm_flat[0:H + 1, FT * KD * H:FT * KD * H + FT * P].rearrange("p (s n) -> p s n", n=P)

        block = ctx.enter_context(nc.Block())

        def edge_schedule(eng, octet):
            with eng.Fori(0, MAXO) as i:
                octet(i, "max", i)
            q = MAXO
            octet(q, "max_last", None)
            octet(q + 1, "sum_first", None)
            q += 2
            with eng.Fori(0, PAIRS - 1) as i:
                octet(i + q, "sum", i)
            q += PAIRS - 1
            octet(q, "sum_last", PAIRS - 1)
            octet(q + 1, "small_a", None)
            octet(q + 2, "small_b", None)
            octet(q + 3, "small_c", None)
            q += 4
            with eng.Fori(0, PAIRS) as i:
                octet(i + q, "early", i)
            q += PAIRS
            octet(q, "early_last", None)
            q += 1
            with eng.Fori(0, NZ) as i:
                octet(i + q, "product", i)
            assert q + NZ == NOCT

        def row_values(eng, row, greatest):
            return nc.values_load_multi_w_load_instructions(row, engines=(eng.engine,), min_val=0, max_val=greatest)[1]

        @block.sync
        def _(sp):
            sp.dma_start(dstr_i[0:ETAB // ROWG, :], dst_rows.rearrange("(r g) e -> r (g e)", g=ROWG)).then_inc(rows_loaded, 16)
            for g in range(GROUPS):
                full = GT if g < GROUPS - 1 else GT - 1
                a = g * GT * P
                if g == GROUPS - 1:
                    sp.wait_ge(pad_zeroed, 1)
                    sp.dma_start(xn[0:LAST, NT - 1, 0:D], x[(NT - 1) * P:N, :]).then_inc(x_loaded[g], 16)
                sp.dma_start(xn[:, g * GT:g * GT + full, 0:D],
                             x[a:a + full * P, :].rearrange("(t p) f -> p t f", p=P)).then_inc(x_loaded[g], 16)
            sp.wait_ge(bounds_ready, 1)
            sp.dma_start(bounds_d[0, :].rearrange("(r g) -> r g", g=WROW), low[:, :]).then_inc(bounds_stored, 16)
            sp.dma_start(bounds_d[1, :].rearrange("(r g) -> r g", g=WROW), span[:, :]).then_inc(bounds_stored, 16)
            sp.wait_ge(bounds_stored, 32)
            sp.dma_start(base_bc, bounds_d[0:1, :].to_broadcast([P, NWIN])).then_inc(bounds_loaded, 16)
            sp.dma_start(base_row[:, :], bounds_d[0:1, :]).then_inc(bounds_loaded, 16)
            sp.dma_start(span_row[:, :], bounds_d[1:2, :]).then_inc(bounds_loaded, 16)
            for g in range(GROUPS):
                full = GT if g < GROUPS - 1 else GT - 1
                a = g * GT * P
                sp.wait_ge(ln_done, g + 1)
                sp.wait_ge(ln_act, (g + 1) * GA)
                sp.dma_start(xn_d[a:a + full * P, :].rearrange("(t p) f -> p t f", p=P),
                             xn[:, g * GT:g * GT + full, 0:D]).then_inc(xn_stored, 16)
            sp.dma_start(xn_d[(NT - 1) * P:N, :], xn[0:LAST, NT - 1, 0:D]).then_inc(xn_stored, 16)
            for dst, frm in ((wk[:, :, :], w_qk[1].rearrange("(k p) f -> p k f", p=P)),
                             (cmat[:, :, 0:D], loop_w.rearrange("(k p) f -> p k f", p=P)),
                             (wq[:, :, :], w_qk[0].rearrange("(k p) f -> p k f", p=P)),
                             (wv[:, :, :], w_v.rearrange("(k p) f -> p k f", p=P)),
                             (rw[:, :], router_w),
                             (rb_row[:, :], router_b.rearrange("(a e) -> a e", a=1)),
                             (bv_bc[:, :], b_v.rearrange("(a f) -> a f", a=1).to_broadcast([P, D])),
                             (gam_bc[:, :], ln_gamma.rearrange("(a f) -> a f", a=1).to_broadcast([P, D]))):
                sp.dma_start(dst, frm).then_inc(weights_loaded, 16)
            with nc.allow_non_contiguous_dma(reason="a few short bias vectors as columns"):
                for dst, frm in ((qk_col[:, 0, :], b_qk[0]), (qk_col[:, 1, :], b_qk[1]), (bn_col[:, 0, :], bn_gamma),
                                 (bn_col[:, 1, :], bn_beta), (hb_col[:, 0, :], h_bias), (hb_col[:, 1, :], ln_beta)):
                    sp.dma_start(dst, frm.rearrange("(k p) -> p k", p=P)).then_inc(weights_loaded, 16)
            sp.wait_ge(s_copied, 1)
            sp.wait_ge(m_mult, 1)
            sp.sem_inc(eout_free, 2)

            def load_basis(m):
                sp.dma_start(basis_sb[m], basis[:, m * P:(m + 1) * P, :].rearrange("b p f -> p b f")).then_inc(basis_loaded[m], 16)

            sp.wait_ge(keyed, NT)
            sp.wait_ge(summed, NT)
            load_basis(0)
            def early_tiles(i, last=False):
                for j in range(2):
                    sp.wait_ge(pre_out, 2 * i + j + 3)
                    sp.wait_ge(mix_out, 2 * i + j + 3)
                    here = early_d[ds(2 * i + j, 1), :, :].rearrange("a p f -> (a p) f") if not last else early_d[2 * i + j, :, :]
                    sp.dma_start(here, eout[:, j, :]).then_inc(early_stored[j], 16)
                    if not last:
                        sp.dma_start(xin[:, j, :], x[ds(2 * P * i + P * (j + 2), P), :]).then_inc(xin_loaded[j], 16)
                    elif j == 0:
                        sp.dma_start(xin[0:LAST, 0, :], x[(NT - 1) * P:N, :]).then_inc(xin_loaded[0], 16)
                for j in range(2):
                    sp.wait_ge(early_stored[j], 16 * i + 16)
                    sp.sem_inc(eout_free, 1)

            for j in range(2):
                sp.wait_ge(mix_out, j + 1)
                sp.dma_start(xin[:, j, :], x[P * j:P * (j + 1), :]).then_inc(xin_loaded[j], 16)
            with sp.Fori(0, PAIRS - 1) as i:
                early_tiles(i)
            early_tiles(PAIRS - 1, last=True)
            t = NT - 1
            sp.wait_ge(early_mult, NT + 1)
            load_basis(1)
            sp.wait_ge(pre_out, t + 3)
            sp.wait_ge(mix_out, t + 3)
            sp.dma_start(early_d[t, 0:LAST, :], eout[0:LAST, 0, :]).then_inc(early_stored[0], 16)

            sp.wait_ge(empty_made, 2)
            sp.wait_ge(early_stored[0], 16 * (PAIRS + 1))
            sp.wait_ge(early_stored[1], 16 * PAIRS)
            sp.wait_ge(early_mult, NT + 1)
            for t in range(NT):
                if t == 4:
                    with sp.Fori(0, SLOT_TILES // FG) as i:
                        sp.wait_ge(z_part, i + 1)
                        sp.dma_start(slots_d[ds(i * FG * P, FG * P), :].rearrange("(a p) f -> p a f", p=P),
                                     empty[:, :].unsqueeze(1).to_broadcast([P, FG, ROW])).then_inc(slots_cleared, 16)
                    sp.wait_ge(multiplied, OCT * (NOCT + 1))
                if t >= EI:
                    sp.wait_ge(x2_done, t - EI + 1)
                sp.dma_start(early_in[t % EI][0:rows(t), :], early_d[t, 0:rows(t), :]).then_inc(early_loaded[t % EI], 16)
            sp.wait_ge(z_mult, LATE)
            sp.dma_start(w1_sb, w1.rearrange("e (k p) h -> p e k h", p=P)).then_inc(ffn_loaded, 16)
            sp.dma_start(w2_sb[0:H, :].rearrange("p (e f) -> p e f", f=D), w2.rearrange("e h f -> h e f")).then_inc(ffn_loaded, 16)
            sp.dma_start(w2_sb[H:H + 1, :].rearrange("p (e f) -> p e f", f=D), b2.rearrange("(a e) f -> a e f", a=1)).then_inc(ffn_loaded, 16)
            sp.dma_start(b1_sb, b1_t).then_inc(ffn_loaded, 16)

            sp.wait_ge(scattered, 16 * NT)
            for s in range(FG * FT):
                sp.dma_start(f_x[:, s, :], slots_d[s * P:(s + 1) * P, :]).then_inc(f_in[s], 16)
            with sp.Fori(0, SLOT_TILES // (FG * FT) - 1) as i:
                for s in range(FG * FT):
                    sp.wait_ge(f_y, FG * FT * i + s + FT + 1)
                    sp.dma_start(f_x[:, s, :], slots_d[ds((FG * FT * i + FG * FT + s) * P, P), :]).then_inc(f_in[s], 16)
            for s in range(FG * FT):
                sp.wait_ge(f_stored[s], 16 * SLOT_TILES // (FG * FT))

        @block.gpsimd
        def _(pool):
            g = nc.gpsimd
            p_own.mark(g.memset(ident[:, :], 0.0))
            p_own.mark(g.memset(identb[:, :], 0.0))
            p_own.mark(g.memset(before[:, :], 1.0))
            p_own.mark(g.memset(neg_half[:, :], -0.5))
            g.memset(onesb[:, :], 1.0).then_inc(consts_made, 1)
            g.memset(ones_row[:, :], 1.0).then_inc(consts_made, 1)
            g.memset(empty[:, 0:2 * D], 0.0).then_inc(empty_made, 1)
            g.memset(empty[:, 2 * D:ROW].bitcast(I32), NOWHERE).then_inc(empty_made, 1)
            at = p_own.mark(g.iota(iota_i[:, :], pattern=[[1, P]], base=0, channel_multiplier=0))
            g.iota(reach[:, :], pattern=[[P, NZ], [0, OCT // PAIR]], base=P, channel_multiplier=0).then_inc(consts_made, 1)
            pool.wait_ge(p_own.sem, at)
            g.affine_select(out=ident[:, :], in_=ident[:, :], compare_op=ALU.not_equal, fill=1.0, base=0,
                            pattern=[[-1, P]], channel_multiplier=1).then_inc(consts_made, 1)
            g.affine_select(out=identb[:, :], in_=identb[:, :], compare_op=ALU.not_equal, fill=1.0, base=0,
                            pattern=[[-1, P]], channel_multiplier=1).then_inc(consts_made, 1)
            g.affine_select(out=before[:, :], in_=before[:, :], compare_op=ALU.is_gt, fill=0.0, base=0,
                            pattern=[[1, P]], channel_multiplier=-1).then_inc(consts_made, 1)
            g.tensor_copy(iota[:, :], iota_i[:, :]).then_inc(consts_made, 1)
            g.memset(acc_raw[:, TC * P:], 0.0).then_inc(acc_zeroed, 1)
            pool.wait_ge(xn_stored, 16 * (GROUPS + 1))
            pool.wait_ge(rel_ready, 1)

            def octet(q, beside, i):
                for k in range(OCT):
                    if k % (OCT // 2) == 0:
                        pool.wait_ge(idx_staged, 2 * q + 2 * k // OCT + 1)
                    pool.wait_ge(multiplied, OCT * q + k + 1)
                    pool.sem_inc(slots_taken, 1)
                    g.indirect_dma_start(gath[:, k, :], None, xn_d,
                                         bass.IndirectOffsetOnAxis(ap=idx_st[:, k:k + 1], axis=0)).then_inc(gathered[k], 16)

            edge_schedule(pool, octet)

            pool.wait_ge(flag_ready, 2)
            far = pool.value_load(flag[0:1, 0:1], min_val=0, max_val=1)
            with pool.If(far > 0):
                pool.wait_ge(multiplied, OCT * (NOCT + 1))
                pool.wait_ge(idx_staged, 2 * (NOCT + 1))
                with pool.Fori(0, NOCT * OCT) as t:
                    pool.wait_ge(slow_step, (2 * NT + 2) * t + 1)
                    g.tensor_copy(idx_st[:, 0:1], src_i[:, ds(t, 1)]).then_inc(slow_idx, 1)
                    pool.wait_ge(slow_idx, t + 1)
                    pool.sem_inc(slots_taken, 1)
                    g.indirect_dma_start(gath[:, 0, :], None, xn_d,
                                         bass.IndirectOffsetOnAxis(ap=idx_st[:, 0:1], axis=0)).then_inc(slow_gath, 16)
                    pool.wait_ge(slow_gath, 16 * t + 16)

            pool.wait_ge(c_copied, NT)
            g.iota(token[:, :, 2 * D:ROW].bitcast(I32), pattern=[[P, NT], [0, 1]], base=0, channel_multiplier=1).then_inc(numbered, 1)
            for t in range(1, NT + 4):
                pool.wait_ge(var_ab, within(t) + within(t - 3))
                if t >= 3:
                    pool.wait_ge(lna_done, within(t - 2))
                if t >= 6:
                    pool.wait_ge(lnb_done, within(t - 5))
                at = p_own.mark(g.tensor_scalar(rs_ab[:, t % 2, :], mv_ab[:, t % 2, :, 1], EPS, None, ALU.add))
                pool.wait_ge(p_own.sem, at)
                g.tensor_tensor(rs_ab[:, t % 2, :], rs_ab[:, t % 2, :], neg_half[:, 0:1].to_broadcast([P, 2]), ALU.pow).then_inc(rs_ready, 1)
                a = t - 2
                if 0 <= a < NT:
                    n = rows(a)
                    pool.wait_ge(lna_done, a + 1)
                    at = p_own.mark(g.tensor_tensor(yg[0:n, a % 2, :], y[0:n, a % 2, :], gam_bc[0:n, :], ALU.mult))
                    pool.wait_ge(early_loaded[a % EI], 16 * (a // EI + 1))
                    pool.wait_ge(p_own.sem, at)
                    g.tensor_tensor(x2[0:n, a, :], yg[0:n, a % 2, :], early_in[a % EI][0:n, D:2 * D], ALU.add).then_inc(x2_done, 1)
            pool.wait_ge(numbered, 1)
            pool.wait_ge(slots_cleared, 16 * SLOT_TILES // FG)
            for t in range(NT):
                n = rows(t)
                pool.wait_ge(pos_ready, 1 if t < POS_PARTS[0].stop else 2)
                g.indirect_dma_start(slots_d, bass.IndirectOffsetOnAxis(ap=pos_i[0:n, t:t + 1], axis=0),
                                     token[0:n, t, :], None).then_inc(scattered, 16)
            with pool.Fori(0, SLOT_TILES // (FG * FT)) as i:
                for s in range(FG * FT):
                    pool.wait_ge(f_numbers, FG * FT * i + s + 1)
                    pool.wait_ge(f_y, FG * FT * i + s + FT + 1)
                    pool.sem_inc(slots_taken, 1)
                    g.indirect_dma_start(out, bass.IndirectOffsetOnAxis(ap=f_id[:, s:s + 1], axis=0),
                                         f_ys[:, s, :], None, bounds_check=N - 1, oob_is_err=False).then_inc(f_stored[s], 16)

        @block.scalar
        def _(act):
            s = nc.scalar
            act.dma_start(comp_diag[:, :, :], group_mask).then_inc(types_loaded, 16)
            act.dma_start(rel_of[:, :], relation_of).then_inc(types_loaded, 16)
            act.dma_start(comp_rep[:, :], comp.rearrange("(a r) b -> a r b", a=1).to_broadcast([TG, R, B])).then_inc(types_loaded, 16)
            act.dma_start(type_g, type_rows.rearrange("(g a c) e -> g a (c e)", g=TG, a=1).to_broadcast([TG, R, TC * P])).then_inc(types_loaded, 16)
            act.dma_start(dst_i[:, :], dst_t).then_inc(tables_loaded, 16)
            act.dma_start(src_i[:, :], src_t).then_inc(tables_loaded, 16)
            act.wait_ge(eps_made, 1)
            def xnt_out(w):
                n = 2 * P if w < PAIRS else P
                act.wait_ge(turned, w + 1)
                s.copy(xnt[:, :, 2 * P * w:2 * P * w + n],
                       ps_mix[w % 2][:, :].rearrange("p (k n) -> p k n", k=KD)[:, :, 0:n]).then_inc(xnt_ready, 1)

            for g in range(GROUPS):
                act.wait_ge(var_ready, g + 1)
                s.activation(rstd[:, g * GT:(g + 1) * GT], mv[:, g * GT:(g + 1) * GT, 1], ACT.Sqrt, bias=eps_col[:, :]).then_inc(std_ready, 1)
                act.wait_ge(rstd_ready, g + 1)
                for t in range(g * GT, g * GT + GA):
                    s.activation(xn[:, t, 0:D], xn[:, t, 0:D], ACT.Identity, bias=nmr[:, t:t + 1], scale=rstd[:, t:t + 1]).then_inc(ln_act, 1)
                if g == 1:
                    for w in pairs_within(g - 1):
                        xnt_out(w)
                if g == 2:
                    act.wait_ge(tables_loaded, 32)
                    s.copy(idx_st[:, :], src_i[:, 0:OCT]).then_inc(idx_staged, 2)
            for n, c in enumerate(range(0, TC, CB)):
                w = min(CB, TC - c)
                act.wait_ge(wts_mult, n + 1)
                s.copy(wts[:, :, :].rearrange("p b (g c) -> p c g b", g=TG)[:, c:c + w, :, :],
                       ps_edge[n][:, 0:w * TG * B].rearrange("p (c g b) -> p c g b", c=w, b=B)).then_inc(wts_ready, 1)
            for g in range(1, GROUPS):
                for w in pairs_within(g):
                    xnt_out(w)
            act.wait_ge(rwt_turned, 1)
            s.copy(rwt[:, :, :], ps_sum[0][:, 0:KD * X].rearrange("p (k e) -> p k e", k=KD)).then_inc(rwt_ready, 1)

            def stage_idx(q, half):
                w = OCT // 2
                for k in range(half * w, half * w + w):
                    act.wait_ge(gathered[k], 16 * q + 16)
                s.copy(idx_st[:, half * w:half * w + w], src_i[:, ds(OCT * q + OCT + half * w, w)]).then_inc(idx_staged, 1)

            def octet(q, beside, i):
                if beside in ("sum", "sum_last"):
                    act.wait_ge(keyed, 2 * i + 1)
                    for j in range(2):
                        s.copy(xst[:, j, :, :], xnt[:, :, ds(2 * P * i + P * j, P)]).then_inc(st_copied, 1)
                if beside == "sum_first":
                    s.copy(xst[:, 0, :, :], xnt[:, :, (NT - 1) * P:NT * P]).then_inc(st_copied, 1)
                if beside == "early":
                    act.wait_ge(early_mult, 2 * i + 1)
                    for j in range(2):
                        s.copy(xst[:, j, :, :], xnt[:, :, ds(2 * P * i + P * j, P)]).then_inc(c_copied, 1)
                if beside == "early_last":
                    act.wait_ge(early_mult, 2 * PAIRS + 1)
                    s.copy(xst[:, 0, :, :], xnt[:, :, (NT - 1) * P:NT * P]).then_inc(c_copied, 1)
                if beside == "product":
                    act.wait_ge(added, KD * (OCT // PAIR * q + 4))
                    act.wait_ge(z_part, 2 * i + 1)
                    s.copy(zst[0], acc[:, 0:B, ds(P * i, P)]).then_inc(z_staged, 1)
                    act.wait_ge(z_part, 2 * i + 2)
                    s.copy(zst[1], acc[:, B:2 * B, ds(P * i, P)]).then_inc(z_staged, 1)

                def first(j):
                    if beside in ("sum", "sum_last"):
                        act.wait_ge(summed, 2 * i + 1)
                        act.wait_ge(keyed, 2 * i + j + 2)
                        s.activation(et[:, j, :], ps_mix[j][:, 0:D], ACT.Exp).then_inc(exped, 1)
                    if beside == "early":
                        act.wait_ge(early_mult, 2 * i + j + 2)
                        act.wait_ge(eout_free, 2 * i + j + 1)
                        s.copy(eout[:, j, 0:D], ps_mix[j][:, 0:D]).then_inc(pre_out, 1)

                stage_idx(q, 0)
                if beside == "small_b":
                    act.wait_ge(var_ready, GROUPS + 1)
                    s.activation(rstd[:, 0:KD], mv[:, 0:KD, 1], ACT.Sqrt, bias=eps_col[:, :]).then_inc(std_ready, 1)
                first(0)
                if beside == "sum_first":
                    act.wait_ge(keyed, 1)
                    s.activation(et[0:LAST, 0, :], ps_mix[0][0:LAST, 0:D], ACT.Exp).then_inc(exped, 1)
                if beside == "early_last":
                    act.wait_ge(early_mult, NT + 1)
                    act.wait_ge(eout_free, NT)
                    s.copy(eout[0:LAST, 0, 0:D], ps_mix[0][0:LAST, 0:D]).then_inc(pre_out, 1)
                if beside in ("sum", "sum_last", "early"):
                    stage_idx(q, 1)
                    first(1)
                if beside == "small_c":
                    act.wait_ge(m_mult, 1)
                    s.copy(cmat[:, :, D:2 * D], ps_mix[0][:, :].rearrange("p (k f) -> p k f", k=KD)).then_inc(m_copied, 1)
                if beside not in ("sum", "sum_last", "early"):
                    stage_idx(q, 1)
                if beside == "product":
                    act.wait_ge(z_part, 2 * i + 4)
                    s.copy(x2n[:, ds(i, 1), :], ps_mix[0][:, 0:D].rearrange("p (a f) -> p a f", a=1)).then_inc(z_out, 1)
                if beside == "small_a":
                    act.wait_ge(s_turned, 2)
                    s.copy(tnt, ps_mix[0][:, :].rearrange("p (k d) -> p k d", k=KD)).then_inc(s_copied, 1)
                    s.copy(wqt, ps_mix[1][:, :].rearrange("p (m i) -> p m i", m=KD)).then_inc(s_copied, 1)

            act.sem_inc(pre_out, 2)
            act.sem_inc(z_out, 1)
            edge_schedule(act, octet)

            act.wait_ge(z_out, NZ + 1)
            act.wait_ge(flag_ready, 2)
            redo = act.value_load(flag[0:1, 1:2], min_val=0, max_val=1)
            with act.If(redo > 0):
                for t in range(NZ):
                    act.wait_ge(z_redone, t + 1)
                    s.copy(x2n[:, t, :], ps[t % 2][:, 0:D]).then_inc(z_out, 1)
                act.wait_ge(z_out, 2 * NZ + 1)
            act.sem_inc(z_ready, 1)

            for t in range(NT + 9):
                a = t - 6
                if 0 <= a < NT:
                    act.wait_ge(t_turned, a + 1)
                    if a >= 2:
                        act.wait_ge(logits_mult, a - 1)
                    s.copy(x2nt[:, a % 2, :, 0:rows(a)],
                           ps[2 + a % 2][:, 0:KD * P].rearrange("p (k n) -> p k n", k=KD)[:, :, 0:rows(a)]).then_inc(t_copied, 1)
                if t < NT:
                    n = rows(t)
                    act.wait_ge(u_done, t + 1)
                    if t >= 2:
                        act.wait_ge(lna_done, t - 1)
                    s.activation(h[0:n, t % 2, :], u[0:n, t % 2, :], ACT.Gelu).then_inc(gelu_done, 1)
                if t < 2 * LATE and t % 2 == 1:
                    j = t // 2
                    act.wait_ge(z_mult, j + 1)
                    s.copy(x2n[0:rows(NZ + j), NZ + j, :], ps[j % 2][0:rows(NZ + j), 0:D]).then_inc(z_ready, 1)
                b = t - 9
                if 0 <= b < NT:
                    act.wait_ge(ranked, b + 1)
                    s.copy(rk[:, b, :], ps[6 + b % 2][:, 0:X]).then_inc(rank_out, 1)

            act.wait_ge(expert_ready, 1)
            act.wait_ge(ffn_loaded, 64)
            for f, e in enumerate(row_values(act, ex_i[0:1, 0:FT], X - 1)):
                s.copy(f_w[:, f, :], w1_flat[:, ds(e * (KD * H), KD * H)]).then_inc(f_w1, 1)
            with act.Fori(0, SLOT_TILES // (FG * FT)) as body:
                for g in range(FG):
                    i = FG * body + g
                    for f in range(FT):
                        act.wait_ge(f_turned, FT * i + f + 1)
                        s.copy(f_xts[:, f, :], ps[f][:, 0:D]).then_inc(f_xt, 1)
                    for f, e in enumerate(row_values(act, ex_i[0:1, ds(FT * i + FT, FT)], X - 1)):
                        act.wait_ge(f_hid, FT * i + f + 1)
                        s.copy(f_w[:, f, :], w1_flat[:, ds(e * (KD * H), KD * H)]).then_inc(f_w1, 1)

        @block.tensor
        def _(pe):
            t_ = nc.tensor
            pe.wait_ge(consts_made, 7)
            pe.sem_inc(z_part, 2)

            def turn(w):
                tiles = [2 * w, 2 * w + 1] if w < PAIRS else [NT - 1]
                pe.wait_ge(ln_done, tiles[-1] // GT + 1)
                pe.wait_ge(ln_act, (tiles[-1] // GT + 1) * GA)
                if w >= 2:
                    pe.wait_ge(xnt_ready, w - 1)
                for j, t in enumerate(tiles):
                    for k in range(KD):
                        ins = t_.transpose(ps_mix[w % 2][:, k * 2 * P + j * P:k * 2 * P + j * P + P],
                                           xn[:, t, k * P:(k + 1) * P], ident[:, :])
                ins.then_inc(turned, 1)

            for g in range(GROUPS):
                for w in pairs_within(g):
                    turn(w)
                if g == 0:
                    pe.wait_ge(hot_ready, 3)
                    for n, c0 in enumerate(range(0, TC, CB)):
                        for c in range(c0, min(c0 + CB, TC)):
                            for part in range(3):
                                ins = t_.matmul(ps_edge[n][:, (c - c0) * TG * B:(c - c0 + 1) * TG * B], type_hot[:, c * P:(c + 1) * P],
                                                comp3[:, part, :], start=part == 0, stop=part == 2)
                        ins.then_inc(wts_mult, 1)
                    pe.wait_ge(wts_mult, -(-TC // CB))
                    pe.sem_inc(multiplied, OCT)
            pe.wait_ge(weights_loaded, 16 * 14)
            for k in range(KD):
                ins = t_.transpose(ps_sum[0][:, k * X:(k + 1) * X], rw[:, k * P:(k + 1) * P], ident[0:X, 0:X])
            ins.then_inc(rwt_turned, 1)
            pe.wait_ge(xnt_ready, PAIRS + 1)
            pe.wait_ge(rwt_ready, 1)
            pe.wait_ge(loopw_ready, 1)

            def edges(q, quarter):
                if quarter % 2 == 0:
                    pe.wait_ge(wmat_built, 2 * q + quarter // 2 + 1)
                pair = range(PAIR * quarter, PAIR * quarter + PAIR)
                pe.wait_ge(added, KD * (4 * q + quarter + 1))
                for m in range(KD):
                    for k in pair:
                        if m == 0:
                            pe.wait_ge(gathered[k], 16 * q + 16)
                        ins = t_.matmul(ps_edge[quarter][:, m * B * WIN:(m + 1) * B * WIN], gath[:, k, m * P:(m + 1) * P],
                                        wmat[:, k, :, :].rearrange("p b w -> p (b w)"), start=k == pair[0], stop=k == pair[-1])
                        if m == KD - 1:
                            ins.then_inc(multiplied, 1)

            def key_max(m, first, n):
                for k in range(KD):
                    ins = t_.matmul(ps_mix[m][:, 0:n], wk[:, k, m * P:(m + 1) * P],
                                    xnt[:, k, ds(first, n)], start=k == 0, stop=k == KD - 1)
                ins.then_inc(max_mult, 1)

            def keys(j, n):
                for k in range(KD):
                    t_.matmul(ps_mix[j][0:n, 0:D], xst[:, j, k, 0:n], wk[:, k, :], start=k == 0, stop=False)
                t_.matmul(ps_mix[j][0:n, 0:D], onesb[0:3, 0:n], shift3[:, :], start=False, stop=True).then_inc(keyed, 1)

            def weigh(j, tile, n, start, stop):
                for m in range(KD):
                    ins = t_.matmul(ps_sum[m][:, 0:D + 1], et[0:n, j, m * P:(m + 1) * P], tile,
                                    start=start, stop=stop)
                ins.then_inc(summed, 1)

            def early(j, n):
                for k in range(KD):
                    t_.matmul(ps_mix[j][0:n, :], xst[:, j, k, 0:n], cmat[:, k, :], start=k == 0, stop=False)
                t_.matmul(ps_mix[j][0:n, :], onesb[0:3, 0:n], bias3[:, :], start=False, stop=True).then_inc(early_mult, 1)

            def turn_wq():
                pe.wait_ge(exped, NT)
                for m in range(KD):
                    for k in range(KD):
                        ins = t_.transpose(ps_mix[1][:, m * D + k * P:m * D + (k + 1) * P],
                                           wq[:, k, m * P:(m + 1) * P], ident[:, :])
                ins.then_inc(s_turned, 1)

            def turn_sums():
                pe.wait_ge(tn_ready, 2)
                for m in range(KD):
                    for k in range(KD):
                        ins = t_.transpose(ps_mix[0][:, k * D + m * P:k * D + (m + 1) * P],
                                           tn[:, m, k * P:(k + 1) * P], ident[:, :])
                ins.then_inc(s_turned, 1)

            def lam_product():
                pe.wait_ge(s_copied, 2)
                for m in range(KD):
                    for k in range(KD):
                        ins = t_.matmul(ps_sum[0][:, m * D:(m + 1) * D], tnt[:, k, m * P:(m + 1) * P], wv[:, k, :],
                                        start=k == 0, stop=k == KD - 1)
                ins.then_inc(lam_mult, 1)

            def m_product():
                pe.wait_ge(bn_ready, 2)
                for k in range(KD):
                    for m in range(KD):
                        t_.matmul(ps_mix[0][:, k * D:(k + 1) * D], wqt[:, m, k * P:(k + 1) * P], lam[:, m, :],
                                  start=m == 0, stop=m == KD - 1)
                for k in range(KD):
                    for m in range(KD):
                        ins = t_.matmul(ps_mix[1][:, k:k + 1], lam[:, m, k * P:(k + 1) * P], qk_col[:, 0, m:m + 1],
                                        start=m == 0, stop=m == KD - 1)
                ins.then_inc(m_mult, 1)

            def to_rows(n, bank, done):
                for c in range(n):
                    ins = t_.matmul(bank[0:3, c * P:(c + 1) * P], parts[:, c, :], identb[:, :], start=True, stop=True)
                ins.then_inc(done, 1)

            def piece(quarter, beside, i):
                j = quarter // 2
                if beside == "product":
                    product(quarter, i)
                elif beside == "max":
                    pe.wait_ge(max_done, 4 * i + quarter + 1)
                    key_max(quarter % 2, 2 * P * (2 * i + j), 2 * P)
                elif beside == "max_last" and quarter < 2:
                    pe.wait_ge(max_done, 2 * PAIRS + quarter + 1)
                    key_max(quarter, (NT - 1) * P, LAST)
                elif beside == "max_last" and quarter == 3:
                    pe.wait_ge(shift_cols, 1)
                    to_rows(KD, ps_sum[0], shift_turned)
                elif beside == "sum_first" and quarter == 1:
                    pe.wait_ge(shift_ready, 1)
                    pe.wait_ge(st_copied, 1)
                    keys(0, LAST)
                elif beside == "sum_first" and quarter == 3:
                    pe.wait_ge(exped, 1)
                    weigh(0, xn[0:LAST, NT - 1, :], LAST, True, False)
                elif beside in ("sum", "sum_last") and quarter < 2:
                    pe.wait_ge(exped, 2 * i + 1)
                    pe.wait_ge(st_copied, 2 * i + quarter + 2)
                    keys(quarter, P)
                elif beside in ("sum", "sum_last"):
                    j = quarter - 2
                    pe.wait_ge(exped, 2 * i + j + 2)
                    weigh(j, xn_raw[:, ds((D + 1) * (2 * i + j), D + 1)], P, False, beside == "sum_last" and j == 1)
                elif beside == "small_a" and quarter == 1:
                    turn_wq()
                elif beside == "small_a" and quarter == 3:
                    turn_sums()
                elif beside == "small_b" and quarter == 0:
                    lam_product()
                elif beside == "small_c" and quarter == 1:
                    m_product()
                elif beside == "small_c" and quarter == 3:
                    pe.wait_ge(cols_ready, 1)
                    to_rows(4, ps_sum[1], bias_turned)
                    pe.wait_ge(bias_ready, 1)
                    pe.wait_ge(m_copied, 1)
                    pe.sem_inc(early_mult, 1)
                elif beside == "early" and quarter in (0, 2):
                    pe.wait_ge(c_copied, 2 * i + j + 1)
                    pe.wait_ge(pre_out, 2 * i + j + 1)
                    pe.wait_ge(mix_out, 2 * i + j + 1)
                    early(j, P)
                elif beside == "early_last" and quarter == 0:
                    pe.wait_ge(c_copied, NT)
                    pe.wait_ge(pre_out, NT)
                    pe.wait_ge(mix_out, NT)
                    early(0, LAST)

            def product(quarter, i):
                m = quarter // 2
                if quarter == 0:
                    pe.wait_ge(z_out, i + 1)
                if quarter % 2 == 0:
                    pe.wait_ge(basis_loaded[m], 16)
                    pe.wait_ge(z_staged, 2 * i + m + 1)
                for b in range(quarter % 2 * B // 2, (quarter % 2 + 1) * B // 2):
                    ins = t_.matmul(ps_mix[0][:, 0:D], zst[m][:, b, :], basis_sb[m][:, b, :],
                                    start=m == b == 0, stop=m == KD - 1 and b == B - 1)
                if quarter % 2 == 1:
                    ins.then_inc(z_part, 1)

            def octet(q, beside, i):
                for quarter in range(4):
                    edges(q, quarter)
                    piece(quarter, beside, i)

            edge_schedule(pe, octet)

            pe.wait_ge(flag_ready, 2)
            far = pe.value_load(flag[0:1, 0:1], min_val=0, max_val=1)
            with pe.If(far > 0):
                with pe.Fori(0, NOCT * OCT) as t:
                    pe.wait_ge(slow_gath, 16 * t + 16)
                    pe.sem_inc(slow_seen, 1)
                    with pe.Fori(0, NT) as w:
                        pe.wait_ge(slow_built, NT * t + w + 1)
                        for m in range(KD):
                            ins = t_.matmul(ps_edge[m][:, :], gath[:, 0, m * P:(m + 1) * P], far_w4,
                                            start=True, stop=True)
                        ins.then_inc(slow_mult, 1)

            def product_half(j, m, t, n):
                for b in range(B):
                    ins = t_.matmul(ps[j % 2][0:n, 0:D], acc[:, m * B + b, t * P:t * P + n], basis_sb[m][:, b, :],
                                    start=m == b == 0, stop=m == KD - 1 and b == B - 1)
                return ins

            pe.wait_ge(acc_final, 1)
            for m in range(KD):
                pe.wait_ge(basis_loaded[m], 16)
            redo = pe.value_load(flag[0:1, 1:2], min_val=0, max_val=1)
            with pe.If(redo > 0):
                for t in range(NZ):
                    pe.wait_ge(z_out, NZ + max(t, 1))
                    for m in range(KD):
                        ins = product_half(t, m, t, P)
                    ins.then_inc(z_redone, 1)

            pe.wait_ge(z_ready, 1)
            for t in range(NT + 9):
                if t < 2 * LATE:
                    j, m = t // 2, t % 2
                    n = rows(NZ + j)
                    if m == 0 and j >= 2:
                        pe.wait_ge(z_ready, j)
                    ins = product_half(j, m, NZ + j, n)
                    if m == 1:
                        ins.then_inc(z_mult, 1)
                a = t - 6
                if 0 <= a < NT:
                    n = rows(a)
                    pe.wait_ge(lnb_done, a + 1)
                    if a >= 2:
                        pe.wait_ge(t_copied, a - 1)
                    for k in range(KD):
                        ins = t_.transpose(ps[2 + a % 2][:, k * P:k * P + n], x2n[0:n, a, k * P:(k + 1) * P], ident[0:n, 0:n])
                    ins.then_inc(t_turned, 1)
                b = t - 7
                if 0 <= b < NT:
                    n = rows(b)
                    pe.wait_ge(t_copied, b + 1)
                    if b >= 2:
                        pe.wait_ge(routed, b - 1)
                    for k in range(KD):
                        t_.matmul(ps[4 + b % 2][0:n, 0:X], x2nt[:, b % 2, k, 0:n], rwt[:, k, :], start=k == 0, stop=False)
                    t_.matmul(ps[4 + b % 2][0:n, 0:X], ones_row[:, 0:n], rb_row[:, :], start=False, stop=True).then_inc(logits_mult, 1)
                c = t - 9
                if 0 <= c < NT:
                    pe.wait_ge(routed, c + 1)
                    if c >= 2:
                        pe.wait_ge(rank_out, c - 1)
                    t_.matmul(ps[6 + c % 2][:, 0:X], before[:, :], oh[:, c, :], start=True, stop=False)
                    t_.matmul(ps[6 + c % 2][:, 0:X], onesb[:, :], oh_sum[:, c, :], start=False, stop=True).then_inc(ranked, 1)
            t_.matmul(ps[0][:, 0:X], onesb[:, :], oh_sum[:, NT, :], start=True, stop=True).then_inc(counted, 1)

            pe.wait_ge(expert_ready, 1)
            pe.wait_ge(rank_out, NT)
            pe.wait_ge(ffn_loaded, 64)
            with pe.Fori(0, SLOT_TILES // (FG * FT)) as body:
                for g in range(FG):
                    i = FG * body + g
                    for f in range(FT):
                        pe.wait_ge(f_in[FT * g + f], 16 * body + 16)
                        pe.wait_ge(f_xt, FT * i + f + 1)
                        for k in range(KD):
                            ins = t_.transpose(ps[f][:, k * P:(k + 1) * P], f_x[:, FT * g + f, k * P:(k + 1) * P], ident[:, :])
                        ins.then_inc(f_turned, 1)
                    for f in range(FT):
                        pe.wait_ge(f_xt, FT * i + FT + f + 1)
                        pe.wait_ge(f_w1, FT * i + f + 1)
                        pe.wait_ge(f_y, FT * i + f + 1)
                        for k in range(KD):
                            ins = t_.matmul(ps[FT + f][0:H, 0:P], f_w[:, f, k * H:(k + 1) * H], f_xts[:, f, k * P:(k + 1) * P],
                                            start=k == 0, stop=k == KD - 1)
                        ins.then_inc(f_hid, 1)
                    for f, e in enumerate(row_values(pe, ex_i[0:1, ds(FT * i, FT)], X - 1)):
                        pe.wait_ge(f_relu, FT * i + f + 1)
                        t_.matmul(ps[FT + f][:, 0:D], f_hts[:, f, :], w2_sb[:, ds(e * D, D)], start=True, stop=True).then_inc(f_out, 1)

        @block.vector
        def _(v):
            d = nc.vector

            def own(at):
                v.wait_ge(v_own.sem, at)

            d.memset(xn[:, NT - 1, :], 0.0).then_inc(pad_zeroed, 1)
            v.wait_ge(pad_zeroed, 1)
            v_own.mark(d.memset(xn[:, :, D:D + 1], 1.0))
            d.memset(eps_col[:, :], EPS).then_inc(eps_made, 1)
            v.wait_ge(rows_loaded, 16)
            er = ETAB // ROWG
            dr = dstr_i[0:er, :].rearrange("p (g e) -> p g e", g=WROW)
            v_own.mark(d.tensor_reduce(low[:, :], dr, AX.X, ALU.min))
            at = v_own.mark(d.tensor_reduce(high[:, :], dr, AX.X, ALU.max))
            own(at)
            d.tensor_tensor(span[:, :], high[:, :], low[:, :], ALU.subtract).then_inc(bounds_ready, 1)
            def statistics(g):
                v.wait_ge(x_loaded[g], 16 if g < GROUPS - 1 else 32)
                for t in range(g * GT, (g + 1) * GT):
                    at = v_own.mark(d.bn_stats(stats[:, t % GT, :], xn[:, t, 0:D]))
                own(at)
                for t in range(g * GT, (g + 1) * GT):
                    at = v_own.mark(d.bn_aggr(mv[:, t, :], stats[:, t % GT, :]))
                own(at)
                v.sem_inc(var_ready, 1)

            def normalise(g):
                v.wait_ge(std_ready, g + 1)
                cut = slice(g * GT, (g + 1) * GT)
                at = v_own.mark(d.reciprocal(rstd[:, cut], rstd[:, cut]))
                own(at)
                d.scalar_tensor_tensor(nmr[:, cut], mv[:, cut, 0], -1.0, rstd[:, cut], ALU.mult, ALU.mult).then_inc(rstd_ready, 1)
                for t in range(g * GT + GA, (g + 1) * GT):
                    at = v_own.mark(d.tensor_scalar(xn[:, t, 0:D], xn[:, t, 0:D], mv[:, t, 0:1], rstd[:, t:t + 1], ALU.subtract, ALU.mult))
                own(at)
                v.sem_inc(ln_done, 1)

            for g in range(GROUPS + 1):
                if g < GROUPS:
                    statistics(g)
                if g > 0:
                    normalise(g - 1)
                if g == 2:
                    v.wait_ge(types_loaded, 64)
                    d.tensor_scalar(type_hot, type_g, rel_of[:, :], None, ALU.is_equal).then_inc(hot_ready, 1)
                    d.tensor_tensor(comp_diag[:, :, :], comp_diag[:, :, :], comp_rep[:, :].unsqueeze(1).to_broadcast([P, TG, B]), ALU.mult).then_inc(hot_ready, 1)
                    v.wait_ge(hot_ready, 2)
                    rest_of = comp_diag[:, :, :].rearrange("p g b -> p (g b)")
                    for part in range(3):
                        at = v_own.mark(d.tensor_copy(comp3[:, part, :], rest_of))
                        own(at)
                        if part < 2:
                            at = v_own.mark(d.tensor_tensor(rest_of, rest_of, comp3[:, part, :], ALU.subtract))
                            own(at)
                    v.sem_inc(hot_ready, 1)
            v.wait_ge(bounds_loaded, 48)
            v.wait_ge(tables_loaded, 32)
            d.tensor_tensor(rel[:, :].rearrange("p (w j) -> p w j", j=PAIR), dst_i[:, :].rearrange("p (w j) -> p w j", j=PAIR),
                            base_bc.unsqueeze(2).to_broadcast([P, NWIN, PAIR]), ALU.subtract).then_inc(rel_ready, 1)
            v.wait_ge(consts_made, 7)
            v.wait_ge(rel_ready, 1)
            v.wait_ge(wts_ready, -(-TC // CB))

            def build_hit(q, half):
                w = OCT // 2
                n = 2 * q + half
                cut = ds(OCT * q + half * w, w) if not isinstance(q, int) else slice(OCT * q + half * w, OCT * q + half * w + w)
                v.wait_ge(wmat_built, n) if not isinstance(q, int) or n > 0 else None
                d.tensor_tensor(hit[:, :, :], rel[:, cut].unsqueeze(2).to_broadcast([P, w, WIN]),
                                iota[:, 0:WIN].unsqueeze(1).to_broadcast([P, w, WIN]), ALU.is_equal).then_inc(hit_built, 1)

            def build_weights(q, half):
                w = OCT // 2
                n = 2 * q + half
                cut = ds(OCT * q + half * w, w) if not isinstance(q, int) else slice(OCT * q + half * w, OCT * q + half * w + w)
                if not isinstance(q, int) or q > 0:
                    v.wait_ge(multiplied, OCT * q + half * w + w)
                v.wait_ge(hit_built, n + 1)
                d.tensor_tensor(wmat[:, half * w:half * w + w, :, :], hit[:, :, :].unsqueeze(2).to_broadcast([P, w, B, WIN]),
                                wts[:, :, cut].rearrange("p b t -> p t b").unsqueeze(3).to_broadcast([P, w, B, WIN]),
                                ALU.mult).then_inc(wmat_built, 1)

            for half in range(2):
                build_hit(0, half)
                build_weights(0, half)
            d.memset(acc_raw[:, 0:TC * P].bitcast(BF16), 0.0).then_inc(acc_zeroed, 1)
            for k in range(KD):
                blockk = cmat[:, k, k * P:(k + 1) * P]
                if k == 0:
                    v.wait_ge(weights_loaded, 16 * 14)
                at = v_own.mark(d.tensor_tensor(blockk, blockk, ident[:, :], ALU.add))
            own(at)
            v.sem_inc(loopw_ready, 1)
            v.wait_ge(acc_zeroed, 2)
            v.sem_inc(added, 4 * KD)
            v.sem_inc(max_done, 2)
            v.sem_inc(mix_out, 2)

            def add_edges(q, half, bases):
                for w in range(half * OCT // PAIR // 2, (half + 1) * OCT // PAIR // 2):
                    v.wait_ge(multiplied, OCT * q + PAIR * (w + 1) + OCT)
                    for m in range(KD):
                        place = acc[:, m * B:(m + 1) * B, ds(bases[w], WIN)]
                        v.wait_ge(added, KD * (OCT // PAIR * q + w + 3) + m + 1)
                        d.tensor_tensor(place, place, ps_edge[w][:, m * B * WIN:(m + 1) * B * WIN].rearrange("p (b w) -> p b w", w=WIN),
                                        ALU.add).then_inc(added, 1)
                    if w % 2 == 0:
                        build_hit(q + 1, half)
                build_weights(q + 1, half)

            def reduce_max(i, m, n):
                v.wait_ge(max_mult, 2 * i + m + 1)
                d.tensor_reduce(top[:, ds(2 * i + m, 1)], ps_mix[m][:, 0:n], AX.X, ALU.max).then_inc(max_done, 1)

            def early_out(i, j):
                v.wait_ge(early_mult, 2 * i + j + 2)
                v.wait_ge(pre_out, 2 * i + j + 3)
                v.wait_ge(xin_loaded[j], 16 * i + 16)
                v.wait_ge(eout_free, 2 * i + j + 1)
                d.tensor_tensor(eout[:, j, D:2 * D], ps_mix[j][:, D:2 * D], xin[:, j, :], ALU.add).then_inc(mix_out, 1)

            def split3(ncol, at):
                own(at)
                at = v_own.mark(d.tensor_copy(parts[:, 0:ncol, 0], cols[:, 0:ncol]))
                own(at)
                at = v_own.mark(d.tensor_tensor(rest[:, 0, 0:ncol], cols[:, 0:ncol], parts[:, 0:ncol, 0], ALU.subtract))
                own(at)
                at = v_own.mark(d.tensor_copy(parts[:, 0:ncol, 1], rest[:, 0, 0:ncol]))
                own(at)
                at = v_own.mark(d.tensor_tensor(rest[:, 1, 0:ncol], rest[:, 0, 0:ncol], parts[:, 0:ncol, 1], ALU.subtract))
                own(at)
                return d.tensor_copy(parts[:, 0:ncol, 2], rest[:, 1, 0:ncol])

            def octet(q, beside, i):
                bases = row_values(v, base_row[0:1, ds(OCT // PAIR * q, OCT // PAIR)], N - 1)
                if beside == "product":
                    v.wait_ge(z_staged, 2 * i + 2)
                add_edges(q, 0, bases)
                if beside == "max":
                    reduce_max(2 * i, 0, 2 * P)
                    reduce_max(2 * i, 1, 2 * P)
                elif beside == "max_last":
                    reduce_max(PAIRS, 0, LAST)
                    reduce_max(PAIRS, 1, LAST)
                    v.wait_ge(max_done, 2 * PAIRS + 4)
                    at = v_own.mark(d.tensor_reduce(cols[:, 4:4 + KD], top[:, :].rearrange("p (i m) -> p m i", m=KD), AX.X, ALU.max))
                    own(at)
                    at = v_own.mark(d.tensor_tensor(cols[:, 6:6 + KD], cols[:, 4:4 + KD], qk_col[:, 1, :], ALU.add))
                    own(at)
                    at = v_own.mark(d.tensor_tensor(cols[:, 0:KD], qk_col[:, 1, :], cols[:, 6:6 + KD], ALU.subtract))
                    split3(KD, at).then_inc(shift_cols, 1)
                elif beside == "early":
                    early_out(i, 0)
                elif beside == "early_last":
                    v.wait_ge(early_mult, NT + 1)
                    v.wait_ge(pre_out, NT + 2)
                    v.wait_ge(eout_free, NT)
                    v.wait_ge(xin_loaded[0], 16 * (PAIRS + 1))
                    d.tensor_tensor(eout[0:LAST, 0, D:2 * D], ps_mix[0][0:LAST, D:2 * D], xin[0:LAST, 0, :], ALU.add).then_inc(mix_out, 1)
                elif beside == "small_a":
                    v.wait_ge(summed, NT)
                    for m in range(KD):
                        at = v_own.mark(d.reciprocal(cols[:, m:m + 1], ps_sum[m][:, D:D + 1]))
                    own(at)
                    for m in range(KD):
                        d.tensor_scalar(tn[:, m, :], ps_sum[m][:, 0:D], cols[:, m:m + 1], None, ALU.mult).then_inc(tn_ready, 1)
                elif beside == "small_b":
                    v.wait_ge(lam_mult, 1)
                    for m in range(KD):
                        at = v_own.mark(d.tensor_tensor(lam[:, m, :], ps_sum[0][:, m * D:(m + 1) * D], bv_bc[:, :], ALU.add))
                    own(at)
                    for m in range(KD):
                        at = v_own.mark(d.bn_stats(stats[:, m, :], lam[:, m, :]))
                    own(at)
                    for m in range(KD):
                        at = v_own.mark(d.bn_aggr(mv[:, m, :], stats[:, m, :]))
                    own(at)
                    v.sem_inc(var_ready, 1)
                    v.wait_ge(std_ready, GROUPS + 1)
                    at = v_own.mark(d.reciprocal(rstd[:, 0:KD], rstd[:, 0:KD]))
                    own(at)
                    at = v_own.mark(d.tensor_tensor(cols[:, 0:KD], rstd[:, 0:KD], bn_col[:, 0, :], ALU.mult))
                    own(at)
                    for m in range(KD):
                        at = v_own.mark(d.tensor_scalar(lam[:, m, :], lam[:, m, :], mv[:, m, 0:1], cols[:, m:m + 1], ALU.subtract, ALU.mult))
                    own(at)
                    for m in range(KD):
                        d.tensor_scalar(lam[:, m, :], lam[:, m, :], bn_col[:, 1, m:m + 1], None, ALU.add).then_inc(bn_ready, 1)
                elif beside == "small_c":
                    v.wait_ge(m_mult, 1)
                    v_own.mark(d.tensor_copy(cols[:, 0:KD], hb_col[:, 0, :]))
                    at = v_own.mark(d.tensor_tensor(cols[:, KD:2 * KD], ps_mix[1][:, 0:KD], hb_col[:, 1, :], ALU.add))
                    split3(4, at).then_inc(cols_ready, 1)
                add_edges(q, 1, bases)
                if beside == "max":
                    reduce_max(2 * i + 1, 0, 2 * P)
                    reduce_max(2 * i + 1, 1, 2 * P)
                elif beside == "max_last":
                    v.wait_ge(shift_turned, 1)
                    d.tensor_copy(shift3[:, :], ps_sum[0][0:3, 0:D]).then_inc(shift_ready, 1)
                elif beside == "early":
                    early_out(i, 1)
                elif beside == "small_c":
                    v.wait_ge(bias_turned, 1)
                    d.tensor_copy(bias3[:, :], ps_sum[1][0:3, :]).then_inc(bias_ready, 1)

            at = v_own.mark(d.tensor_reduce(high[0:1, 0:1], span_row[:, :], AX.X, ALU.max))
            own(at)
            d.tensor_scalar(flag[:, 0:1], high[0:1, 0:1], float(WIN - 1), None, ALU.is_gt).then_inc(flag_ready, 1)
            at = v_own.mark(d.tensor_tensor(reach[:, :], base_row[0:1, (NOCT - NZ) * OCT // PAIR:NOCT * OCT // PAIR], reach[:, :], ALU.subtract))
            own(at)
            at = v_own.mark(d.tensor_reduce(late[:, 0:1], reach[:, :], AX.X, ALU.min))
            own(at)
            at = v_own.mark(d.tensor_scalar(late[:, 1:2], late[:, 0:1], 0.0, None, ALU.is_lt))
            own(at)
            v.wait_ge(flag_ready, 1)
            d.tensor_tensor(flag[:, 1:2], late[:, 1:2], flag[:, 0:1], ALU.max).then_inc(flag_ready, 1)

            edge_schedule(v, octet)

            v.wait_ge(flag_ready, 2)
            v.wait_ge(added, KD * (NOCT * OCT // PAIR + 4))
            far = v.value_load(flag[0:1, 0:1], min_val=0, max_val=1)
            far_w = cols[:, 0:B]
            far_dst = cols[:, 5:6]
            sgath = hit[:, :, :].rearrange("p a w -> p (a w)")[:, 0:P]
            with v.If(far > 0):
                v.wait_ge(multiplied, OCT * (NOCT + 1))
                v.sem_inc(slow_step, 1)
                with v.Fori(0, NOCT * OCT) as t:
                    a = (2 * NT + 2) * t
                    v.wait_ge(slow_step, a + 1)
                    for b in range(B):
                        ins = d.scalar_tensor_tensor(far_w[:, b:b + 1], rel[:, ds(t, 1)], float(WIN), wts[:, b, ds(t, 1)], ALU.is_ge, ALU.mult)
                    d.tensor_copy(far_dst, dst_i[:, ds(t, 1)]).then_inc(slow_step, 1)
                    with v.Fori(0, NT) as w:
                        v.wait_ge(slow_step, a + 2 * w + 2)
                        d.tensor_scalar(sgath, iota[:, :], far_dst, None, ALU.is_equal).then_inc(slow_step, 1)
                        v.wait_ge(slow_step, a + 2 * w + 3)
                        d.tensor_tensor(far_w4.rearrange("p (b n) -> p b n", b=B),
                                        sgath.unsqueeze(1).to_broadcast([P, B, P]),
                                        far_w.unsqueeze(2).to_broadcast([P, B, P]), ALU.mult).then_inc(slow_built, 1)
                        d.tensor_scalar(far_dst, far_dst, float(-P), None, ALU.add)
                        v.wait_ge(slow_mult, NT * t + w + 1)
                        for m in range(KD):
                            place = acc[:, m * B:(m + 1) * B, ds(P * w, P)]
                            ins = d.tensor_tensor(place, place, ps_edge[m][:, :].rearrange("p (b n) -> p b n", b=B), ALU.add)
                        ins.then_inc(slow_step, 1)
                    v.wait_ge(slow_step, a + 2 * NT + 2)
                    v.sem_inc(slow_step, 1)
            v.sem_inc(acc_final, 1)

            v.wait_ge(early_mult, NT + 1)
            v_own.mark(d.memset(oh[:, NT - 1, :], 0.0))
            at = v_own.mark(d.memset(oh_sum[:, 0, :], 0.0))
            own(at)
            at = v_own.mark(d.memset(mv_ab, 1.0))
            own(at)
            for t in range(NT + 8):
                a, a2, b, b2, c = t - 1, t - 2, t - 4, t - 5, t - 8
                j = t % 2
                if t < NT:
                    n = rows(t)
                    v.wait_ge(z_ready, 1 if t < NZ else t - NZ + 2)
                    v.wait_ge(early_loaded[t % EI], 16 * (t // EI + 1))
                    if t >= 2:
                        v.wait_ge(gelu_done, t - 1)
                    d.tensor_tensor(u[0:n, t % 2, :], x2n[0:n, t, :], early_in[t % EI][0:n, 0:D], ALU.add).then_inc(u_done, 1)
                if 0 <= c < NT:
                    m = rows(c)
                    v.wait_ge(logits_mult, c + 1)
                    if c >= 1:
                        v.wait_ge(routed, c)
                    at_c = v_own.mark(d.max(best[0:m, :], ps[4 + c % 2][0:m, 0:X]))
                if t >= 2:
                    v.wait_ge(var_ab, within(t - 1) + within(t - 4))
                if 0 <= a < NT:
                    v.wait_ge(gelu_done, a + 1)
                    at_a = v_own.mark(d.bn_stats(stat_a[0:rows(a), :], h[0:rows(a), a % 2, :]))
                if 0 <= c < NT:
                    own(at_c)
                    at_c = v_own.mark(d.max_index(best_i[0:m, :], best[0:m, :], ps[4 + c % 2][0:m, 0:X]))
                if 0 <= b < NT:
                    v.wait_ge(x2_done, b + 1)
                    at_b = v_own.mark(d.bn_stats(stat_b[0:rows(b), :], x2[0:rows(b), b, :]))
                if 0 <= c < NT:
                    own(at_c)
                    at_c = v_own.mark(d.tensor_copy(best_f[0:m, :], best_i[0:m, 0:1]))
                if 0 <= a < NT:
                    own(at_a)
                    d.bn_aggr(mv_ab[0:rows(a), j, 0, :], stat_a[0:rows(a), :]).then_inc(var_ab, 1)
                if 0 <= b < NT:
                    own(at_b)
                    d.bn_aggr(mv_ab[0:rows(b), j, 1, :], stat_b[0:rows(b), :]).then_inc(var_ab, 1)
                if 0 <= c < NT:
                    own(at_c)
                    at_c = v_own.mark(d.tensor_scalar(oh[0:m, c, :], iota[0:m, 0:X], best_f[0:m, :], None, ALU.is_equal))
                if t >= 2 and (a2 < NT or b2 < NT):
                    v.wait_ge(rs_ready, t - 1)
                if 0 <= a2 < NT:
                    if a2 >= 2:
                        v.wait_ge(x2_done, a2 - 1)
                    n = rows(a2)
                    d.tensor_scalar(y[0:n, a2 % 2, :], h[0:n, a2 % 2, :], mv_ab[0:n, 1 - j, 0, 0:1], rs_ab[0:n, 1 - j, 0:1],
                                    ALU.subtract, ALU.mult).then_inc(lna_done, 1)
                if 0 <= b2 < NT:
                    n = rows(b2)
                    d.tensor_scalar(x2n[0:n, b2, :], x2[0:n, b2, :], mv_ab[0:n, 1 - j, 1, 0:1], rs_ab[0:n, 1 - j, 1:2],
                                    ALU.subtract, ALU.mult).then_inc(lnb_done, 1)
                if 0 <= c < NT:
                    own(at_c)
                    d.tensor_tensor(oh_sum[:, c + 1, :], oh_sum[:, c, :], oh[:, c, :], ALU.add).then_inc(routed, 1)
            v.wait_ge(routed, NT)

            v.wait_ge(z_mult, LATE)
            v.wait_ge(counted, 1)
            at = v_own.mark(d.tensor_scalar(cnt, ps[0][:, 0:X], P / 2 - 0.5, 1.0 / P, ALU.add, ALU.mult))
            own(at)
            at = v_own.mark(d.tensor_scalar(cnt, cnt, ROUND, None, ALU.add))
            own(at)
            at = v_own.mark(d.tensor_scalar(n_tiles, cnt, -ROUND, None, ALU.add))
            own(at)
            at = v_own.mark(d.tensor_tensor_scan(tile_end, onesb[:, 0:X], n_tiles, 0.0, ALU.mult, ALU.add))
            own(at)
            at = v_own.mark(d.tensor_tensor(slot_base, tile_end, n_tiles, ALU.subtract))
            own(at)
            at = v_own.mark(d.tensor_scalar(slot_base, slot_base, float(P), None, ALU.mult))
            own(at)
            v.wait_ge(rank_out, NT)
            for some in POS_PARTS:
                w = some.stop - some.start
                at = v_own.mark(d.tensor_tensor(rk[:, some], rk[:, some], slot_base.unsqueeze(1).to_broadcast([P, w, X]), ALU.add))
                own(at)
                at = v_own.mark(d.tensor_tensor(rank_pick[:, some], rk[:, some], oh[:, some, :], ALU.mult))
                own(at)
                at = v_own.mark(d.tensor_reduce(pos_f[:, some], rank_pick[:, some], AX.X, ALU.add))
                own(at)
                d.tensor_copy(pos_i[:, some], pos_f[:, some]).then_inc(pos_ready, 1)
            at = v_own.mark(d.tensor_tensor(ended, tile_end.unsqueeze(1).to_broadcast([P, SLOT_TILES, X]),
                                            iota[:, 0:SLOT_TILES].unsqueeze(2).to_broadcast([P, SLOT_TILES, X]), ALU.is_le))
            own(at)
            at = v_own.mark(d.tensor_reduce(ex_f, ended, AX.X, ALU.add))
            own(at)
            at = v_own.mark(d.tensor_scalar(ex_f, ex_f, float(X - 1), None, ALU.min))
            own(at)
            at = v_own.mark(d.tensor_copy(ex_i[:, 0:SLOT_TILES], ex_f))
            at = v_own.mark(d.memset(ex_i[:, SLOT_TILES:SLOT_TILES + FT], 0))
            at = v_own.mark(d.memset(f_hts[H:H + 1, :, :], 1.0))
            own(at)
            v.sem_inc(expert_ready, 1)
            v.sem_inc(f_y, FT)
            v.sem_inc(f_xt, FT)

            def relus(body, first=False):
                for g in range(FG):
                    i = FG * body + g
                    for f, e in enumerate(row_values(v, ex_i[0:1, ds(FT * i, FT)] if not first else ex_i[0:1, FT * i:FT * i + FT], X - 1)):
                        v.wait_ge(f_hid, FT * i + f + 1)
                        d.tensor_scalar(f_hts[0:H, f, :], ps[FT + f][0:H, 0:P], b1_sb[:, ds(e, 1)], 0.0, ALU.add, ALU.max).then_inc(f_relu, 1)
                    for f in range(FT):
                        v.wait_ge(f_out, FT * i + f + 1)
                        if not first:
                            v.wait_ge(f_stored[FT * g + f], 16 * body)
                        d.tensor_copy(f_id[:, FT * g + f:FT * g + f + 1], f_x[:, FT * g + f, 2 * D:ROW].bitcast(I32)).then_inc(f_numbers, 1)
                        d.scalar_tensor_tensor(f_ys[:, FT * g + f, :], ps[FT + f][:, 0:D], 0.0, f_x[:, FT * g + f, D:2 * D],
                                               ALU.max, ALU.add).then_inc(f_y, 1)

            relus(0, first=True)
            with v.Fori(1, SLOT_TILES // (FG * FT)) as body:
                relus(body)


_INS = ["x", "src_t", "type_rows", "dst_t", "dst_rows", "L0_gnn_basis", "L0_gnn_comp", "L0_gnn_loop_w", "L0_gnn_h_bias",
        "L0_gnn_ln_gamma", "L0_gnn_ln_beta", "L0_mix_W_qk", "L0_mix_b_qk", "L0_mix_W_v", "L0_mix_b_v", "L0_mix_gamma",
        "L0_mix_beta", "L0_ffn_router_w", "L0_ffn_router_b", "L0_ffn_W1", "b1_t", "L0_ffn_W2", "L0_ffn_b2",
        "relation_of", "group_mask"]


def lay_out(inputs):
    import numpy as np

    arrays = {k: np.ascontiguousarray(v) for k, v in inputs.items()}
    pad = ETAB * P - E
    src = np.pad(arrays.pop("src"), (0, pad)).reshape(ETAB, P)
    types = np.pad(arrays.pop("edge_type_8"), (0, pad), constant_values=R).reshape(ETAB, P)
    dst = np.pad(arrays.pop("dst"), (0, pad), mode="edge").reshape(ETAB, P)
    arrays["b1_t"] = np.ascontiguousarray(arrays.pop("L0_ffn_b1").T)
    arrays["src_t"] = np.ascontiguousarray(src.T)
    arrays["type_rows"] = np.ascontiguousarray(types)
    arrays["dst_t"] = np.ascontiguousarray(dst.T)
    arrays["dst_rows"] = np.ascontiguousarray(dst)
    arrays["relation_of"] = (np.arange(P, dtype=np.float32) % R).reshape(P, 1)
    arrays["group_mask"] = np.repeat(np.repeat(np.eye(TG, dtype=np.float32), R, 0)[:, :, None], B, 2)
    return arrays


def kernel(**inputs):
    import numpy as np
    import concourse.bacc as bacc
    from concourse.bass_utils import run_bass_kernel_spmd

    laid = lay_out(inputs)
    nc = bacc.Bacc("TRN2", target_bir_lowering=False, num_devices=1)
    arrays, args = {}, []
    for name in _INS:
        a = laid[name]
        arrays[f"in_{name}"] = a
        args.append(nc.dram_tensor(f"in_{name}", a.shape, mybir.dt.from_np(a.dtype), kind="ExternalInput").ap())
    args.append(nc.dram_tensor("out_0", (N, D), F32, kind="ExternalOutput").ap())
    gps_layer(nc, *args)
    r = run_bass_kernel_spmd(nc, [arrays], core_ids=[0])
    return r.results[0]["out_0"]
```
